# Optimizing a Trainium2 kernel written in Bass

```python
import numpy as np
import jax
import jax.numpy as jnp

def _softmax(x, axis=-1):
    return jax.nn.softmax(x, axis=axis)

def _gelu(x):
    return jax.nn.gelu(x, approximate=True)

def _silu(x):
    return jax.nn.silu(x)

def _sigmoid(x):
    return jax.nn.sigmoid(x)

def _layernorm(x, axis=-1, eps=1e-05):
    m = jnp.mean(x, axis=axis, keepdims=True)
    v = jnp.var(x, axis=axis, keepdims=True)
    return (x - m) / jnp.sqrt(v + eps)

def _scatter_add(tgt, idx, src, axis=0):
    return tgt.at[idx].add(src)

def _segment_sum(src, seg, n):
    return jax.ops.segment_sum(src, seg, n)
kernel_name = 'mk_xattn_ffn_d2_seqx_r8_60255c'

def setup_inputs(seed: int=0):
    np.random.seed(seed)
    _w = jnp.asarray

    def _rec_inputs():
        import jax
        import jax.numpy as jnp
        _rk = jax.random.key(seed)
        x = -0.0002928 + 1 * jax.random.normal(jax.random.fold_in(_rk, 1), (32, 64, 128), jnp.float32)
        _lenS = 64 - jax.random.randint(jax.random.fold_in(_rk, 7), (32,), 0, max(1, 64 // 4) + 1, jnp.int32)
        _lenS2 = 64 - jax.random.randint(jax.random.fold_in(_rk, 8), (32,), 0, max(1, 64 // 4) + 1, jnp.int32)
        _ctx_1024P = jax.random.normal(jax.random.fold_in(_rk, 11), (32, 16, 128), jnp.float32)
        _ctx_1024c = jax.random.dirichlet(jax.random.fold_in(_rk, 511), 0.3 * jnp.ones((16,), jnp.float32), (32, 64))
        _ctx_1024t = jnp.einsum('bsk,bkd->bsd', _ctx_1024c, _ctx_1024P)
        _ctx_1024t = _ctx_1024t * jax.lax.rsqrt(jnp.mean(jnp.square(_ctx_1024t)) + 1e-12) * 0.953939
        ctx_1024 = -1.39393e-06 + 0.999914 * (_ctx_1024t + 0.3 * jax.random.normal(jax.random.fold_in(_rk, 611), (32, 64, 128), jnp.float32))
        return (x, ctx_1024)
    x, ctx_1024 = _rec_inputs()

    def _L0_xattn_setup():
        import jax, jax.numpy as jnp
        import numpy as np
        D_MODEL = 128
        NUM_HEADS = 16
        D_K = D_MODEL // NUM_HEADS
        key = jax.random.key(seed)
        ks = jax.random.split(key, 11)
        B, S = (2, 256)
        scale = 1.0 / np.sqrt(D_MODEL)
        inp = {'Q': jax.random.normal(ks[0], (B, S, D_MODEL), jnp.float32), 'K': jax.random.normal(ks[1], (B, S, D_MODEL), jnp.float32), 'V': jax.random.normal(ks[2], (B, S, D_MODEL), jnp.float32), 'W_q': jax.random.normal(ks[3], (D_MODEL, D_MODEL), jnp.float32) * scale, 'b_q': jnp.zeros((D_MODEL,), jnp.float32), 'W_k': jax.random.normal(ks[4], (D_MODEL, D_MODEL), jnp.float32) * scale, 'b_k': jnp.zeros((D_MODEL,), jnp.float32), 'W_v': jax.random.normal(ks[5], (D_MODEL, D_MODEL), jnp.float32) * scale, 'b_v': jnp.zeros((D_MODEL,), jnp.float32), 'W_o': jax.random.normal(ks[6], (D_MODEL, D_MODEL), jnp.float32) * scale, 'b_o': jnp.zeros((D_MODEL,), jnp.float32)}
        return inp
    _L0_xattn_all = _L0_xattn_setup()
    _L0_xattn_in = {k: v for k, v in _L0_xattn_all.items() if k in ('W_q', 'b_q', 'W_k', 'b_k', 'W_v', 'b_v', 'W_o', 'b_o')}
    del _L0_xattn_all

    def _L0_ffn_setup():
        import jax, jax.numpy as jnp
        import numpy as np
        from jax import lax
        D = 128
        H = 176
        E = 8
        K = 2
        ROUTER_SCALE = 1.0

        def _expert(x, w1, b1, w3, b3, w2, b2):
            h = jax.nn.silu((x @ w1 + b1) * (x @ w3 + b3))
            return h @ w2 + b2
        key = jax.random.key(seed)
        ks = jax.random.split(key, 16)
        s = 0.02
        inp = {'x': jax.random.normal(ks[0], (2, 256, D), dtype=jnp.float32), 'gate_w': jax.random.normal(ks[1], (E, D), dtype=jnp.float32) * s, 'gate_b': jax.random.normal(ks[2], (E,), dtype=jnp.float32) * s, 'w1': jax.random.normal(ks[3], (E, D, H), dtype=jnp.float32) * s, 'b1': jax.random.normal(ks[4], (E, H), dtype=jnp.float32) * s, 'w3': jax.random.normal(ks[5], (E, D, H), dtype=jnp.float32) * s, 'b3': jax.random.normal(ks[6], (E, H), dtype=jnp.float32) * s, 'w2': jax.random.normal(ks[7], (E, H, D), dtype=jnp.float32) * s, 'b2': jax.random.normal(ks[8], (E, D), dtype=jnp.float32) * s, 'sw1': jax.random.normal(ks[9], (D, H), dtype=jnp.float32) * s, 'sb1': jax.random.normal(ks[10], (H,), dtype=jnp.float32) * s, 'sw3': jax.random.normal(ks[11], (D, H), dtype=jnp.float32) * s, 'sb3': jax.random.normal(ks[12], (H,), dtype=jnp.float32) * s, 'sw2': jax.random.normal(ks[13], (H, D), dtype=jnp.float32) * s, 'sb2': jax.random.normal(ks[14], (D,), dtype=jnp.float32) * s}
        return inp
    _L0_ffn_all = _L0_ffn_setup()
    _L0_ffn_in = {k: v for k, v in _L0_ffn_all.items() if k in ('gate_w', 'gate_b', 'w1', 'b1', 'w3', 'b3', 'w2', 'b2', 'sw1', 'sb1', 'sw3', 'sb3', 'sw2', 'sb2')}
    del _L0_ffn_all

    def _L1_xattn_setup():
        import jax, jax.numpy as jnp
        import numpy as np
        B, S, H, NH = (2, 256, 128, 4)
        DH = H // NH
        EPS = 1e-06

        def _parallel_stabilized(qh, kh, vh, ig, fg):
            log_fg = jax.nn.log_sigmoid(fg)
            cs = jnp.cumsum(log_fg, axis=2)
            ltr = jnp.tril(jnp.ones((qh.shape[2], qh.shape[2]), dtype=bool))
            log_fg_mat = jnp.where(ltr, cs - jnp.swapaxes(cs, 2, 3), -jnp.inf)
            log_D = log_fg_mat + jnp.swapaxes(ig, 2, 3)
            max_log_D = jnp.max(log_D, axis=-1, keepdims=True)
            D = jnp.exp(log_D - max_log_D)
            qk = jnp.einsum('bhsd,bhtd->bhst', qh, kh) / jnp.sqrt(jnp.float32(DH))
            C = qk * D
            normalizer = jnp.maximum(jnp.abs(jnp.sum(C, axis=-1, keepdims=True)), jnp.exp(-max_log_D))
            return jnp.einsum('bhst,bhtd->bhsd', C / (normalizer + EPS), vh)
        key = jax.random.key(seed)
        ks = jax.random.split(key, 6)
        q = jax.random.normal(ks[0], (B, S, H), dtype=jnp.float32)
        k = jax.random.normal(ks[1], (B, S, H), dtype=jnp.float32)
        v = jax.random.normal(ks[2], (B, S, H), dtype=jnp.float32)
        igate_kernel = jax.random.normal(ks[3], (3 * H, NH), dtype=jnp.float32) * 0.02
        fgate_kernel = jax.random.normal(ks[4], (3 * H, NH), dtype=jnp.float32) * 0.02
        igate_bias = jax.random.normal(ks[5], (NH,), dtype=jnp.float32) * 0.1
        fgate_bias = jnp.linspace(3.0, 6.0, NH, dtype=jnp.float32)
        outnorm_scale = jnp.ones((H,), dtype=jnp.float32)
        return {'q': q, 'k': k, 'v': v, 'igate_kernel': igate_kernel, 'igate_bias': igate_bias, 'fgate_kernel': fgate_kernel, 'fgate_bias': fgate_bias, 'outnorm_scale': outnorm_scale}
    _L1_xattn_all = _L1_xattn_setup()
    _L1_xattn_in = {k: v for k, v in _L1_xattn_all.items() if k in ('igate_kernel', 'igate_bias', 'fgate_kernel', 'fgate_bias', 'outnorm_scale')}
    del _L1_xattn_all

    def _L1_ffn_setup():
        import jax, jax.numpy as jnp
        import numpy as np
        TOP_K = 8
        NUM_EXPERTS = 32
        CAPACITY = 128
        key = jax.random.key(seed)
        k1, k2, k3, k4 = jax.random.split(key, 4)
        B, S, H, E, F = (2, 128, 128, NUM_EXPERTS, 96)
        return {'hidden_states': jax.random.normal(k1, (B, S, H), dtype=jnp.float32), 'gate_weight': jax.random.normal(k2, (E, H), dtype=jnp.float32) * 0.02, 'gate_up_proj': jax.random.normal(k3, (E, 2 * F, H), dtype=jnp.float32) * 0.02, 'down_proj': jax.random.normal(k4, (E, H, F), dtype=jnp.float32) * 0.02}
    _L1_ffn_all = _L1_ffn_setup()
    _L1_ffn_in = {k: v for k, v in _L1_ffn_all.items() if k in ('gate_weight', 'gate_up_proj', 'down_proj')}
    del _L1_ffn_all
    return {'x': x, 'ctx_1024': ctx_1024, 'L0_xattn_W_q': _L0_xattn_in['W_q'], 'L0_xattn_b_q': _L0_xattn_in['b_q'], 'L0_xattn_W_k': _L0_xattn_in['W_k'], 'L0_xattn_b_k': _L0_xattn_in['b_k'], 'L0_xattn_W_v': _L0_xattn_in['W_v'], 'L0_xattn_b_v': _L0_xattn_in['b_v'], 'L0_xattn_W_o': _L0_xattn_in['W_o'], 'L0_xattn_b_o': _L0_xattn_in['b_o'], 'L0_ffn_gate_w': _L0_ffn_in['gate_w'], 'L0_ffn_gate_b': _L0_ffn_in['gate_b'], 'L0_ffn_w1': _L0_ffn_in['w1'], 'L0_ffn_b1': _L0_ffn_in['b1'], 'L0_ffn_w3': _L0_ffn_in['w3'], 'L0_ffn_b3': _L0_ffn_in['b3'], 'L0_ffn_w2': _L0_ffn_in['w2'], 'L0_ffn_b2': _L0_ffn_in['b2'], 'L0_ffn_sw1': _L0_ffn_in['sw1'], 'L0_ffn_sb1': _L0_ffn_in['sb1'], 'L0_ffn_sw3': _L0_ffn_in['sw3'], 'L0_ffn_sb3': _L0_ffn_in['sb3'], 'L0_ffn_sw2': _L0_ffn_in['sw2'], 'L0_ffn_sb2': _L0_ffn_in['sb2'], 'L1_xattn_igate_kernel': _L1_xattn_in['igate_kernel'], 'L1_xattn_igate_bias': _L1_xattn_in['igate_bias'], 'L1_xattn_fgate_kernel': _L1_xattn_in['fgate_kernel'], 'L1_xattn_fgate_bias': _L1_xattn_in['fgate_bias'], 'L1_xattn_outnorm_scale': _L1_xattn_in['outnorm_scale'], 'L1_ffn_gate_weight': _L1_ffn_in['gate_weight'], 'L1_ffn_gate_up_proj': _L1_ffn_in['gate_up_proj'], 'L1_ffn_down_proj': _L1_ffn_in['down_proj']}

def reference(x, ctx_1024, L0_xattn_W_q, L0_xattn_b_q, L0_xattn_W_k, L0_xattn_b_k, L0_xattn_W_v, L0_xattn_b_v, L0_xattn_W_o, L0_xattn_b_o, L0_ffn_gate_w, L0_ffn_gate_b, L0_ffn_w1, L0_ffn_b1, L0_ffn_w3, L0_ffn_b3, L0_ffn_w2, L0_ffn_b2, L0_ffn_sw1, L0_ffn_sb1, L0_ffn_sw3, L0_ffn_sb3, L0_ffn_sw2, L0_ffn_sb2, L1_xattn_igate_kernel, L1_xattn_igate_bias, L1_xattn_fgate_kernel, L1_xattn_fgate_bias, L1_xattn_outnorm_scale, L1_ffn_gate_weight, L1_ffn_gate_up_proj, L1_ffn_down_proj):
    import jax
    import jax.numpy as jnp

    def _L0_xattn_ref(Q, K, V, W_q, b_q, W_k, b_k, W_v, b_v, W_o, b_o):
        import jax, jax.numpy as jnp
        import numpy as np
        D_MODEL = 128
        NUM_HEADS = 16
        D_K = D_MODEL // NUM_HEADS
        B, S, _ = Q.shape
        H, d_k = (NUM_HEADS, D_K)
        q = Q @ W_q.T + b_q
        k = K @ W_k.T + b_k
        v = V @ W_v.T + b_v
        q = q.reshape(B, S, H, d_k).transpose(0, 2, 1, 3)
        k = k.reshape(B, S, H, d_k).transpose(0, 2, 1, 3)
        v = v.reshape(B, S, H, d_k).transpose(0, 2, 1, 3)
        scores = jnp.einsum('bhqd,bhkd->bhqk', q, k) / jnp.sqrt(jnp.float32(d_k)).astype(q.dtype)
        attn = jax.nn.softmax(scores, axis=-1)
        out = jnp.einsum('bhqk,bhkd->bhqd', attn, v)
        out = out.transpose(0, 2, 1, 3).reshape(B, S, H * d_k)
        return out @ W_o.T + b_o

    def _L0_ffn_ref(x, gate_w, gate_b, w1, b1, w3, b3, w2, b2, sw1, sb1, sw3, sb3, sw2, sb2):
        import jax, jax.numpy as jnp
        import numpy as np
        from jax import lax
        D = 128
        H = 176
        E = 8
        K = 2
        ROUTER_SCALE = 1.0

        def _expert(x, w1, b1, w3, b3, w2, b2):
            h = jax.nn.silu((x @ w1 + b1) * (x @ w3 + b3))
            return h @ w2 + b2
        shape = x.shape
        xf = x.reshape(-1, D)
        T = xf.shape[0]
        scores = jax.nn.softmax(xf @ gate_w.T, axis=-1)
        biased = scores + gate_b
        _, idx = lax.top_k(biased, K)
        w = jnp.take_along_axis(scores, idx, axis=-1) * ROUTER_SCALE
        rw = jnp.zeros((T, E), dtype=xf.dtype).at[jnp.arange(T)[:, None], idx].add(w)
        h = jax.nn.silu((jnp.einsum('td,edh->teh', xf, w1) + b1) * (jnp.einsum('td,edh->teh', xf, w3) + b3))
        oe = jnp.einsum('teh,ehd->ted', h, w2) + b2
        y = jnp.einsum('te,ted->td', rw, oe)
        z = _expert(xf, sw1, sb1, sw3, sb3, sw2, sb2)
        return (y + z).reshape(shape)

    def _L1_xattn_ref(q, k, v, igate_kernel, igate_bias, fgate_kernel, fgate_bias, outnorm_scale):
        import jax, jax.numpy as jnp
        import numpy as np
        B, S, H, NH = (2, 256, 128, 4)
        DH = H // NH
        EPS = 1e-06

        def _parallel_stabilized(qh, kh, vh, ig, fg):
            log_fg = jax.nn.log_sigmoid(fg)
            cs = jnp.cumsum(log_fg, axis=2)
            ltr = jnp.tril(jnp.ones((qh.shape[2], qh.shape[2]), dtype=bool))
            log_fg_mat = jnp.where(ltr, cs - jnp.swapaxes(cs, 2, 3), -jnp.inf)
            log_D = log_fg_mat + jnp.swapaxes(ig, 2, 3)
            max_log_D = jnp.max(log_D, axis=-1, keepdims=True)
            D = jnp.exp(log_D - max_log_D)
            qk = jnp.einsum('bhsd,bhtd->bhst', qh, kh) / jnp.sqrt(jnp.float32(DH))
            C = qk * D
            normalizer = jnp.maximum(jnp.abs(jnp.sum(C, axis=-1, keepdims=True)), jnp.exp(-max_log_D))
            return jnp.einsum('bhst,bhtd->bhsd', C / (normalizer + EPS), vh)
        Bq, Sq, Hq = q.shape
        x = jnp.concatenate([q, k, v], axis=-1)
        ig = x @ igate_kernel + igate_bias
        fg = x @ fgate_kernel + fgate_bias
        ig = jnp.transpose(ig, (0, 2, 1))[..., None]
        fg = jnp.transpose(fg, (0, 2, 1))[..., None]
        qh = jnp.transpose(q.reshape(Bq, Sq, NH, DH), (0, 2, 1, 3))
        kh = jnp.transpose(k.reshape(Bq, Sq, NH, DH), (0, 2, 1, 3))
        vh = jnp.transpose(v.reshape(Bq, Sq, NH, DH), (0, 2, 1, 3))
        h = _parallel_stabilized(qh, kh, vh, ig, fg)
        mean = jnp.mean(h, axis=-1, keepdims=True)
        var = jnp.mean((h - mean) ** 2, axis=-1, keepdims=True)
        h_norm = (h - mean) * jax.lax.rsqrt(var + 1e-05)
        h_norm = h_norm * outnorm_scale.reshape(1, NH, 1, DH)
        out = jnp.transpose(h_norm, (0, 2, 1, 3)).reshape(Bq, Sq, Hq)
        return out

    def _L1_ffn_ref(hidden_states, gate_weight, gate_up_proj, down_proj):
        import jax, jax.numpy as jnp
        import numpy as np
        TOP_K = 8
        NUM_EXPERTS = 32
        CAPACITY = 128
        B, S, H = hidden_states.shape
        E = gate_weight.shape[0]
        N = B * S
        x = hidden_states.reshape(N, H)
        logits = x @ gate_weight.T
        probs = jax.nn.softmax(logits.astype(jnp.float32), axis=-1)
        topw, topi = jax.lax.top_k(probs, TOP_K)
        topw = topw / topw.sum(-1, keepdims=True)
        topw = topw.astype(x.dtype)
        flat_e = topi.reshape(-1)
        flat_w = topw.reshape(-1)
        flat_x = jnp.repeat(x, TOP_K, axis=0)
        oh = jax.nn.one_hot(flat_e, E, dtype=jnp.int32)
        pos = (jnp.cumsum(oh, axis=0) * oh).sum(-1) - 1
        buf = jnp.zeros((E, CAPACITY, H), x.dtype).at[flat_e, pos].set(flat_x, mode='drop')
        gu = jnp.einsum('ech,efh->ecf', buf, gate_up_proj)
        gate, up = jnp.split(gu, 2, axis=-1)
        h = jax.nn.silu(gate) * up
        eo = jnp.einsum('ecf,ehf->ech', h, down_proj)
        tok_out = eo.at[flat_e, pos].get(mode='fill', fill_value=0)
        out = (tok_out * flat_w[:, None]).reshape(N, TOP_K, H).sum(1)
        return out.reshape(B, S, H)
    x = x + _L0_xattn_ref(_layernorm(x, axis=-1), ctx_1024, ctx_1024, L0_xattn_W_q, L0_xattn_b_q, L0_xattn_W_k, L0_xattn_b_k, L0_xattn_W_v, L0_xattn_b_v, L0_xattn_W_o, L0_xattn_b_o)
    x = x + _L0_ffn_ref(_layernorm(x, axis=-1), L0_ffn_gate_w, L0_ffn_gate_b, L0_ffn_w1, L0_ffn_b1, L0_ffn_w3, L0_ffn_b3, L0_ffn_w2, L0_ffn_b2, L0_ffn_sw1, L0_ffn_sb1, L0_ffn_sw3, L0_ffn_sb3, L0_ffn_sw2, L0_ffn_sb2)
    x = x + _L1_xattn_ref(_layernorm(x, axis=-1), ctx_1024, ctx_1024, L1_xattn_igate_kernel, L1_xattn_igate_bias, L1_xattn_fgate_kernel, L1_xattn_fgate_bias, L1_xattn_outnorm_scale)
    x = x + _L1_ffn_ref(_layernorm(x, axis=-1), L1_ffn_gate_weight, L1_ffn_gate_up_proj, L1_ffn_down_proj)
    return x

_drawn_inputs = setup_inputs


def setup_inputs(seed=0):
    import zlib

    import numpy as np

    out = dict(_drawn_inputs(seed))
    spreads = {'L0_xattn_b_q': (0.0, 0.1),
     'L0_xattn_b_k': (0.0, 2.0),
     'L0_xattn_b_v': (0.0, 0.1),
     'L0_xattn_b_o': (0.0, 0.1),
     'L1_xattn_outnorm_scale': (1.0, 0.2)}
    factors = {'L0_ffn_gate_w': 8.0,
     'L0_ffn_gate_b': 8.0,
     'L0_ffn_w1': 8.0,
     'L0_ffn_b1': 8.0,
     'L0_ffn_w3': 8.0,
     'L0_ffn_b3': 8.0,
     'L0_ffn_w2': 8.0,
     'L0_ffn_b2': 7.76,
     'L0_ffn_sw1': 7.361,
     'L0_ffn_sb1': 8.0,
     'L0_ffn_sw3': 4.814,
     'L0_ffn_sb3': 8.0,
     'L0_ffn_sw2': 5.276,
     'L1_xattn_igate_bias': 64.0,
     'L1_xattn_fgate_kernel': 4.925,
     'L1_ffn_gate_weight': 8.0,
     'L1_ffn_gate_up_proj': 8.0,
     'L1_ffn_down_proj': 8.0,
     'L0_ffn_sb2': 2.971}
    for name, (base, spread) in spreads.items():
        noise = np.random.default_rng([zlib.crc32(name.encode()), seed]).standard_normal(out[name].shape)
        drawn = base * np.exp(spread * noise) if base else spread * noise
        out[name] = jnp.asarray(drawn.astype(out[name].dtype))
    for name, factor in factors.items():
        out[name] = (out[name] * factor).astype(out[name].dtype)
    return out
```

```python
from contextlib import ExitStack

import numpy as np
import concourse.bass as bass
from concourse import mybir

ALU = mybir.AluOpType
ACT = mybir.ActivationFunctionType
AX = mybir.AxisListType
F32 = mybir.dt.float32
BF16 = mybir.dt.bfloat16

P = 128
D = 128
B, S = 32, 64
TILES = B * S // P
TPC = 4
CHUNKS = TILES // TPC
N = TPC * P
SPC = N // S
BANK = 512

HEADS, DK = 16, 8
E0, HID0 = 8, 176
HCOLS = (E0 + 1) * HID0
HT = -(-HCOLS // P)
HLAST = HCOLS - (HT - 1) * P
NH, DH = 4, 32
E1, F1, TOP1, CAP = 32, 96, 8, 128
LN_EPS = 1e-5
MLSTM_EPS = 1e-6
GATE_ROW = 32
PART = 32
LOWEST = -1e30


def build(nc, t, out):
    with ExitStack() as ctx:
        def sb(name, shape, dt=F32):
            return ctx.enter_context(nc.sbuf_tensor(name, shape, dt))

        def sem(name):
            return ctx.enter_context(nc.semaphore(name))

        ps = ctx.enter_context(nc.psum_tensor("ps", [P, 8, BANK], F32))
        psb = ps[:, :, :].bitcast(BF16)

        x = sb("x_sb", [P, TILES, D])
        ctx_tok = sb("ctx_tok", [P, TILES, D])
        ctxT = sb("ctxT_sb", [P, TILES * P])
        xnT_all = sb("xnT_all", [P, TILES * P])
        loaded = {}
        for name, ap in t.items():
            if name in ("x", "ctx", "ctxT"):
                continue
            loaded[name] = sb(name + "_sb", list(ap.shape), ap.dtype)
        w = loaded
        ident, identb = w["ident"], w["identb"]

        ln_stats = sb("ln_stats", [P, TPC, 6])
        ln_mv = sb("ln_mv", [P, TPC, 2])
        ln_var = sb("ln_var", [P, TPC])
        ln_rstd = sb("ln_rstd", [P, TPC])
        xn = sb("xn", [P, TPC, D])
        xnT = sb("xnT", [P, N])
        ctxTc = sb("ctxTc", [P, N])
        carrier = sb("carrier", [P, 2])
        minus_half = sb("minus_half", [P, 16])

        load_w = sem("load_w")
        load_x = [sem(f"load_x{i}") for i in range(CHUNKS)]
        consts_set = sem("consts_set")
        set_step = sem("set_step")
        stored = sem("stored")

        class Layer:
            def __init__(self, k):
                self.ln_var_ready, self.ln_rstd_ready = sem(f"ln_var_ready_{k}"), sem(f"ln_rstd_ready_{k}")
                self.xn_ready, self.turned, self.xnT_ready = sem(f"xn_ready_{k}"), sem(f"turned_{k}"), sem(f"xnT_ready_{k}")
                self.x_updated = sem(f"x_updated_{k}")
                self.dve_step, self.pool_step = sem(f"dve_step_{k}"), sem(f"pool_step_{k}")

        A, Bf, Cg, C, Dl = (Layer(k) for k in ("attn", "ffn0", "gates", "mlstm", "ffn1"))

        class Steps:
            def __init__(self, eng, s, per_chunk, c):
                self.eng, self.s, self.per, self.c, self.n = eng, s, per_chunk, c, 0

            def step(self, ins):
                ins.then_inc(self.s, 1)
                self.n += 1
                self.eng.wait_ge(self.s, self.c * self.per + self.n)

            def step_by_memset(self, ins):
                self.step(ins)
                self.eng.memset(carrier[:, :], 0.0)

            def close(self):
                assert self.n == self.per, (self.n, self.per)

        def tile(c, j):
            return c * TPC + j

        LN_STEPS = 2

        def ln_dve(dve, L, c, st):
            for j in range(TPC):
                last = dve.bn_stats(ln_stats[:, j, :], x[:, bass.ds(tile(c, j), 1), :])
            st.step_by_memset(last)
            for j in range(TPC):
                last = dve.bn_aggr(ln_mv[:, j, :], ln_stats[:, j, :])
            st.step(last)
            dve.tensor_scalar(ln_var[:, :], ln_mv[:, :, 1], LN_EPS, None, ALU.add).then_inc(L.ln_var_ready, 1)
            dve.wait_ge(L.ln_rstd_ready, c + 1)
            for j in range(TPC):
                last = dve.tensor_scalar(xn[:, j, :], x[:, bass.ds(tile(c, j), 1), :].rearrange("p a d -> p (a d)"), ln_mv[:, j, 0:1],
                                         ln_rstd[:, j:j + 1], ALU.subtract, ALU.mult)
            last.then_inc(L.xn_ready, 1)

        def ln_pool(pool, L, c):
            pool.wait_ge(L.ln_var_ready, c + 1)
            pool.tensor_tensor(ln_rstd[:, :], ln_var[:, :], minus_half[:, 0:TPC],
                               ALU.pow).then_inc(L.ln_rstd_ready, 1)

        def ln_pe(pe, L, c, bank):
            pe.wait_ge(L.xn_ready, c + 1)
            for j in range(TPC):
                last = pe.transpose(ps[:, bank, j * P:(j + 1) * P], xn[:, j, :], ident[:, :])
            last.then_inc(L.turned, 1)

        def ln_act(act, L, c, bank):
            act.wait_ge(L.turned, c + 1)
            act.activation(xnT[:, :], ps[:, bank, :], ACT.Copy).then_inc(L.xnT_ready, 1)

        kT, qT = sb("kT", [P, N]), sb("qT", [P, N])
        kbd = sb("kbd", [P, 4, N])
        ctxdup = sb("ctxdup", [P, SPC, 2, S])
        vbd = sb("vbd", [P, SPC, HEADS // 2, 2, DK + 1])
        smax = sb("smax", [P, HEADS])
        attn_work = sb("attn_work", [P, 4 * HEADS * S])
        prob = attn_work[:, 0:2 * HEADS * S].rearrange("p (a h k) -> p a h k", a=2, h=HEADS)
        probT = attn_work[:, 2 * HEADS * S:].rearrange("p (a h q) -> p a h q", a=2, h=HEADS // 2)
        rden = sb("rden", [P, HEADS])
        o_tok = sb("o_tok", [P, TPC, D])
        oT = sb("oT", [P, N])
        ctx_copied, q_proj, k_proj, v_proj = sem("ctx_copied"), sem("q_proj"), sem("k_proj"), sem("v_proj")
        qT_ready, kT_ready, v_ready, kbd_ready = sem("qT_ready"), sem("kT_ready"), sem("v_ready"), sem("kbd_ready")
        scores_ready, centred, exp_done = sem("scores_ready"), sem("centred"), sem("exp_done")
        prob_turned, probT_a, probT_b = sem("prob_turned"), sem("probT_a"), sem("probT_b")
        pv_done, o_ready, o_turned, oT_ready, y_ready = (sem("pv_done"), sem("o_ready"), sem("o_turned"),
                                                         sem("oT_ready"), sem("y_ready"))
        A_DVE = LN_STEPS + 2 * TPC

        def attn_pool(pool):
            with pool.Fori(0, CHUNKS) as c:
                pool.wait_ge(A.x_updated, c + 1)
                chunk = ctxT[:, bass.ds(c * N, N)]
                pool.tensor_copy(ctxTc[:, :], chunk)
                for half in range(2):
                    last = pool.tensor_copy(ctxdup[:, :, half, :], chunk.rearrange("p (b s) -> p b s", s=S))
                last.then_inc(ctx_copied, 1)
                ln_pool(pool, A, c)

        def attn_dve(dve):
            with dve.Fori(0, CHUNKS) as c:
                st = Steps(dve, A.dve_step, A_DVE, c)
                ln_dve(dve, A, c, st)
                dve.wait_ge(kT_ready, c + 1)
                for h in range(4):
                    last = dve.tensor_scalar(kbd[:, h, :], kT[:, :], w["headmask"][:, h:h + 1], None, ALU.mult)
                last.then_inc(kbd_ready, 1)
                dve.wait_ge(v_proj, c + 1)
                for bank in range(2):
                    for half in range(2):
                        rows = slice(S * half, S * half + S)
                        src = ps[rows, 2 + bank, :].rearrange("p (b h d) -> p b h d", b=4, h=HEADS)
                        for g in range(4):
                            last = dve.tensor_copy(
                                vbd[rows, bank * 4 + g, :, half, 0:DK],
                                src[:, g, half:HEADS:2, :])
                last.then_inc(v_ready, 1)

                def softmax(j):
                    dve.wait_ge(scores_ready, c * TPC + j + 1)
                    sc = ps[:, 4:8, 0:4 * S].rearrange("p i (h k) -> p i h k", h=4)
                    st.step(dve.tensor_reduce(smax[:, :], sc, AX.X, ALU.max))
                    pr = prob[:, j % 2, :, :].rearrange("p (i h) k -> p i h k", i=4)
                    if j >= 2:
                        dve.wait_ge(prob_turned, c * TPC + j - 1)
                    for i in range(4):
                        last = dve.tensor_tensor(pr[:, i], sc[:, i],
                                                 smax[:, 4 * i:4 * i + 4].unsqueeze(2).to_broadcast([P, 4, S]),
                                                 ALU.subtract)
                    last.then_inc(centred, 1)

                def second_half(j):
                    dve.wait_ge(prob_turned, c * TPC + j + 1)
                    if j >= 2:
                        dve.wait_ge(pv_done, c * TPC + j - 1)
                    dve.tensor_copy(probT[:, j % 2, 4:8, :],
                                    ps[:, 3, :].rearrange("p (h q) -> p h q", h=4)).then_inc(probT_b, 1)

                def normalise(j):
                    dve.wait_ge(pv_done, c * TPC + j + 1)
                    o = ps[:, j % 2, 0:HEADS * (DK + 1)].rearrange("p (h d) -> p h d", d=DK + 1)
                    st.step(dve.reciprocal(rden[:, :], o[:, :, DK]))
                    dve.tensor_tensor(o_tok[:, j, :].rearrange("p (h d) -> p h d", d=DK), o[:, :, 0:DK],
                                      rden[:, :].unsqueeze(2).to_broadcast([P, HEADS, DK]),
                                      ALU.mult).then_inc(o_ready, 1)

                for j in range(TPC + 1):
                    if j < TPC:
                        softmax(j)
                    if j >= 1:
                        second_half(j - 1)
                        normalise(j - 1)
                dve.wait_ge(y_ready, c + 1)
                xc = x[:, bass.ds(c * TPC, TPC), :]
                st.close()
                dve.tensor_tensor(xc, xc, ps[:, 5, :].rearrange("p (j d) -> p j d", d=D),
                                  ALU.add).then_inc(A.x_updated, 1)
                dve.wait_ge(A.x_updated, c + 2)

        def attn_act(act):
            with act.Fori(0, CHUNKS) as c:
                ln_act(act, A, c, 0)
                act.wait_ge(q_proj, c + 1)
                act.activation(qT[:, :], ps[:, 1, :], ACT.Identity, bias=w["bq"][:, :]).then_inc(qT_ready, 1)
                act.wait_ge(k_proj, c + 1)
                act.activation(kT[:, :], ps[:, 4, :], ACT.Identity, bias=w["bk"][:, :]).then_inc(kT_ready, 1)

                def exps(j):
                    act.wait_ge(centred, c * TPC + j + 1)
                    act.activation(prob[:, j % 2, :, :], prob[:, j % 2, :, :], ACT.Exp,
                                   scale=float(1 / np.sqrt(np.float32(DK)))).then_inc(exp_done, 1)

                def first_half(j):
                    act.wait_ge(prob_turned, c * TPC + j + 1)
                    if j >= 2:
                        act.wait_ge(pv_done, c * TPC + j - 1)
                    act.activation(probT[:, j % 2, 0:4, :], ps[:, 2, :].rearrange("p (h q) -> p h q", h=4),
                                   ACT.Copy).then_inc(probT_a, 1)

                for j in range(TPC + 1):
                    if j < TPC:
                        exps(j)
                    if j >= 1:
                        first_half(j - 1)
                act.wait_ge(o_turned, c + 1)
                act.activation(oT[:, :], ps[:, 4, :], ACT.Identity, bias=w["bv"][:, :]).then_inc(oT_ready, 1)

        def attn_pe(pe):
            with pe.Fori(0, CHUNKS) as c:
                pe.wait_ge(A.x_updated, c + 1)
                pe.wait_ge(ctx_copied, c + 1)
                pe.matmul(ps[:, 4, :], w["wkT"][:, :], ctxTc[:, :], start=True, stop=True).then_inc(k_proj, 1)
                for b in range(SPC):
                    last = pe.matmul(ps[:, 2 + b // 4, (b % 4) * D:(b % 4 + 1) * D], ctxdup[:, b, :, :],
                                     w["wvT"][:, :], start=True, stop=True)
                last.then_inc(v_proj, 1)
                ln_pe(pe, A, c, 0)
                pe.wait_ge(A.xnT_ready, c + 1)
                pe.matmul(ps[:, 1, :], w["wqT"][:, :], xnT[:, :], start=True, stop=True).then_inc(q_proj, 1)

                def scores(j):
                    if j == 0:
                        pe.wait_ge(qT_ready, c + 1)
                        pe.wait_ge(kbd_ready, c + 1)
                    else:
                        pe.wait_ge(centred, c * TPC + j)
                    for i in range(4):
                        for b2 in range(2):
                            b = 2 * j + b2
                            last = pe.matmul(ps[S * b2:S * b2 + S, 4 + i, 0:4 * S],
                                             qT[32 * i:32 * i + 32, b * S:b * S + S],
                                             kbd[32 * i:32 * i + 32, :, b * S:b * S + S], start=True, stop=True)
                    last.then_inc(scores_ready, 1)

                def turn(j):
                    pe.wait_ge(exp_done, c * TPC + j + 1)
                    if j == 0:
                        pe.wait_ge(v_ready, c + 1)
                    else:
                        pe.wait_ge(probT_a, c * TPC + j)
                        pe.wait_ge(probT_b, c * TPC + j)
                    for hp in range(HEADS // 2):
                        last = pe.transpose(ps[:, 2 + hp // 4, (hp % 4) * P:(hp % 4 + 1) * P],
                                            prob[:, j % 2, 2 * hp:2 * hp + 2, :], ident[:, :])
                    last.then_inc(prob_turned, 1)

                def weighted(j):
                    pe.wait_ge(probT_a, c * TPC + j + 1)
                    pe.wait_ge(probT_b, c * TPC + j + 1)
                    if j >= 2:
                        pe.wait_ge(o_ready, c * TPC + j - 1)
                    W = 2 * (DK + 1)
                    for hp in range(HEADS // 2):
                        for b2 in range(2):
                            last = pe.matmul(ps[S * b2:S * b2 + S, j % 2, hp * W:(hp + 1) * W],
                                             probT[:, j % 2, hp, S * b2:S * b2 + S],
                                             vbd[:, 2 * j + b2, hp, :, :], start=True, stop=True)
                    last.then_inc(pv_done, 1)

                scores(0)
                for j in range(TPC):
                    if j + 1 < TPC:
                        scores(j + 1)
                    turn(j)
                    weighted(j)
                pe.wait_ge(o_ready, c * TPC + TPC)
                for j in range(TPC):
                    last = pe.transpose(ps[:, 4, j * P:(j + 1) * P], o_tok[:, j, :], ident[:, :])
                last.then_inc(o_turned, 1)
                pe.wait_ge(oT_ready, c + 1)
                for j in range(TPC):
                    pe.matmul(ps[:, 5, j * D:(j + 1) * D], oT[:, j * P:(j + 1) * P], w["woT"][:, :],
                              start=True, stop=False)
                    last = pe.matmul(ps[:, 5, j * D:(j + 1) * D], w["ones_row"][:, :], w["bo"][:, :],
                                     start=False, stop=True)
                last.then_inc(y_ready, 1)

        logit = sb("logit", [P, TPC, E0])
        lmax = sb("lmax", [P, TPC])
        lsum = sb("lsum", [P, TPC])
        gate = sb("gate", [P, TPC, E0])
        biased = sb("biased", [P, TPC, 16])
        top8 = sb("top8", [P, TPC, 8])
        chosen = sb("chosen", [P, TPC, 8])
        rest = sb("rest", [P, TPC, 16])
        rw = sb("rw", [P, TPC, E0 + 1])
        rw3 = sb("rw3", [P, TPC, 3 * PART], BF16)
        rwrem = sb("rwrem", [P, TPC, E0])
        rwT = sb("rwT", [E0 + 1, N])
        rw3T = sb("rw3T", [3 * PART, N], BF16)
        up_a = sb("up_a", [P, 2, N])
        zbuf = sb("zbuf", [P, 2, N])
        hact = sb("hact", [P, 2, N])
        hbuf = sb("hbuf", [P, 2, N])
        yT = sb("yT", [P, N])
        names = ("logits", "l_centred", "l_exp", "rw_ready", "rw_turned", "rwT_ready", "rw3T_ready", "a_ps", "c_ps", "w_ps",
                 "a_ready", "z_ready", "s_ready", "h_ready", "yT_ready", "y_turned", "h_used")
        s0 = {n: sem("f0_" + n) for n in names}
        s1 = {n: sem("f1_" + n) for n in names}

        def moe_tail_act(act, s, c, per):
            act.wait_ge(s["h_used"], (c + 1) * per)
            act.activation(yT[:, :], ps[:, 0, :], ACT.Copy).then_inc(s["yT_ready"], 1)

        def moe_tail_pe(pe, s, c):
            pe.wait_ge(s["yT_ready"], c + 1)
            for j in range(TPC):
                last = pe.transpose(ps[:, 1, j * P:(j + 1) * P], yT[:, j * P:(j + 1) * P], ident[:, :])
            last.then_inc(s["y_turned"], 1)

        def moe_tail_dve(dve, s, L, c):
            dve.wait_ge(s["y_turned"], c + 1)
            xc = x[:, bass.ds(c * TPC, TPC), :]
            dve.tensor_tensor(xc, xc, ps[:, 1, :].rearrange("p (j d) -> p j d", d=D),
                              ALU.add).then_inc(L.x_updated, 1)
            dve.wait_ge(L.x_updated, c + 2)

        def hidden(k):
            return HLAST if k == HT - 1 else P

        B_DVE = LN_STEPS + 15

        def ffn0_pool(pool):
            pool.wait_ge(A.x_updated, CHUNKS + 1)
            with pool.Fori(0, CHUNKS) as c:
                ln_pool(pool, Bf, c)

        def softmax_dve(dve, st, s, c, bank, E, lg, pr):
            dve.wait_ge(s["logits"], c + 1)
            src = ps[:, bank, 0:TPC * E].rearrange("p (j e) -> p j e", e=E)
            st.step(dve.tensor_reduce(lmax[:, :], src, AX.X, ALU.max))
            dve.tensor_tensor(lg, src, lmax[:, :].unsqueeze(2).to_broadcast([P, TPC, E]),
                              ALU.subtract).then_inc(s["l_centred"], 1)
            dve.wait_ge(s["l_exp"], c + 1)
            st.step(dve.tensor_reduce(lsum[:, :], lg, AX.X, ALU.add))
            st.step(dve.reciprocal(lsum[:, :], lsum[:, :]))
            st.step(dve.tensor_tensor(pr, lg, lsum[:, :].unsqueeze(2).to_broadcast([P, TPC, E]), ALU.mult))

        def split3(dve, st, src, rem, dst, E, s):
            st.step(dve.tensor_copy(dst[:, :, 0:E], src))
            st.step(dve.tensor_tensor(rem, src, dst[:, :, 0:E], ALU.subtract))
            st.step(dve.tensor_copy(dst[:, :, PART:PART + E], rem))
            st.step(dve.tensor_tensor(rem, rem, dst[:, :, PART:PART + E], ALU.subtract))
            dve.tensor_copy(dst[:, :, 2 * PART:2 * PART + E], rem).then_inc(s["rw_ready"], 1)

        def ffn0_dve(dve):
            s = s0
            with dve.Fori(0, CHUNKS) as c:
                st = Steps(dve, Bf.dve_step, B_DVE, c)
                ln_dve(dve, Bf, c, st)
                softmax_dve(dve, st, s, c, 1, E0, logit[:, :, :], gate[:, :, :])
                st.step_by_memset(dve.tensor_tensor(biased[:, :, 0:E0], gate[:, :, :],
                                          w["gate_b"][:, :].unsqueeze(1).to_broadcast([P, TPC, E0]), ALU.add))
                for j in range(TPC):
                    last = dve.max(top8[:, j, :], biased[:, j, :])
                st.step(last)
                st.step_by_memset(dve.tensor_copy(chosen[:, :, 0:2], top8[:, :, 0:2]))
                for j in range(TPC):
                    last = dve.match_replace(rest[:, j, :], chosen[:, j, :], biased[:, j, :], 2 * LOWEST)
                st.step(last)
                st.step(dve.tensor_tensor(rest[:, :, 0:E0], rest[:, :, 0:E0], biased[:, :, 0:E0], ALU.not_equal))
                st.step(dve.tensor_tensor(rw[:, :, 0:E0], gate[:, :, :], rest[:, :, 0:E0], ALU.mult))
                split3(dve, st, rw[:, :, 0:E0], rwrem[:, :, :], rw3, E0, s)
                dve.wait_ge(s["rw_turned"], c + 1)
                st.step(dve.tensor_copy(rwT[:, :], ps[0:E0 + 1, 2, :]))
                dve.tensor_copy(rw3T[:, :], psb[0:3 * PART, 3, 0:N]).then_inc(s["rw3T_ready"], 1)

                def gated(k):
                    M, g = hidden(k), c * HT + k
                    dve.wait_ge(s["a_ready"], g + 1)
                    dve.wait_ge(s["c_ps"], g + 1)
                    if k >= 2:
                        dve.wait_ge(s["s_ready"], g - 1)
                    dve.scalar_tensor_tensor(zbuf[0:M, k % 2, :], ps[0:M, 4 + k % 2, :], w["b3"][0:M, k:k + 1],
                                             up_a[0:M, k % 2, :], ALU.add, ALU.mult).then_inc(s["z_ready"], 1)

                def weigh(k):
                    M, g = hidden(k), c * HT + k
                    dve.wait_ge(s["s_ready"], g + 1)
                    dve.wait_ge(s["w_ps"], g + 1)
                    if k >= 2:
                        dve.wait_ge(s["h_used"], g - 1)
                    dve.tensor_tensor(hbuf[0:M, k % 2, :], hact[0:M, k % 2, :], ps[0:M, 6 + k % 2, :],
                                      ALU.mult).then_inc(s["h_ready"], 1)

                for k in range(HT + 1):
                    if k < HT:
                        gated(k)
                    if k >= 1:
                        weigh(k - 1)
                moe_tail_dve(dve, s, Bf, c)
                st.close()

        def ffn0_act(act):
            s = s0
            with act.Fori(0, CHUNKS) as c:
                ln_act(act, Bf, c, 0)
                act.wait_ge(s["l_centred"], c + 1)
                act.activation(logit[:, :, :], logit[:, :, :], ACT.Exp).then_inc(s["l_exp"], 1)

                def up(k):
                    M, g = hidden(k), c * HT + k
                    act.wait_ge(s["a_ps"], g + 1)
                    if k >= 2:
                        act.wait_ge(s["z_ready"], g - 1)
                    act.activation(up_a[0:M, k % 2, :], ps[0:M, 2 + k % 2, :], ACT.Identity,
                                   bias=w["b1"][0:M, k:k + 1]).then_inc(s["a_ready"], 1)

                def silu(k):
                    M, g = hidden(k), c * HT + k
                    act.wait_ge(s["z_ready"], g + 1)
                    if k >= 2:
                        act.wait_ge(s["h_ready"], g - 1)
                    act.activation(hact[0:M, k % 2, :], zbuf[0:M, k % 2, :],
                                   ACT.Silu).then_inc(s["s_ready"], 1)

                for k in range(HT + 1):
                    if k < HT:
                        up(k)
                    if k >= 1:
                        silu(k - 1)
                moe_tail_act(act, s, c, HT)

        def ffn0_pe(pe):
            s = s0
            pe.wait_ge(A.x_updated, CHUNKS + 1)
            with pe.Fori(0, CHUNKS) as c:
                pe.wait_ge(Bf.x_updated, c + 1)
                ln_pe(pe, Bf, c, 0)
                pe.wait_ge(Bf.xnT_ready, c + 1)
                for j in range(TPC):
                    last = pe.matmul(ps[:, 1, j * E0:(j + 1) * E0], xnT[:, j * P:(j + 1) * P], w["gwT0"][:, :],
                                     start=True, stop=True)
                last.then_inc(s["logits"], 1)
                pe.wait_ge(s["rw_ready"], c + 1)
                for j in range(TPC):
                    pe.transpose(ps[0:E0 + 1, 2, j * P:(j + 1) * P], rw[:, j, :], ident[:, :])
                    last = pe.transpose(psb[0:3 * PART, 3, j * P:(j + 1) * P], rw3[:, j, :], identb[:, :])
                last.then_inc(s["rw_turned"], 1)
                pe.wait_ge(s["rw3T_ready"], c + 1)
                pe.matmul(ps[:, 0, :], w["b2"][:, :], rwT[:, :], start=True, stop=False, skip_group_check=True)

                def products(k):
                    M, g = hidden(k), c * HT + k
                    cols = slice(k * P, k * P + M)
                    if k >= 2:
                        pe.wait_ge(s["a_ready"], g - 1)
                    pe.matmul(ps[0:M, 2 + k % 2, :], w["w1"][:, cols], xnT[:, :], start=True,
                              stop=True).then_inc(s["a_ps"], 1)
                    if k >= 2:
                        pe.wait_ge(s["z_ready"], g - 1)
                    pe.matmul(ps[0:M, 4 + k % 2, :], w["w3"][:, cols], xnT[:, :], start=True,
                              stop=True).then_inc(s["c_ps"], 1)
                    if k >= 2:
                        pe.wait_ge(s["h_ready"], g - 1)
                    pe.matmul(ps[0:M, 6 + k % 2, :], w["sel0"][:, cols], rw3T[:, :], start=True,
                              stop=True).then_inc(s["w_ps"], 1)

                def down(k):
                    M, g = hidden(k), c * HT + k
                    pe.wait_ge(s["h_ready"], g + 1)
                    lhs = w["w2"][:, k, :] if k < HT - 1 else w["w2last"][:, :]
                    mm = pe.matmul(ps[:, 0, :], lhs, hbuf[0:M, k % 2, :], start=False,
                                   stop=(k == HT - 1), skip_group_check=True)
                    mm.then_inc(s["h_used"], 1)

                for k in range(HT + 2):
                    if k < HT:
                        products(k)
                    if k >= 2:
                        down(k - 2)
                moe_tail_pe(pe, s, c)

        GR = GATE_ROW + NH
        gk_ctx = sb("gk_ctx", [P, GR])
        gates = sb("gates", [GR, TILES * P])
        ig_r, fg_r = sb("ig_r", [P, S]), sb("fg_r", [P, S])
        t0, t1, t2 = sb("row_t0", [P, S]), sb("row_t1", [P, S]), sb("row_t2", [P, S])
        cum, g_r, m_r, neg_m, en_r = (sb("cum", [P, S]), sb("g_r", [P, S]), sb("m_r", [P, S]), sb("neg_m", [P, S]),
                                      sb("en_r", [P, S]))
        ones_r = sb("ones_r", [P, S])
        g4 = kbd[0:NH, :, :].rearrange("p h n -> p (h n)")
        m2 = attn_work[0:2, :].rearrange("p (a h s) -> p a h s", a=TILES, h=NH)
        en_tok = sb("en_tok", [P, TILES, NH])
        xnT_kept, gates_ps, gates_ready, rows_in = sem("xnT_kept"), sem("gates_ps"), sem("gates_ready"), sem("rows_in")
        row_dve, row_act, row_ready, rows_out = sem("row_dve"), sem("row_act"), sem("row_ready"), sem("rows_out")
        en_turned, en_copied, gk_summed = sem("en_turned"), sem("en_copied"), sem("gk_summed")

        def gates_pool(pool):
            pool.wait_ge(Bf.x_updated, CHUNKS + 1)
            with pool.Fori(0, CHUNKS) as c:
                ln_pool(pool, Cg, c)
                pool.wait_ge(Cg.xnT_ready, c + 1)
                pool.tensor_copy(xnT_all[:, bass.ds(c * N, N)], xnT[:, :]).then_inc(xnT_kept, 1)

        def gates_pe(pe):
            pe.wait_ge(Bf.x_updated, CHUNKS + 1)
            pe.wait_ge(gk_summed, 1)
            with pe.Fori(0, CHUNKS) as c:
                pe.wait_ge(gates_ready, c + 1)
                ln_pe(pe, Cg, c, 0)
                pe.wait_ge(Cg.xnT_ready, c + 1)
                pe.matmul(ps[0:GR, 1, :], w["gk_q"][:, :], xnT[:, :], start=True, stop=False)
                pe.matmul(ps[0:GR, 1, :], gk_ctx[:, :], ctxT[:, bass.ds(c * N, N)], start=False,
                          stop=True).then_inc(gates_ps, 1)
            pe.wait_ge(row_ready, 1)
            pe.transpose(ps[0:S, 2, 0:P], en_r[:, :], ident[:, :]).then_inc(en_turned, 1)

        def gates_act(act):
            with act.Fori(0, CHUNKS) as c:
                act.wait_ge(xnT_kept, c + 1)
                ln_act(act, Cg, c, 0)
                act.wait_ge(gates_ps, c + 1)
                act.activation(gates[:, bass.ds(c * N, N)], ps[0:GR, 1, :], ACT.Identity,
                               bias=w["gk_bias"][:, :]).then_inc(gates_ready, 1)
            act.wait_ge(rows_in, 16 * 2 * NH)
            act.activation(t0[:, :], fg_r[:, :], ACT.Abs).then_inc(row_act, 1)
            act.wait_ge(row_act, 1)
            act.activation(t0[:, :], t0[:, :], ACT.Exp, scale=-1.0).then_inc(row_act, 1)
            act.wait_ge(row_act, 2)
            act.activation(t0[:, :], t0[:, :], ACT.Ln, bias=1.0).then_inc(row_act, 1)
            act.wait_ge(row_dve, 6)
            act.activation(en_r[:, :], t2[:, :], ACT.Exp, scale=-1.0).then_inc(row_ready, 1)

        def gates_dve(dve):
            dve.tensor_tensor(gk_ctx[:, :], w["gk_k"][:, :], w["gk_v"][:, :], ALU.add).then_inc(gk_summed, 1)
            with dve.Fori(0, CHUNKS) as c:
                dve.wait_ge(gates_ready, c + 1)
                st = Steps(dve, Cg.dve_step, LN_STEPS, c)
                ln_dve(dve, Cg, c, st)
                st.close()
            dve.wait_ge(rows_in, 16 * 2 * NH)
            dve.tensor_scalar(t1[:, :], fg_r[:, :], 0.0, None, ALU.min).then_inc(row_dve, 1)
            dve.wait_ge(row_dve, 1)
            dve.wait_ge(row_act, 3)
            dve.tensor_tensor(t1[:, :], t1[:, :], t0[:, :], ALU.subtract).then_inc(row_dve, 1)
            dve.wait_ge(row_dve, 2)
            dve.tensor_tensor_scan(cum[:, :], ones_r[:, :], t1[:, :], 0.0, ALU.mult, ALU.add).then_inc(row_dve, 1)
            dve.wait_ge(row_dve, 3)
            dve.tensor_tensor(g_r[:, :], ig_r[:, :], cum[:, :], ALU.subtract).then_inc(row_dve, 1)
            dve.wait_ge(row_dve, 4)
            dve.tensor_tensor_scan(m_r[:, :], g_r[:, :], g_r[:, :], -3e38, ALU.max, ALU.max).then_inc(row_dve, 1)
            dve.wait_ge(row_dve, 5)
            dve.tensor_tensor(t2[:, :], cum[:, :], m_r[:, :], ALU.add).then_inc(row_dve, 1)
            dve.tensor_scalar(neg_m[:, :], m_r[:, :], -1.0, None, ALU.mult).then_inc(row_dve, 1)
            dve.wait_ge(en_turned, 1)
            src = ps[0:S, 2, 0:P].rearrange("s (h p b) -> s p h b", h=NH, b=2)
            for b2 in range(2):
                last = dve.tensor_copy(en_tok[S * b2:S * b2 + S, :, :], src[:, :, :, b2])
            last.then_inc(en_copied, 1)

        def gates_sp(sp):
            sp.wait_ge(gates_ready, CHUNKS + 1)
            for h in range(NH):
                for row, dst in ((h, ig_r), (GATE_ROW + h, fg_r)):
                    sp.dma_start(dst[B * h:B * h + B, :],
                                 gates[row:row + 1, :].rearrange("o (b s) -> o b s", s=S)).then_inc(rows_in, 16)
            sp.wait_ge(row_dve, 7)
            for h in range(NH):
                sp.dma_start(g4[h:h + 1, :].rearrange("o (b s) -> o b s", s=S),
                             g_r[B * h:B * h + B, :]).then_inc(rows_out, 16)
                for b2 in range(2):
                    sp.dma_start(m2[b2:b2 + 1, :, h, :], neg_m[B * h + b2:B * h + B:2, :]).then_inc(rows_out, 16)

        xnTc, g4c = sb("xnTc", [P, N]), sb("g4c", [NH, N])
        vext = sb("vext", [P, 2, TPC, NH, DH + 1])
        dmat = up_a[:, :, :].rearrange("p a (b h s) -> p (a b) h s", b=2, h=NH)
        cmat = zbuf[:, :, :].rearrange("p a (b h s) -> p (a b) h s", b=2, h=NH)
        n_a, n_b = sb("n_a", [P, TPC, NH]), sb("n_b", [P, TPC, NH])
        ho = hact[:, 0, :].rearrange("p (j h d) -> p j h d", j=TPC, h=NH)
        hsq = hbuf[:, 0, :].rearrange("p (j h d) -> p j h d", j=TPC, h=NH)
        hm, hv = sb("hm", [P, TPC * NH]), sb("hv", [P, TPC * NH])
        c_copied, xnTc_ready, qk_ps, logd_ps, d_ready = (sem("c_copied"), sem("xnTc_ready"), sem("qk_ps"),
                                                         sem("logd_ps"), sem("d_ready"))
        cmat_ready, hc_ready, hsq_ready, hvar_ready, hrstd_ready, h_ps = (
            sem("cmat_ready"), sem("hc_ready"), sem("hsq_ready"), sem("hvar_ready"), sem("hrstd_ready"), sem("h_ps"))
        C_DVE = 11

        def mlstm_pool(pool):
            pool.wait_ge(rows_out, 16 * 3 * NH)
            with pool.Fori(0, CHUNKS) as c:
                pool.wait_ge(C.x_updated, c + 1)
                pool.tensor_copy(ctxTc[:, :], ctxT[:, bass.ds(c * N, N)])
                pool.tensor_copy(g4c[:, :], g4[:, bass.ds(c * N, N)]).then_inc(C.pool_step, 1)
                pool.wait_ge(C.pool_step, c + 1)
                for b2 in range(2):
                    rows = slice(S * b2, S * b2 + S)
                    last = pool.tensor_copy(
                        vext[rows, b2, :, :, 0:DH],
                        ctx_tok[rows, bass.ds(c * TPC, TPC), :].rearrange("p j (h d) -> p j h d", h=NH))
                last.then_inc(c_copied, 1)
                pool.wait_ge(hvar_ready, c + 1)
                pool.tensor_tensor(hv[:, :], hv[:, :], minus_half[:, :], ALU.pow).then_inc(hrstd_ready, 1)

        def mlstm_act(act):
            act.wait_ge(xnT_kept, CHUNKS + 1)
            with act.Fori(0, CHUNKS) as c:
                act.wait_ge(C.x_updated, c + 1)
                act.activation(xnTc[:, :], xnT_all[:, bass.ds(c * N, N)], ACT.Copy).then_inc(xnTc_ready, 1)
                act.wait_ge(logd_ps, c + 1)
                act.activation(dmat[:, :, :, :].rearrange("p j h s -> p (j h s)"),
                               ps[:, 4:6, :].rearrange("p a n -> p (a n)"), ACT.Exp).then_inc(d_ready, 1)
                act.wait_ge(hc_ready, c + 1)
                act.activation(hsq[:, :, :, :], ho[:, :, :, :], ACT.Square).then_inc(hsq_ready, 1)

        def mlstm_pe(pe):
            pe.wait_ge(en_copied, 1)
            with pe.Fori(0, CHUNKS) as c:
                pe.wait_ge(C.x_updated, c + 1)
                pe.wait_ge(c_copied, c + 1)
                for j in range(TPC):
                    o = ps[:, 4 + j // 2, (j % 2) * NH * S:(j % 2 + 1) * NH * S]
                    pe.matmul(o, g4c[:, j * P:(j + 1) * P], w["head_ind"][:, :], start=True, stop=False)
                    pe.matmul(o, w["seq_sel"][:, :],
                              m2[:, bass.ds(c * TPC + j, 1), :, :].rearrange("b a h s -> b (a h s)"),
                              start=False, stop=False)
                    last = pe.matmul(o, identb[:, :], w["causal"][:, :], start=False, stop=True)
                last.then_inc(logd_ps, 1)
                pe.wait_ge(xnTc_ready, c + 1)
                for j in range(TPC):
                    for h in range(NH):
                        for b2 in range(2):
                            rows, cols = slice(DH * h, DH * h + DH), slice((2 * j + b2) * S, (2 * j + b2 + 1) * S)
                            last = pe.matmul(ps[S * b2:S * b2 + S, h, j * S:(j + 1) * S], ctxTc[rows, cols],
                                             xnTc[rows, cols], start=True, stop=True)
                last.then_inc(qk_ps, 1)
                pe.wait_ge(cmat_ready, c + 1)
                for j in range(TPC):
                    for h in range(NH):
                        for b2 in range(2):
                            col = (j % 2) * NH * (DH + 1) + h * (DH + 1)
                            last = pe.matmul(ps[S * b2:S * b2 + S, 6 + j // 2, col:col + DH + 1],
                                             cmat[:, j, h, :], vext[:, b2, j, h, :], start=True, stop=True)
                last.then_inc(h_ps, 1)

        def mlstm_dve(dve):
            dve.wait_ge(en_copied, 1)
            with dve.Fori(0, CHUNKS) as c:
                st = Steps(dve, C.dve_step, C_DVE, c)
                dve.wait_ge(d_ready, c + 1)
                dve.wait_ge(qk_ps, c + 1)
                for j in range(TPC):
                    last = dve.scalar_tensor_tensor(cmat[:, j, :, :], ps[:, 0:NH, j * S:(j + 1) * S],
                                                    float(1 / np.sqrt(np.float32(DH))), dmat[:, j, :, :],
                                                    ALU.mult, ALU.mult)
                last.then_inc(cmat_ready, 1)
                dve.wait_ge(h_ps, c + 1)
                W = DH + 1
                o = ps[:, 6:8, 0:2 * NH * W].rearrange("p a (n d) -> p a n d", d=W)
                two = lambda a: a.rearrange("p (a j) h -> p a (j h)", a=2)
                na, nb = two(n_a[:, :, :]), two(n_b[:, :, :])
                st.step(dve.tensor_copy(na, o[:, :, :, DH]))
                st.step(dve.scalar_tensor_tensor(n_b[:, :, :], n_a[:, :, :], -1.0, n_a[:, :, :], ALU.mult, ALU.max))
                st.step(dve.tensor_tensor(n_a[:, :, :], n_b[:, :, :], en_tok[:, bass.ds(c * TPC, TPC), :], ALU.max))
                st.step(dve.tensor_scalar(n_b[:, :, :], n_a[:, :, :], MLSTM_EPS, None, ALU.add))
                st.step(dve.reciprocal(n_a[:, :, :], n_b[:, :, :]))
                hn = ho[:, :, :, :].rearrange("p j h d -> p (j h) d")
                st.step(dve.tensor_tensor(ho[:, :, :, :].rearrange("p (a j) h d -> p a (j h) d", a=2), o[:, :, :, 0:DH],
                                          na.unsqueeze(3).to_broadcast([P, 2, 2 * NH, DH]), ALU.mult))
                st.step(dve.tensor_reduce(hm[:, :], hn, AX.X, ALU.add))
                st.step(dve.tensor_scalar(hm[:, :], hm[:, :], -1.0 / DH, None, ALU.mult))
                dve.tensor_tensor(hn, hn, hm[:, :].unsqueeze(2).to_broadcast([P, TPC * NH, DH]),
                                  ALU.add).then_inc(hc_ready, 1)
                dve.wait_ge(hsq_ready, c + 1)
                st.step(dve.tensor_reduce(hv[:, :], hsq[:, :, :, :].rearrange("p j h d -> p (j h) d"), AX.X, ALU.add))
                dve.tensor_scalar(hv[:, :], hv[:, :], 1.0 / DH, LN_EPS, ALU.mult, ALU.add).then_inc(hvar_ready, 1)
                dve.wait_ge(hrstd_ready, c + 1)
                st.step(dve.tensor_tensor(hn, hn, hv[:, :].unsqueeze(2).to_broadcast([P, TPC * NH, DH]), ALU.mult))
                hd = ho[:, :, :, :].rearrange("p j h d -> p j (h d)")
                st.step(dve.tensor_tensor(hd, hd, w["out_scale"][:, :].unsqueeze(1).to_broadcast([P, TPC, D]),
                                          ALU.mult))
                st.close()
                xc = x[:, bass.ds(c * TPC, TPC), :]
                dve.tensor_tensor(xc, xc, hd, ALU.add).then_inc(C.x_updated, 1)
                dve.wait_ge(C.x_updated, c + 2)

        logit1, gate1 = sb("logit1", [P, TPC, E1]), sb("gate1", [P, TPC, E1])
        rest1, mask1 = sb("rest1", [P, TPC, E1]), sb("mask1", [P, TPC, E1], BF16)
        gsel, pos = sb("gsel", [P, TPC, E1]), sb("pos", [P, TPC, E1])
        counts = sb("counts", [P, TPC + 1, E1])
        rem1 = sb("rem1", [P, TPC, E1])
        rw3b = sb("rw3b", [P, TPC, 3 * PART], BF16)
        D_DVE = LN_STEPS + 21
        mask_ready, ranks_ps = sem("mask_ready"), sem("ranks_ps")

        def ffn1_pool(pool):
            pool.wait_ge(C.x_updated, CHUNKS + 1)
            with pool.Fori(0, CHUNKS) as c:
                ln_pool(pool, Dl, c)

        def ffn1_dve(dve):
            s = s1
            with dve.Fori(0, CHUNKS) as c:
                st = Steps(dve, Dl.dve_step, D_DVE, c)
                ln_dve(dve, Dl, c, st)
                softmax_dve(dve, st, s, c, 1, E1, logit1[:, :, :], gate1[:, :, :])
                dve.memset(carrier[:, :], 0.0)
                for j in range(TPC):
                    last = dve.max(top8[:, j, :], gate1[:, j, :])
                st.step_by_memset(last)
                for j in range(TPC):
                    last = dve.match_replace(rest1[:, j, :], top8[:, j, :], gate1[:, j, :], -1.0)
                st.step(last)
                dve.tensor_tensor(mask1[:, :, :], rest1[:, :, :], gate1[:, :, :],
                                  ALU.not_equal).then_inc(mask_ready, 1)
                dve.wait_ge(mask_ready, c + 1)
                st.step(dve.tensor_tensor(gsel[:, :, :], gate1[:, :, :], mask1[:, :, :], ALU.mult))
                st.step(dve.tensor_reduce(lsum[:, :], gsel[:, :, :], AX.X, ALU.add))
                st.step(dve.reciprocal(lmax[:, :], lsum[:, :]))
                st.step(dve.tensor_tensor(gsel[:, :, :], gsel[:, :, :],
                                          lmax[:, :].unsqueeze(2).to_broadcast([P, TPC, E1]), ALU.mult))
                dve.wait_ge(ranks_ps, c + 1)
                ranks = ps[:, 2, 0:TPC * E1].rearrange("p (j e) -> p j e", e=E1)
                totals = ps[:, 2, TPC * E1:2 * TPC * E1].rearrange("p (j e) -> p j e", e=E1)
                for j in range(TPC):
                    st.step(dve.tensor_tensor(counts[:, j + 1, :], counts[:, j, :], totals[:, j, :], ALU.add))
                st.step(dve.tensor_tensor(pos[:, :, :], ranks, counts[:, 0:TPC, :], ALU.add))
                st.step(dve.scalar_tensor_tensor(gsel[:, :, :], pos[:, :, :], float(CAP), gsel[:, :, :],
                                                 ALU.is_lt, ALU.mult))
                st.step(dve.tensor_copy(counts[:, 0, :], counts[:, TPC, :]))
                split3(dve, st, gsel[:, :, :], rem1[:, :, :], rw3b, E1, s)
                dve.wait_ge(s["rw_turned"], c + 1)
                dve.tensor_copy(rw3T[:, :], psb[0:3 * PART, 3, 0:N]).then_inc(s["rw3T_ready"], 1)

                def gated(k):
                    g = c * E1 + k
                    dve.wait_ge(s["s_ready"], g + 1)
                    dve.wait_ge(s["c_ps"], g + 1)
                    if k >= 2:
                        dve.wait_ge(s["h_ready"], g - 1)
                    dve.tensor_tensor(zbuf[0:F1, k % 2, :], hact[0:F1, k % 2, :], ps[0:F1, 4 + k % 2, :],
                                      ALU.mult).then_inc(s["z_ready"], 1)

                def weigh(k):
                    g = c * E1 + k
                    dve.wait_ge(s["z_ready"], g + 1)
                    dve.wait_ge(s["w_ps"], g + 1)
                    if k >= 2:
                        dve.wait_ge(s["h_used"], g - 1)
                    dve.tensor_tensor(hbuf[0:F1, k % 2, :], zbuf[0:F1, k % 2, :], ps[0:F1, 6 + k % 2, :],
                                      ALU.mult).then_inc(s["h_ready"], 1)

                for k in range(E1 + 1):
                    if k < E1:
                        gated(k)
                    if k >= 1:
                        weigh(k - 1)
                moe_tail_dve(dve, s, Dl, c)
                st.close()

        def ffn1_act(act):
            s = s1
            with act.Fori(0, CHUNKS) as c:
                ln_act(act, Dl, c, 0)
                act.wait_ge(s["l_centred"], c + 1)
                act.activation(logit1[:, :, :], logit1[:, :, :], ACT.Exp).then_inc(s["l_exp"], 1)
                for k in range(E1):
                    g = c * E1 + k
                    act.wait_ge(s["a_ps"], g + 1)
                    if k >= 2:
                        act.wait_ge(s["z_ready"], g - 1)
                    act.activation(hact[0:F1, k % 2, :], ps[0:F1, 2 + k % 2, :],
                                   ACT.Silu).then_inc(s["s_ready"], 1)
                moe_tail_act(act, s, c, E1)

        def ffn1_pe(pe):
            s = s1
            pe.wait_ge(C.x_updated, CHUNKS + 1)
            with pe.Fori(0, CHUNKS) as c:
                pe.wait_ge(Dl.x_updated, c + 1)
                ln_pe(pe, Dl, c, 0)
                pe.wait_ge(Dl.xnT_ready, c + 1)
                for j in range(TPC):
                    last = pe.matmul(ps[:, 1, j * E1:(j + 1) * E1], xnT[:, j * P:(j + 1) * P], w["gwT1"][:, :],
                                     start=True, stop=True)
                last.then_inc(s["logits"], 1)
                pe.wait_ge(mask_ready, c + 1)
                mask = mask1[:, :, :].rearrange("p j e -> p (j e)")
                pe.matmul(ps[:, 2, 0:TPC * E1], w["before"][:, :], mask, start=True, stop=True)
                pe.matmul(ps[:, 2, TPC * E1:2 * TPC * E1], w["onesb"][:, :], mask, start=True,
                          stop=True).then_inc(ranks_ps, 1)
                pe.wait_ge(s["rw_ready"], c + 1)
                for j in range(TPC):
                    last = pe.transpose(psb[0:3 * PART, 3, j * P:(j + 1) * P], rw3b[:, j, :], identb[:, :])
                last.then_inc(s["rw_turned"], 1)
                pe.wait_ge(s["rw3T_ready"], c + 1)

                def products(k):
                    g = c * E1 + k
                    if k >= 2:
                        pe.wait_ge(s["s_ready"], g - 1)
                    pe.matmul(ps[0:F1, 2 + k % 2, :], w["wg"][:, k, :], xnT[:, :], start=True,
                              stop=True).then_inc(s["a_ps"], 1)
                    if k >= 2:
                        pe.wait_ge(s["z_ready"], g - 1)
                    pe.matmul(ps[0:F1, 4 + k % 2, :], w["wu"][:, k, :], xnT[:, :], start=True,
                              stop=True).then_inc(s["c_ps"], 1)
                    if k >= 2:
                        pe.wait_ge(s["h_ready"], g - 1)
                    pe.matmul(ps[0:F1, 6 + k % 2, :], w["sel1"][:, k, :], rw3T[:, :], start=True,
                              stop=True).then_inc(s["w_ps"], 1)

                def down(k):
                    pe.wait_ge(s["h_ready"], c * E1 + k + 1)
                    pe.matmul(ps[:, 0, :], w["wd"][:, k, :], hbuf[0:F1, k % 2, :], start=(k == 0),
                              stop=(k == E1 - 1), skip_group_check=True).then_inc(s["h_used"], 1)

                for k in range(E1 + 2):
                    if k < E1:
                        products(k)
                    if k >= 2:
                        down(k - 2)
                moe_tail_pe(pe, s, c)

        block = ctx.enter_context(nc.Block())
        order = list(w)

        @block.sync
        def _(sp):
            for c in range(CHUNKS):
                cols = slice(c * N, (c + 1) * N)
                tl = slice(c * TPC, (c + 1) * TPC)
                sp.dma_start(x[:, tl, :], t["x"][:, tl, :]).then_inc(load_x[c], 16)
                sp.dma_start(ctxT[:, cols], t["ctxT"][:, cols]).then_inc(load_x[c], 16)
            for n in order:
                sp.dma_start(w[n].ap(), t[n]).then_inc(load_w, 16)
            sp.dma_start(ctx_tok[:, :, :], t["ctx"]).then_inc(load_w, 16)
            gates_sp(sp)
            sp.wait_ge(Dl.x_updated, CHUNKS + 1)
            sp.dma_start(out, x[:, :, :]).then_inc(stored, 16)
            sp.wait_ge(stored, 16)

        n_loads = 16 * (len(order) + 1)

        def all_loaded(eng):
            eng.wait_ge(load_w, n_loads)
            for c in range(CHUNKS):
                eng.wait_ge(load_x[c], 32)
            eng.wait_ge(consts_set, 1)

        @block.gpsimd
        def _(pool):
            all_loaded(pool)
            attn_pool(pool)
            ffn0_pool(pool)
            gates_pool(pool)
            mlstm_pool(pool)
            ffn1_pool(pool)

        @block.vector
        def _(dve):
            for n, L in enumerate((A, Bf, C, Dl)):
                dve.memset(minus_half[:, 4 * n:4 * n + 4], -0.5).then_inc(L.x_updated, 1)
            dve.memset(vbd[:, :, :, :, :], 0.0).then_inc(set_step, 1)
            dve.wait_ge(set_step, 1)
            for half in range(2):
                dve.memset(vbd[S * half:S * half + S, :, :, half, DK:DK + 1], 1.0)
            dve.memset(ones_r[:, :], 1.0).then_inc(gates_ready, 1)
            dve.memset(counts[:, :, :], 0.0).then_inc(xnT_kept, 1)
            dve.memset(vext[:, :, :, :, :], 0.0).then_inc(set_step, 1)
            dve.wait_ge(set_step, 2)
            for half in range(2):
                dve.memset(vext[S * half:S * half + S, half, :, :, DH:DH + 1], 1.0)
            dve.memset(biased[:, :, E0:16], LOWEST)
            dve.memset(chosen[:, :, 2:8], LOWEST)
            dve.memset(rw[:, :, E0:E0 + 1], 1.0)
            dve.memset(rw3[:, :, :], 0.0).then_inc(set_step, 1)
            dve.wait_ge(set_step, 3)
            dve.memset(rw3[:, :, E0:E0 + 1], 1.0).then_inc(consts_set, 1)
            all_loaded(dve)
            attn_dve(dve)
            ffn0_dve(dve)
            gates_dve(dve)
            mlstm_dve(dve)
            ffn1_dve(dve)

        @block.scalar
        def _(act):
            all_loaded(act)
            attn_act(act)
            ffn0_act(act)
            gates_act(act)
            mlstm_act(act)
            ffn1_act(act)

        @block.tensor
        def _(pe):
            all_loaded(pe)
            attn_pe(pe)
            ffn0_pe(pe)
            gates_pe(pe)
            mlstm_pe(pe)
            ffn1_pe(pe)


def _layout(inputs):
    bf16 = np.dtype(mybir.dt.np(BF16))
    f = {k: np.asarray(v) for k, v in inputs.items()}
    a = {}
    a["x"] = f["x"].reshape(TILES, P, D).transpose(1, 0, 2)
    a["ctx"] = f["ctx_1024"].reshape(TILES, P, D).transpose(1, 0, 2)
    a["ctxT"] = f["ctx_1024"].reshape(TILES * P, D).T
    a["ident"] = np.eye(P, dtype=np.float32)
    for n in "qkvo":
        a[f"w{n}T"] = f[f"L0_xattn_W_{n}"].T
    for n in "qkv":
        a[f"b{n}"] = f[f"L0_xattn_b_{n}"][:, None]
    a["bo"] = f["L0_xattn_b_o"][None, :]
    a["ones_row"] = np.ones((1, P), np.float32)
    a["headmask"] = (np.arange(P)[:, None] % 32 // DK == np.arange(4)[None, :]).astype(np.float32)
    a["identb"] = np.eye(P).astype(bf16)
    a["gwT0"] = f["L0_ffn_gate_w"].T
    a["gate_b"] = np.broadcast_to(f["L0_ffn_gate_b"], (P, E0))
    for n in "13":
        a[f"w{n}"] = np.concatenate([f[f"L0_ffn_w{n}"].transpose(1, 0, 2).reshape(D, E0 * HID0),
                                     f[f"L0_ffn_sw{n}"]], axis=1)
        flat = np.concatenate([f[f"L0_ffn_b{n}"].reshape(-1), f[f"L0_ffn_sb{n}"],
                               np.zeros(HT * P - HCOLS, np.float32)])
        a[f"b{n}"] = flat.reshape(HT, P).T
    w2 = np.concatenate([f["L0_ffn_w2"].reshape(E0 * HID0, D), f["L0_ffn_sw2"]], axis=0)
    a["w2"] = w2[:(HT - 1) * P].reshape(HT - 1, P, D).transpose(1, 0, 2)
    a["w2last"] = w2[(HT - 1) * P:]
    a["b2"] = np.concatenate([f["L0_ffn_b2"], f["L0_ffn_sb2"][None]], axis=0)
    sel = np.zeros((3 * PART, HCOLS), np.float32)
    for part in range(3):
        for e in range(E0 + 1):
            sel[part * PART + e, e * HID0:(e + 1) * HID0] = 1
    a["sel0"] = sel.astype(bf16)
    def gate_cols(ig, fg):
        g = np.zeros((ig.shape[0], GATE_ROW + NH), np.float32)
        g[:, 0:NH], g[:, GATE_ROW:] = ig, fg
        return g
    for n, name in enumerate("qkv"):
        a[f"gk_{name}"] = gate_cols(f["L1_xattn_igate_kernel"][n * D:(n + 1) * D],
                                    f["L1_xattn_fgate_kernel"][n * D:(n + 1) * D])
    a["gk_bias"] = gate_cols(f["L1_xattn_igate_bias"][None], f["L1_xattn_fgate_bias"][None]).T
    a["out_scale"] = np.broadcast_to(f["L1_xattn_outnorm_scale"], (P, D))
    a["head_ind"] = np.repeat(np.eye(NH, dtype=np.float32), S, axis=1)
    a["seq_sel"] = np.repeat(np.eye(2, dtype=np.float32), S, axis=1)
    key_time, query_time = np.arange(P)[:, None] % S, np.arange(NH * S)[None, :] % S
    a["causal"] = np.where(key_time <= query_time, 0.0, LOWEST).astype(bf16)
    a["gwT1"] = f["L1_ffn_gate_weight"].T
    gu = f["L1_ffn_gate_up_proj"].transpose(2, 0, 1)
    a["wg"], a["wu"] = gu[:, :, :F1], gu[:, :, F1:]
    a["wd"] = f["L1_ffn_down_proj"].transpose(2, 0, 1)
    sel = np.zeros((3 * PART, E1, F1), np.float32)
    for part in range(3):
        for e in range(E1):
            sel[part * PART + e, e] = 1
    a["sel1"] = sel.astype(bf16)
    a["before"] = np.triu(np.ones((P, P)), 1).astype(bf16)
    a["onesb"] = np.ones((P, P)).astype(bf16)
    return {k: np.ascontiguousarray(v) for k, v in a.items()}


def kernel(**inputs):
    import concourse.bacc as bacc
    from concourse.bass_utils import run_bass_kernel_spmd

    nc = bacc.Bacc("TRN2", target_bir_lowering=False, num_devices=1)
    arrays = _layout(inputs)
    aps = {n: nc.dram_tensor(f"in_{n}", a.shape, mybir.dt.from_np(a.dtype), kind="ExternalInput").ap()
           for n, a in arrays.items()}
    out = nc.dram_tensor("out", (P, TILES, D), F32, kind="ExternalOutput").ap()
    build(nc, aps, out)
    r = run_bass_kernel_spmd(nc, [{f"in_{n}": a for n, a in arrays.items()}], core_ids=[0])
    y = r.results[0]["out"]
    return y.transpose(1, 0, 2).reshape(B, S, D)
```

```python
from contextlib import ExitStack

import numpy as np
import concourse.bass as bass
from concourse import mybir

ALU = mybir.AluOpType
ACT = mybir.ActivationFunctionType
AX = mybir.AxisListType
F32 = mybir.dt.float32
BF16 = mybir.dt.bfloat16

P = 128
D = 128
B, S = 32, 64
TILES = B * S // P
TPC = 4
CHUNKS = TILES // TPC
N = TPC * P
SPC = N // S
BANK = 512

HEADS, DK = 16, 8
E0, HID0 = 8, 176
HCOLS = (E0 + 1) * HID0
HT = -(-HCOLS // P)
HPAD = HT * P - HCOLS
NH, DH = 4, 32
E1, F1, TOP1, CAP = 32, 96, 8, 128
LN_EPS = 1e-5
MLSTM_EPS = 1e-6
GATE_ROW = 32
PART = 32
LOWEST = -1e30


def build(nc, t, out):
    with ExitStack() as ctx:
        def sb(name, shape, dt=F32):
            return ctx.enter_context(nc.sbuf_tensor(name, shape, dt))

        def sem(name):
            return ctx.enter_context(nc.semaphore(name))

        ps = ctx.enter_context(nc.psum_tensor("ps", [P, 8, BANK], F32))
        psb = ps[:, :, :].bitcast(BF16)

        x = sb("x_sb", [P, TILES, D])
        ctx_tok = sb("ctx_tok", [P, TILES, D])
        ctxT = sb("ctxT_sb", [P, TILES * P])
        xnT_all = sb("xnT_all", [P, TILES * P])
        loaded = {}
        for name, ap in t.items():
            if name in ("x", "ctx", "ctxT"):
                continue
            loaded[name] = sb(name + "_sb", list(ap.shape), ap.dtype)
        w = loaded
        ident, identb = w["ident"], w["identb"]

        ln_stats = sb("ln_stats", [P, TILES, 6])
        ln_mv = sb("ln_mv", [P, TILES, 2])
        ln_var = sb("ln_var", [P, TILES])
        ln_rstd = sb("ln_rstd", [P, TILES])
        xn = sb("xn", [P, 2, TPC, D])
        carrier = sb("carrier", [P, 2])
        minus_half = sb("minus_half", [P, 16])

        load_ident = sem("load_ident")
        load_x = [sem(f"load_x{i}") for i in range(CHUNKS)]
        consts_set = sem("consts_set")
        set_step = sem("set_step")
        stored = sem("stored")

        class Layer:
            def __init__(self, k):
                self.ln_var_ready, self.ln_rstd_ready = sem(f"ln_var_ready_{k}"), sem(f"ln_rstd_ready_{k}")
                self.xn_ready, self.turned, self.xnT_ready = sem(f"xn_ready_{k}"), sem(f"turned_{k}"), sem(f"xnT_ready_{k}")
                self.x_updated = sem(f"x_updated_{k}")
                self.ln_step, self.dve_step, self.pool_step = (sem(f"ln_step_{k}"), sem(f"dve_step_{k}"),
                                                               sem(f"pool_step_{k}"))

        A, Bf, C, Dl = (Layer(k) for k in ("attn", "ffn0", "mlstm", "ffn1"))

        class Steps:
            def __init__(self, eng, s, base=0):
                self.eng, self.s, self.base, self.n = eng, s, base, 0

            def step(self, ins):
                ins.then_inc(self.s, 1)
                self.n += 1
                self.eng.wait_ge(self.s, self.base + self.n)

            def close(self, per_chunk):
                assert self.n == per_chunk, (self.n, per_chunk)

        def ln_dve(dve, L, arrived=None):
            st = Steps(dve, L.ln_step)
            for i in range(TILES):
                if arrived and i % TPC == 0:
                    dve.wait_ge(arrived[i // TPC], 16)
                last = dve.bn_stats(ln_stats[:, i, :], x[:, i, :])
            st.step(last)
            for i in range(TILES):
                last = dve.bn_aggr(ln_mv[:, i, :], ln_stats[:, i, :])
            st.step(last)
            dve.tensor_scalar(ln_var[:, :], ln_mv[:, :, 1], LN_EPS, None, ALU.add).then_inc(L.ln_var_ready, 1)
            dve.wait_ge(L.ln_rstd_ready, 1)
            for c in range(CHUNKS):
                if c >= 2:
                    dve.wait_ge(L.turned, c - 1)
                for j in range(TPC):
                    i = c * TPC + j
                    last = dve.tensor_scalar(xn[:, c % 2, j, :], x[:, i, :], ln_mv[:, i, 0:1],
                                             ln_rstd[:, i:i + 1], ALU.subtract, ALU.mult)
                last.then_inc(L.xn_ready, 1)

        def ln_pool(pool, L):
            pool.wait_ge(L.ln_var_ready, 1)
            pool.tensor_tensor(ln_rstd[:, :], ln_var[:, :], minus_half[:, :], ALU.pow).then_inc(L.ln_rstd_ready, 1)

        def ln_pe(pe, L, c):
            pe.wait_ge(L.xn_ready, c + 1)
            if c >= 2:
                pe.wait_ge(L.xnT_ready, c - 1)
            for j in range(TPC):
                last = pe.transpose(ps[:, c % 2, j * P:(j + 1) * P], xn[:, c % 2, j, :], ident[:, :])
            last.then_inc(L.turned, 1)

        def ln_act(act, L, c):
            act.wait_ge(L.turned, c + 1)
            act.activation(xnT_all[:, c * N:(c + 1) * N], ps[:, c % 2, :], ACT.Copy).then_inc(L.xnT_ready, 1)

        kT, qT = sb("kT", [P, N]), sb("qT", [P, N])
        kbd = sb("kbd", [P, 4, N])
        ctxdup = sb("ctxdup", [P, SPC, 2, S])
        vbd = sb("vbd", [P, SPC, HEADS // 2, 2, DK + 1])
        smax = sb("smax", [P, HEADS])
        attn_work = sb("attn_work", [P, 4 * HEADS * S])
        prob = attn_work[:, 0:2 * HEADS * S].rearrange("p (a h k) -> p a h k", a=2, h=HEADS)
        probT = attn_work[:, 2 * HEADS * S:].rearrange("p (a h q) -> p a h q", a=2, h=HEADS // 2)
        rden = sb("rden", [P, 2, HEADS])
        o_tok = sb("o_tok", [P, TPC, D])
        oT = sb("oT", [P, N])
        ctx_copied, q_proj, k_proj, v_proj = sem("ctx_copied"), sem("q_proj"), sem("k_proj"), sem("v_proj")
        qT_ready, kT_ready, v_ready, kbd_ready = sem("qT_ready"), sem("kT_ready"), sem("v_ready"), sem("kbd_ready")
        scores_ready, centred, exp_done = sem("scores_ready"), sem("centred"), sem("exp_done")
        prob_turned, probT_ready, v_ready_act = sem("prob_turned"), sem("probT_ready"), sem("v_ready_act")
        pv_done, o_ready, o_turned, oT_ready, y_ready = (sem("pv_done"), sem("o_ready"), sem("o_turned"),
                                                         sem("oT_ready"), sem("y_ready"))
        A_DVE = 3 * TPC + 1
        HALF = HEADS // 2

        def attn_pool(pool):
            ln_pool(pool, A)
            with pool.Fori(0, CHUNKS) as c:
                chunk = ctxT[:, bass.ds(c * N, N)].rearrange("p (b s) -> p b s", s=S)
                for half in range(2):
                    last = pool.tensor_copy(ctxdup[:, :, half, :], chunk)
                last.then_inc(ctx_copied, 1)
                pool.wait_ge(v_proj, c + 1)

        def vbd_block(bank, half):
            rows = slice(S * half, S * half + S)
            src = ps[rows, 2 + bank, :].rearrange("p (n a d) -> p n a d", a=2, d=DK)[:, :, half, :]
            dst = vbd[rows, bank * 4:bank * 4 + 4, :, half, 0:DK].rearrange("p b h d -> p (b h) d")
            return dst, src

        def attn_dve(dve):
            ln_dve(dve, A, load_x)
            loaded_for(dve, "attn")
            with dve.Fori(0, CHUNKS) as c:
                st = Steps(dve, A.dve_step, c * A_DVE)
                dve.wait_ge(kT_ready, c + 1)
                for h in range(4):
                    last = dve.tensor_scalar(kbd[:, h, :], kT[:, :], w["headmask"][:, h:h + 1], None, ALU.mult)
                last.then_inc(kbd_ready, 1)

                def softmax(j, hf):
                    dve.wait_ge(scores_ready, c * 2 * TPC + 2 * j + hf + 1)
                    sc = ps[:, 4 + 2 * hf:6 + 2 * hf, 0:4 * S].rearrange("p i (h k) -> p i h k", h=4)
                    mx = smax[:, HALF * hf:HALF * hf + HALF].rearrange("p (i h) -> p i h", i=2)
                    st.step(dve.tensor_reduce(mx, sc, AX.X, ALU.max))
                    pr = prob[:, j % 2, HALF * hf:HALF * hf + HALF, :].rearrange("p (i h) k -> p i h k", i=2)
                    if j >= 2:
                        dve.wait_ge(prob_turned, c * TPC + j - 1)
                    dve.tensor_tensor(pr, sc, mx.unsqueeze(3).to_broadcast([P, 2, 4, S]),
                                      ALU.subtract).then_inc(centred, 1)

                def normalise(j):
                    dve.wait_ge(pv_done, c * TPC + j + 1)
                    o = ps[:, j % 2, 0:HEADS * (DK + 1)].rearrange("p (h d) -> p h d", d=DK + 1)
                    st.step(dve.reciprocal(rden[:, j % 2, :], o[:, :, DK]))
                    dve.tensor_tensor(o_tok[:, j, :].rearrange("p (h d) -> p h d", d=DK), o[:, :, 0:DK],
                                      rden[:, j % 2, :].unsqueeze(2).to_broadcast([P, HEADS, DK]),
                                      ALU.mult).then_inc(o_ready, 1)

                for j in range(TPC + 1):
                    if j < TPC:
                        softmax(j, 0)
                        softmax(j, 1)
                    if j == 0:
                        dve.wait_ge(v_proj, c + 1)
                        for half in range(2):
                            last = dve.tensor_copy(*vbd_block(1, half))
                        last.then_inc(v_ready, 1)
                    if j >= 1:
                        normalise(j - 1)
                dve.wait_ge(y_ready, c + 1)
                xc = x[:, bass.ds(c * TPC, TPC), :]
                st.step(dve.tensor_tensor(xc, xc, ps[:, 5, :].rearrange("p (j d) -> p j d", d=D), ALU.add))
                st.close(A_DVE)
                dve.tensor_tensor(xc, xc, w["bo"][:, :].unsqueeze(1).to_broadcast([P, TPC, D]),
                                  ALU.add).then_inc(A.x_updated, 1)
            dve.wait_ge(A.x_updated, CHUNKS + 1)

        def attn_act(act):
            for c in range(CHUNKS):
                ln_act(act, A, c)
            loaded_for(act, "attn")
            with act.Fori(0, CHUNKS) as c:
                act.wait_ge(k_proj, c + 1)
                act.activation(kT[:, :], ps[:, 0, :], ACT.Identity, bias=w["bk"][:, :]).then_inc(kT_ready, 1)
                act.wait_ge(q_proj, c + 1)
                act.activation(qT[:, :], ps[:, 1, :], ACT.Identity, bias=w["bq"][:, :]).then_inc(qT_ready, 1)
                act.wait_ge(v_proj, c + 1)
                for half in range(2):
                    last = act.activation(*vbd_block(0, half), ACT.Copy)
                last.then_inc(v_ready_act, 1)

                def exps(j, hf):
                    act.wait_ge(centred, c * 2 * TPC + 2 * j + hf + 1)
                    pr = prob[:, j % 2, HALF * hf:HALF * hf + HALF, :]
                    act.activation(pr, pr, ACT.Exp, scale=float(1 / np.sqrt(np.float32(DK)))).then_inc(exp_done, 1)

                def copy_turned(j):
                    act.wait_ge(prob_turned, c * TPC + j + 1)
                    if j >= 2:
                        act.wait_ge(pv_done, c * TPC + j - 1)
                    act.activation(probT[:, j % 2, :, :].rearrange("p h q -> p (h q)"),
                                   ps[:, 2:4, :].rearrange("p a n -> p (a n)"), ACT.Copy).then_inc(probT_ready, 1)

                exps(0, 0)
                exps(0, 1)
                for j in range(TPC):
                    if j + 1 < TPC:
                        exps(j + 1, 0)
                    copy_turned(j)
                    if j + 1 < TPC:
                        exps(j + 1, 1)
                act.wait_ge(o_turned, c + 1)
                act.activation(oT[:, :], ps[:, 4, :], ACT.Identity, bias=w["bv"][:, :]).then_inc(oT_ready, 1)

        def attn_pe(pe):
            for c in range(CHUNKS):
                ln_pe(pe, A, c)
            loaded_for(pe, "attn")
            pe.wait_ge(A.xnT_ready, CHUNKS)
            with pe.Fori(0, CHUNKS) as c:
                cols = bass.ds(c * N, N)
                pe.matmul(ps[:, 0, :], w["wkT"][:, :], ctxT[:, cols], start=True, stop=True).then_inc(k_proj, 1)
                pe.matmul(ps[:, 1, :], w["wqT"][:, :], xnT_all[:, cols], start=True, stop=True).then_inc(q_proj, 1)

                def values():
                    pe.wait_ge(ctx_copied, c + 1)
                    for b in range(SPC):
                        last = pe.matmul(ps[:, 2 + b // 4, (b % 4) * D:(b % 4 + 1) * D], ctxdup[:, b, :, :],
                                         w["wvT"][:, :], start=True, stop=True)
                    last.then_inc(v_proj, 1)

                def scores(j, hf):
                    if j == 0 and hf == 0:
                        pe.wait_ge(A.x_updated, c + 1)
                        pe.wait_ge(qT_ready, c + 1)
                        pe.wait_ge(kbd_ready, c + 1)
                    if j >= 1:
                        pe.wait_ge(centred, c * 2 * TPC + 2 * j - 1 + hf)
                    for i in (2 * hf, 2 * hf + 1):
                        for b2 in range(2):
                            b = 2 * j + b2
                            last = pe.matmul(ps[S * b2:S * b2 + S, 4 + i, 0:4 * S],
                                             qT[32 * i:32 * i + 32, b * S:b * S + S],
                                             kbd[32 * i:32 * i + 32, :, b * S:b * S + S], start=True, stop=True)
                    last.then_inc(scores_ready, 1)

                def turn(j):
                    pe.wait_ge(exp_done, c * 2 * TPC + 2 * j + 2)
                    if j == 0:
                        pe.wait_ge(v_ready, c + 1)
                        pe.wait_ge(v_ready_act, c + 1)
                    else:
                        pe.wait_ge(probT_ready, c * TPC + j)
                    for hp in range(HEADS // 2):
                        last = pe.transpose(ps[:, 2 + hp // 4, (hp % 4) * P:(hp % 4 + 1) * P],
                                            prob[:, j % 2, 2 * hp:2 * hp + 2, :], ident[:, :])
                    last.then_inc(prob_turned, 1)

                def weighted(j):
                    pe.wait_ge(probT_ready, c * TPC + j + 1)
                    if j >= 2:
                        pe.wait_ge(o_ready, c * TPC + j - 1)
                    W = 2 * (DK + 1)
                    for hp in range(HEADS // 2):
                        for b2 in range(2):
                            last = pe.matmul(ps[S * b2:S * b2 + S, j % 2, hp * W:(hp + 1) * W],
                                             probT[:, j % 2, hp, S * b2:S * b2 + S],
                                             vbd[:, 2 * j + b2, hp, :, :], start=True, stop=True)
                    last.then_inc(pv_done, 1)

                scores(0, 0)
                scores(0, 1)
                values()
                for j in range(TPC):
                    if j + 1 < TPC:
                        scores(j + 1, 0)
                    turn(j)
                    if j + 1 < TPC:
                        scores(j + 1, 1)
                    weighted(j)
                pe.wait_ge(o_ready, c * TPC + TPC)
                for j in range(TPC):
                    last = pe.transpose(ps[:, 4, j * P:(j + 1) * P], o_tok[:, j, :], ident[:, :])
                last.then_inc(o_turned, 1)
                pe.wait_ge(oT_ready, c + 1)
                for j in range(TPC):
                    last = pe.matmul(ps[:, 5, j * D:(j + 1) * D], oT[:, j * P:(j + 1) * P], w["woT"][:, :],
                                     start=True, stop=True)
                last.then_inc(y_ready, 1)

        logit = sb("logit", [P, TILES, E0])
        lmax = sb("lmax", [P, TILES])
        lsum = sb("lsum", [P, TILES])
        gate = sb("gate", [P, TILES, E0])
        biased = sb("biased", [P, TILES, 16])
        top8 = sb("top8", [P, TILES, 8])
        chosen = sb("chosen", [P, TILES, 8])
        rest = sb("rest", [P, TILES, 16])
        rw = sb("rw", [P, TILES, E0 + 1])
        rw3 = sb("rw3", [P, TILES, 3 * PART], BF16)
        rwrem = sb("rwrem", [P, TILES, E0])
        rwT = kbd[0:E0 + 1, :, :].rearrange("p h n -> p (h n)")
        rw3T = sb("rw3T", [3 * PART, TILES * P], BF16)
        up_a = sb("up_a", [P, 2, N])
        zbuf = sb("zbuf", [P, 2, N])
        hact = sb("hact", [P, 2, N])
        hbuf = sb("hbuf", [P, 2, N])
        yT = oT
        names = ("logits", "l_centred", "l_exp", "rw_ready", "rw_turned", "rwT_ready", "rw3T_ready", "a_ps", "c_ps", "w_ps",
                 "a_ready", "z_ready", "s_ready", "h_ready", "yT_ready", "y_turned", "h_used")
        s0 = {n: sem("f0_" + n) for n in names}
        s1 = {n: sem("f1_" + n) for n in names}

        def moe_tail_act(act, s, c, per):
            act.wait_ge(s["h_used"], (c + 1) * per)
            act.activation(yT[:, :], ps[:, 0, :], ACT.Copy).then_inc(s["yT_ready"], 1)

        def moe_tail_pe(pe, s, c):
            pe.wait_ge(s["yT_ready"], c + 1)
            for j in range(TPC):
                last = pe.transpose(ps[:, 1, j * P:(j + 1) * P], yT[:, j * P:(j + 1) * P], ident[:, :])
            last.then_inc(s["y_turned"], 1)

        def moe_tail_dve(dve, s, L, c):
            dve.wait_ge(s["y_turned"], c + 1)
            xc = x[:, bass.ds(c * TPC, TPC), :]
            dve.tensor_tensor(xc, xc, ps[:, 1, :].rearrange("p (j d) -> p j d", d=D),
                              ALU.add).then_inc(L.x_updated, 1)
            dve.wait_ge(L.x_updated, c + 2)

        def ffn0_pool(pool):
            pool.wait_ge(A.x_updated, CHUNKS + 1)
            ln_pool(pool, Bf)

        def softmax_dve(dve, st, s, E, lg, pr):
            dve.wait_ge(s["logits"], 1)
            src = ps[:, 2, 0:TILES * E].rearrange("p (j e) -> p j e", e=E)
            st.step(dve.tensor_reduce(lmax[:, :], src, AX.X, ALU.max))
            dve.tensor_tensor(lg, src, lmax[:, :].unsqueeze(2).to_broadcast([P, TILES, E]),
                              ALU.subtract).then_inc(s["l_centred"], 1)
            dve.wait_ge(s["l_exp"], 1)
            st.step(dve.tensor_reduce(lsum[:, :], lg, AX.X, ALU.add))
            st.step(dve.reciprocal(lsum[:, :], lsum[:, :]))
            st.step(dve.tensor_tensor(pr, lg, lsum[:, :].unsqueeze(2).to_broadcast([P, TILES, E]), ALU.mult))

        def split3(dve, st, src, rem, dst, E, s):
            st.step(dve.tensor_copy(dst[:, :, 0:E], src))
            st.step(dve.tensor_tensor(rem, src, dst[:, :, 0:E], ALU.subtract))
            st.step(dve.tensor_copy(dst[:, :, PART:PART + E], rem))
            st.step(dve.tensor_tensor(rem, rem, dst[:, :, PART:PART + E], ALU.subtract))
            dve.tensor_copy(dst[:, :, 2 * PART:2 * PART + E], rem).then_inc(s["rw_ready"], 1)

        def logits_pe(pe, s, L, E, gw):
            for c in range(CHUNKS):
                ln_pe(pe, L, c)
            for i in range(TILES):
                if i % TPC == 0:
                    pe.wait_ge(L.xnT_ready, i // TPC + 1)
                last = pe.matmul(ps[:, 2, i * E:(i + 1) * E], xnT_all[:, i * P:(i + 1) * P], gw,
                                 start=True, stop=True)
            last.then_inc(s["logits"], 1)

        def turn_rw3(pe, i):
            return pe.transpose(psb[0:3 * PART, 2 + i // 8, (i % 8) * P:(i % 8 + 1) * P], rw3[:, i, :], identb[:, :])

        def rw3T_dve(dve, s):
            dve.wait_ge(s["rw_turned"], 1)
            for half in range(2):
                cols = slice(half * TILES * P // 2, (half + 1) * TILES * P // 2)
                dve.tensor_copy(rw3T[:, cols], psb[0:3 * PART, 2 + half, :]).then_inc(s["rw3T_ready"], 1)

        def ffn0_dve(dve):
            s = s0
            loaded_for(dve, "ffn0")
            ln_dve(dve, Bf)
            st = Steps(dve, Bf.dve_step)
            softmax_dve(dve, st, s, E0, logit[:, :, :], gate[:, :, :])
            st.step(dve.tensor_tensor(biased[:, :, 0:E0], gate[:, :, :],
                                      w["gate_b"][:, :].unsqueeze(1).to_broadcast([P, TILES, E0]), ALU.add))
            for j in range(TILES):
                last = dve.max(top8[:, j, :], biased[:, j, :])
            st.step(last)
            st.step(dve.tensor_copy(chosen[:, :, 0:2], top8[:, :, 0:2]))
            for j in range(TILES):
                last = dve.match_replace(rest[:, j, :], chosen[:, j, :], biased[:, j, :], 2 * LOWEST)
            st.step(last)
            st.step(dve.tensor_tensor(rest[:, :, 0:E0], rest[:, :, 0:E0], biased[:, :, 0:E0], ALU.not_equal))
            st.step(dve.tensor_tensor(rw[:, :, 0:E0], gate[:, :, :], rest[:, :, 0:E0], ALU.mult))
            split3(dve, st, rw[:, :, 0:E0], rwrem[:, :, :], rw3, E0, s)
            rw3T_dve(dve, s)
            with dve.Fori(0, CHUNKS) as c:
                def gated(k):
                    g = c * HT + k
                    dve.wait_ge(s["a_ready"], g + 1)
                    dve.wait_ge(s["c_ps"], g + 1)
                    if k >= 2:
                        dve.wait_ge(s["s_ready"], g - 1)
                    dve.scalar_tensor_tensor(zbuf[:, k % 2, :], ps[:, 4 + k % 2, :], w["b3"][:, k:k + 1],
                                             up_a[:, k % 2, :], ALU.add, ALU.mult).then_inc(s["z_ready"], 1)

                def weigh(k):
                    g = c * HT + k
                    dve.wait_ge(s["s_ready"], g + 1)
                    dve.wait_ge(s["w_ps"], g + 1)
                    if k >= 2:
                        dve.wait_ge(s["h_used"], g - 1)
                    dve.tensor_tensor(hbuf[:, k % 2, :], hact[:, k % 2, :], ps[:, 6 + k % 2, :],
                                      ALU.mult).then_inc(s["h_ready"], 1)

                for k in range(HT + 1):
                    if k < HT:
                        gated(k)
                    if k >= 1:
                        weigh(k - 1)
                moe_tail_dve(dve, s, Bf, c)

        def ffn0_act(act):
            s = s0
            for c in range(CHUNKS):
                ln_act(act, Bf, c)
            act.wait_ge(s["l_centred"], 1)
            act.activation(logit[:, :, :], logit[:, :, :], ACT.Exp).then_inc(s["l_exp"], 1)
            loaded_for(act, "ffn0")
            act.wait_ge(s["rw_turned"], 1)
            act.activation(rwT[:, :], ps[0:E0 + 1, 4:8, :].rearrange("p a n -> p (a n)"),
                           ACT.Copy).then_inc(s["rwT_ready"], 1)
            with act.Fori(0, CHUNKS) as c:

                def up(k):
                    g = c * HT + k
                    act.wait_ge(s["a_ps"], g + 1)
                    if k >= 2:
                        act.wait_ge(s["z_ready"], g - 1)
                    act.activation(up_a[:, k % 2, :], ps[:, 2 + k % 2, :], ACT.Identity,
                                   bias=w["b1"][:, k:k + 1]).then_inc(s["a_ready"], 1)

                def silu(k):
                    g = c * HT + k
                    act.wait_ge(s["z_ready"], g + 1)
                    if k >= 2:
                        act.wait_ge(s["h_ready"], g - 1)
                    act.activation(hact[:, k % 2, :], zbuf[:, k % 2, :],
                                   ACT.Silu).then_inc(s["s_ready"], 1)

                for k in range(HT + 1):
                    if k < HT:
                        up(k)
                    if k >= 1:
                        silu(k - 1)
                moe_tail_act(act, s, c, HT)

        def ffn0_pe(pe):
            s = s0
            loaded_for(pe, "ffn0")
            pe.wait_ge(A.x_updated, CHUNKS + 1)
            logits_pe(pe, s, Bf, E0, w["gwT0"][:, :])
            pe.wait_ge(s["rw_ready"], 1)
            for i in range(TILES):
                pe.transpose(ps[0:E0 + 1, 4 + i // TPC, (i % TPC) * P:(i % TPC + 1) * P], rw[:, i, :], ident[:, :])
                last = turn_rw3(pe, i)
            last.then_inc(s["rw_turned"], 1)
            pe.wait_ge(s["rw3T_ready"], 2)
            pe.wait_ge(s["rwT_ready"], 1)
            with pe.Fori(0, CHUNKS) as c:
                xnT = xnT_all[:, bass.ds(c * N, N)]
                pe.matmul(ps[:, 0, :], w["b2"][:, :], rwT[:, bass.ds(c * N, N)], start=True, stop=False,
                          skip_group_check=True)

                def products(k):
                    g = c * HT + k
                    cols = slice(k * P, (k + 1) * P)
                    if k >= 2:
                        pe.wait_ge(s["a_ready"], g - 1)
                    pe.matmul(ps[:, 2 + k % 2, :], w["w1"][:, cols], xnT, start=True,
                              stop=True).then_inc(s["a_ps"], 1)
                    if k >= 2:
                        pe.wait_ge(s["z_ready"], g - 1)
                    pe.matmul(ps[:, 4 + k % 2, :], w["w3"][:, cols], xnT, start=True,
                              stop=True).then_inc(s["c_ps"], 1)
                    if k >= 2:
                        pe.wait_ge(s["h_ready"], g - 1)
                    pe.matmul(ps[:, 6 + k % 2, :], w["sel0"][:, cols], rw3T[:, bass.ds(c * N, N)], start=True,
                              stop=True).then_inc(s["w_ps"], 1)

                def down(k):
                    g = c * HT + k
                    pe.wait_ge(s["h_ready"], g + 1)
                    pe.matmul(ps[:, 0, :], w["w2"][:, k, :], hbuf[:, k % 2, :], start=False,
                              stop=(k == HT - 1), skip_group_check=True).then_inc(s["h_used"], 1)

                for k in range(HT + 2):
                    if k < HT:
                        products(k)
                    if k >= 2:
                        down(k - 2)
                moe_tail_pe(pe, s, c)

        GR = GATE_ROW + NH
        gk_ctx = sb("gk_ctx", [P, GR])
        gates = sb("gates", [GR, TILES * P])
        ig_r, fg_r = sb("ig_r", [P, S]), sb("fg_r", [P, S])
        t0, t1, t2 = sb("row_t0", [P, S]), sb("row_t1", [P, S]), sb("row_t2", [P, S])
        cum, g_r, m_r, neg_m, en_r = (sb("cum", [P, S]), sb("g_r", [P, S]), sb("m_r", [P, S]), sb("neg_m", [P, S]),
                                      sb("en_r", [P, S]))
        ones_r = sb("ones_r", [P, S])
        g4 = kbd[0:NH, :, :].rearrange("p h n -> p (h n)")
        m2 = attn_work[0:2, :].rearrange("p (a h s) -> p a h s", a=TILES, h=NH)
        en_tok = sb("en_tok", [P, TILES, NH])
        gates_ps, gates_ready, rows_in = sem("gates_ps"), sem("gates_ready"), sem("rows_in")
        row_dve, row_act, row_ready, rows_out = sem("row_dve"), sem("row_act"), sem("row_ready"), sem("rows_out")
        en_turned, en_copied, gk_summed = sem("en_turned"), sem("en_copied"), sem("gk_summed")

        def gates_pool(pool):
            pool.wait_ge(Bf.x_updated, CHUNKS + 1)
            ln_pool(pool, C)

        def gates_pe(pe):
            pe.wait_ge(Bf.x_updated, CHUNKS + 1)
            pe.wait_ge(gk_summed, 1)
            for c in range(CHUNKS):
                ln_pe(pe, C, c)
            for c in range(CHUNKS):
                cols = slice(c * N, (c + 1) * N)
                pe.wait_ge(C.xnT_ready, c + 1)
                pe.matmul(ps[0:GR, 2 + c, :], w["gk_q"][:, :], xnT_all[:, cols], start=True, stop=False)
                pe.matmul(ps[0:GR, 2 + c, :], gk_ctx[:, :], ctxT[:, cols], start=False, stop=True).then_inc(gates_ps, 1)
            pe.wait_ge(row_ready, 1)
            pe.transpose(ps[0:S, 0, 0:P], en_r[:, :], ident[:, :]).then_inc(en_turned, 1)

        def gates_act(act):
            for c in range(CHUNKS):
                ln_act(act, C, c)
            for c in range(CHUNKS):
                act.wait_ge(gates_ps, c + 1)
                act.activation(gates[:, c * N:(c + 1) * N], ps[0:GR, 2 + c, :], ACT.Identity,
                               bias=w["gk_bias"][:, :]).then_inc(gates_ready, 1)
            act.wait_ge(rows_in, 16 * 2 * NH)
            act.activation(t0[:, :], fg_r[:, :], ACT.Abs).then_inc(row_act, 1)
            act.wait_ge(row_act, 1)
            act.activation(t0[:, :], t0[:, :], ACT.Exp, scale=-1.0).then_inc(row_act, 1)
            act.wait_ge(row_act, 2)
            act.activation(t0[:, :], t0[:, :], ACT.Ln, bias=1.0).then_inc(row_act, 1)
            act.wait_ge(row_dve, 6)
            act.activation(en_r[:, :], t2[:, :], ACT.Exp, scale=-1.0).then_inc(row_ready, 1)

        def gates_dve(dve):
            loaded_for(dve, "mlstm")
            dve.tensor_tensor(gk_ctx[:, :], w["gk_k"][:, :], w["gk_v"][:, :], ALU.add).then_inc(gk_summed, 1)
            ln_dve(dve, C)
            dve.wait_ge(rows_in, 16 * 2 * NH)
            dve.tensor_scalar(t1[:, :], fg_r[:, :], 0.0, None, ALU.min).then_inc(row_dve, 1)
            dve.wait_ge(row_dve, 1)
            dve.wait_ge(row_act, 3)
            dve.tensor_tensor(t1[:, :], t1[:, :], t0[:, :], ALU.subtract).then_inc(row_dve, 1)
            dve.wait_ge(row_dve, 2)
            dve.tensor_tensor_scan(cum[:, :], ones_r[:, :], t1[:, :], 0.0, ALU.mult, ALU.add).then_inc(row_dve, 1)
            dve.wait_ge(row_dve, 3)
            dve.tensor_tensor(g_r[:, :], ig_r[:, :], cum[:, :], ALU.subtract).then_inc(row_dve, 1)
            dve.wait_ge(row_dve, 4)
            dve.tensor_tensor_scan(m_r[:, :], g_r[:, :], g_r[:, :], -3e38, ALU.max, ALU.max).then_inc(row_dve, 1)
            dve.wait_ge(row_dve, 5)
            dve.tensor_tensor(t2[:, :], cum[:, :], m_r[:, :], ALU.add).then_inc(row_dve, 1)
            dve.tensor_scalar(neg_m[:, :], m_r[:, :], -1.0, None, ALU.mult).then_inc(row_dve, 1)
            dve.wait_ge(en_turned, 1)
            src = ps[0:S, 0, 0:P].rearrange("s (h p b) -> s p h b", h=NH, b=2)
            for b2 in range(2):
                last = dve.tensor_copy(en_tok[S * b2:S * b2 + S, :, :], src[:, :, :, b2])
            last.then_inc(en_copied, 1)

        def gates_sp(sp):
            sp.wait_ge(gates_ready, CHUNKS)
            for h in range(NH):
                for row, dst in ((h, ig_r), (GATE_ROW + h, fg_r)):
                    sp.dma_start(dst[B * h:B * h + B, :],
                                 gates[row:row + 1, :].rearrange("o (b s) -> o b s", s=S)).then_inc(rows_in, 16)
            sp.wait_ge(row_dve, 7)
            for h in range(NH):
                sp.dma_start(g4[h:h + 1, :].rearrange("o (b s) -> o b s", s=S),
                             g_r[B * h:B * h + B, :]).then_inc(rows_out, 16)
                for b2 in range(2):
                    sp.dma_start(m2[b2:b2 + 1, :, h, :], neg_m[B * h + b2:B * h + B:2, :]).then_inc(rows_out, 16)

        xnTc, ctxTc = kT, qT
        g4c = sb("g4c", [NH, N])
        vext = sb("vext", [P, 2, TPC, NH, DH + 1])
        dmat = up_a[:, :, :].rearrange("p a (b h s) -> p (a b) h s", b=2, h=NH)
        cmat = zbuf[:, :, :].rearrange("p a (b h s) -> p (a b) h s", b=2, h=NH)
        n_a, n_b = sb("n_a", [P, TPC, NH]), sb("n_b", [P, TPC, NH])
        ho = hact[:, 0, :].rearrange("p (j h d) -> p j h d", j=TPC, h=NH)
        hsq = hbuf[:, 0, :].rearrange("p (j h d) -> p j h d", j=TPC, h=NH)
        hm, hv = sb("hm", [P, TPC * NH]), sb("hv", [P, TPC * NH])
        g4c_ready, qk_in, vext_ready = sem("g4c_ready"), sem("qk_in"), sem("vext_ready")
        qk_ps, logd_ps, h_ps = sem("qk_ps"), sem("logd_ps"), sem("h_ps")
        hc_ready, hsq_ready, hvar_ready, hrstd_ready = (sem("hc_ready"), sem("hsq_ready"), sem("hvar_ready"),
                                                        sem("hrstd_ready"))
        cmat_ready, dmat_taken, h_read = sem("cmat_ready"), sem("dmat_taken"), sem("h_read")
        C_DVE = 10

        def mlstm_pool(pool):
            def values(c, first=False):
                if not first:
                    pool.wait_ge(h_ps, c)
                for b2 in range(2):
                    rows = slice(S * b2, S * b2 + S)
                    pool.tensor_copy(
                        vext[rows, b2, :, :, 0:DH],
                        ctx_tok[rows, bass.ds(c * TPC, TPC), :].rearrange("p j (h d) -> p j h d", h=NH)
                    ).then_inc(vext_ready, 1)

            def root(c, copied):
                pool.wait_ge(vext_ready, copied * 2)
                pool.wait_ge(hvar_ready, c + 1)
                pool.tensor_tensor(hv[:, :], hv[:, :], minus_half[:, :], ALU.pow).then_inc(hrstd_ready, 1)
                pool.wait_ge(hrstd_ready, c + 1)

            pool.wait_ge(C.ln_rstd_ready, 1)
            values(0, first=True)
            with pool.Fori(0, CHUNKS - 1) as c:
                values(c + 1)
                root(c, c + 2)
            root(CHUNKS - 1, CHUNKS)

        def mlstm_act(act):
            def prepare(c, first=False):
                if not first:
                    act.wait_ge(logd_ps, c)
                act.activation(g4c[:, :], g4[:, bass.ds(c * N, N)], ACT.Copy).then_inc(g4c_ready, 1)
                if not first:
                    act.wait_ge(qk_ps, c)
                act.activation(xnTc[:, :], xnT_all[:, bass.ds(c * N, N)], ACT.Copy)
                act.activation(ctxTc[:, :], ctxT[:, bass.ds(c * N, N)], ACT.Copy).then_inc(qk_in, 1)
                act.wait_ge(logd_ps, c + 1)
                act.wait_ge(cmat_ready, c + 1)
                act.activation(dmat[:, :, :, :].rearrange("p j h s -> p (j h s)"),
                               ps[:, 4:6, :].rearrange("p a n -> p (a n)"), ACT.Exp).then_inc(dmat_taken, 1)

            def squares(c):
                act.wait_ge(hc_ready, c + 1)
                act.activation(hsq[:, :, :, :], ho[:, :, :, :], ACT.Square).then_inc(hsq_ready, 1)

            act.wait_ge(rows_out, 16 * 3 * NH)
            prepare(0, first=True)
            with act.Fori(0, CHUNKS - 1) as c:
                prepare(c + 1)
                squares(c)
            squares(CHUNKS - 1)

        def mlstm_pe(pe):
            def log_d(c):
                pe.wait_ge(g4c_ready, c + 1)
                pe.wait_ge(dmat_taken, c + 1)
                for j in range(TPC):
                    o = ps[:, 4 + j // 2, (j % 2) * NH * S:(j % 2 + 1) * NH * S]
                    pe.matmul(o, g4c[:, j * P:(j + 1) * P], w["head_ind"][:, :], start=True, stop=False)
                    pe.matmul(o, w["seq_sel"][:, :],
                              m2[:, bass.ds(c * TPC + j, 1), :, :].rearrange("b a h s -> b (a h s)"),
                              start=False, stop=False)
                    last = pe.matmul(o, identb[:, :], w["causal"][:, :], start=False, stop=True)
                last.then_inc(logd_ps, 1)

            def q_dot_k(c):
                pe.wait_ge(qk_in, c + 1)
                pe.wait_ge(cmat_ready, c + 1)
                for j in range(TPC):
                    for h in range(NH):
                        for b2 in range(2):
                            rows, cols = slice(DH * h, DH * h + DH), slice((2 * j + b2) * S, (2 * j + b2 + 1) * S)
                            last = pe.matmul(ps[S * b2:S * b2 + S, h, j * S:(j + 1) * S], ctxTc[rows, cols],
                                             xnTc[rows, cols], start=True, stop=True)
                last.then_inc(qk_ps, 1)

            def outputs(c):
                pe.wait_ge(vext_ready, c * 2 + 2)
                pe.wait_ge(cmat_ready, c + 2)
                pe.wait_ge(h_read, c + 1)
                for j in range(TPC):
                    for h in range(NH):
                        for b2 in range(2):
                            col = (j % 2) * NH * (DH + 1) + h * (DH + 1)
                            last = pe.matmul(ps[S * b2:S * b2 + S, 6 + j // 2, col:col + DH + 1],
                                             cmat[:, j, h, :], vext[:, b2, j, h, :], start=True, stop=True)
                last.then_inc(h_ps, 1)

            pe.wait_ge(en_copied, 1)
            log_d(0)
            q_dot_k(0)
            with pe.Fori(0, CHUNKS - 1) as c:
                log_d(c + 1)
                outputs(c)
                q_dot_k(c + 1)
            outputs(CHUNKS - 1)

        def mlstm_dve(dve):
            W = DH + 1
            hn = ho[:, :, :, :].rearrange("p j h d -> p (j h) d")
            hd = ho[:, :, :, :].rearrange("p j h d -> p j (h d)")

            def combine(c):
                dve.wait_ge(dmat_taken, c + 2)
                dve.wait_ge(qk_ps, c + 1)
                for j in range(TPC):
                    last = dve.scalar_tensor_tensor(cmat[:, j, :, :], ps[:, 0:NH, j * S:(j + 1) * S],
                                                    float(1 / np.sqrt(np.float32(DH))), dmat[:, j, :, :],
                                                    ALU.mult, ALU.mult)
                last.then_inc(cmat_ready, 1)

            def divide_and_centre(c, st):
                dve.wait_ge(h_ps, c + 1)
                o = ps[:, 6:8, 0:2 * NH * W].rearrange("p a (n d) -> p a n d", d=W)
                two = lambda a: a.rearrange("p (a j) h -> p a (j h)", a=2)
                na = two(n_a[:, :, :])
                st.step(dve.tensor_copy(na, o[:, :, :, DH]))
                st.step(dve.scalar_tensor_tensor(n_b[:, :, :], n_a[:, :, :], -1.0, n_a[:, :, :], ALU.mult, ALU.max))
                st.step(dve.tensor_tensor(n_a[:, :, :], n_b[:, :, :], en_tok[:, bass.ds(c * TPC, TPC), :], ALU.max))
                st.step(dve.tensor_scalar(n_b[:, :, :], n_a[:, :, :], MLSTM_EPS, None, ALU.add))
                st.step(dve.reciprocal(n_a[:, :, :], n_b[:, :, :]))
                dve.tensor_tensor(ho[:, :, :, :].rearrange("p (a j) h d -> p a (j h) d", a=2), o[:, :, :, 0:DH],
                                  na.unsqueeze(3).to_broadcast([P, 2, 2 * NH, DH]), ALU.mult).then_inc(h_read, 1)
                dve.wait_ge(h_read, c + 2)
                st.step(dve.tensor_reduce(hm[:, :], hn, AX.X, ALU.add))
                st.step(dve.tensor_scalar(hm[:, :], hm[:, :], -1.0 / DH, None, ALU.mult))
                dve.tensor_tensor(hn, hn, hm[:, :].unsqueeze(2).to_broadcast([P, TPC * NH, DH]),
                                  ALU.add).then_inc(hc_ready, 1)

            def scale_and_add(c, st):
                dve.wait_ge(hsq_ready, c + 1)
                st.step(dve.tensor_reduce(hv[:, :], hsq[:, :, :, :].rearrange("p j h d -> p (j h) d"), AX.X, ALU.add))
                dve.tensor_scalar(hv[:, :], hv[:, :], 1.0 / DH, LN_EPS, ALU.mult, ALU.add).then_inc(hvar_ready, 1)
                dve.wait_ge(hrstd_ready, c + 1)
                st.step(dve.tensor_tensor(hn, hn, hv[:, :].unsqueeze(2).to_broadcast([P, TPC * NH, DH]), ALU.mult))
                st.step(dve.tensor_tensor(hd, hd, w["out_scale"][:, :].unsqueeze(1).to_broadcast([P, TPC, D]),
                                          ALU.mult))
                xc = x[:, bass.ds(c * TPC, TPC), :]
                dve.tensor_tensor(xc, xc, hd, ALU.add).then_inc(C.x_updated, 1)
                dve.wait_ge(C.x_updated, c + 2)
                st.close(C_DVE)

            dve.wait_ge(en_copied, 1)
            combine(0)
            with dve.Fori(0, CHUNKS - 1) as c:
                st = Steps(dve, C.dve_step, c * C_DVE)
                divide_and_centre(c, st)
                combine(c + 1)
                scale_and_add(c, st)
            st = Steps(dve, C.dve_step, (CHUNKS - 1) * C_DVE)
            divide_and_centre(CHUNKS - 1, st)
            scale_and_add(CHUNKS - 1, st)

        logit1, gate1, rest1, gsel = (attn_work[:, n * TILES * E1:(n + 1) * TILES * E1]
                                      .rearrange("p (i e) -> p i e", e=E1) for n in range(4))
        mask1 = sb("mask1", [P, TILES, E1], BF16)
        rem1 = logit1
        pos = rest1
        seg = sb("seg", [P, E1, TILES])
        counts = attn_work[:, 4 * TILES * E1:5 * TILES * E1].rearrange("p (e i) -> p e i", e=E1)
        least = sb("least", [P, CHUNKS - 1])
        open_chunks, n_chunks = sb("open_chunks", [P, 1]), sb("n_chunks", [P, 1], mybir.dt.int32)
        mask_ready, ranks_ps, n_ready, finished = sem("mask_ready"), sem("ranks_ps"), sem("n_ready"), sem("finished")

        def chunks_to_do(eng):
            eng.wait_ge(n_ready, 1)
            return eng.value_load(n_chunks[0:1, 0:1], min_val=1, max_val=CHUNKS)

        def ffn1_pool(pool):
            pool.wait_ge(C.x_updated, CHUNKS + 1)
            ln_pool(pool, Dl)

        def ffn1_dve(dve):
            s = s1
            ln_dve(dve, Dl)
            st = Steps(dve, Dl.dve_step)
            softmax_dve(dve, st, s, E1, logit1[:, :, :], gate1[:, :, :])
            for j in range(TILES):
                last = dve.max(top8[:, j, :], gate1[:, j, :])
            st.step(last)
            for j in range(TILES):
                last = dve.match_replace(rest1[:, j, :], top8[:, j, :], gate1[:, j, :], -1.0)
            st.step(last)
            dve.tensor_tensor(mask1[:, :, :], rest1[:, :, :], gate1[:, :, :],
                              ALU.not_equal).then_inc(mask_ready, 1)
            dve.wait_ge(mask_ready, 1)
            st.step(dve.tensor_tensor(gsel[:, :, :], gate1[:, :, :], mask1[:, :, :], ALU.mult))
            st.step(dve.tensor_reduce(lsum[:, :], gsel[:, :, :], AX.X, ALU.add))
            st.step(dve.reciprocal(lmax[:, :], lsum[:, :]))
            st.step(dve.tensor_tensor(gsel[:, :, :], gsel[:, :, :],
                                      lmax[:, :].unsqueeze(2).to_broadcast([P, TILES, E1]), ALU.mult))
            dve.wait_ge(ranks_ps, 1)
            st.step(dve.tensor_tensor_scan(counts[:, :, :].rearrange("p e i -> p (e i)"),
                                           seg[:, :, :].rearrange("p e i -> p (e i)"), ps[:, 4, :], 0.0,
                                           ALU.mult, ALU.add))
            st.step(dve.tensor_reduce(least[:, :], counts[:, :, TPC - 1:TILES - 1:TPC].rearrange("p e c -> p c e"),
                                      AX.X, ALU.min))
            st.step(dve.tensor_scalar(least[:, :], least[:, :], float(CAP), None, ALU.is_lt))
            st.step(dve.tensor_reduce(open_chunks[:, :], least[:, :], AX.X, ALU.add))
            dve.tensor_scalar(n_chunks[:, :], open_chunks[:, :], 1.0, None, ALU.add).then_inc(n_ready, 1)
            st.step(dve.tensor_tensor(pos[:, :, :], ps[:, 3, :].rearrange("p (i e) -> p i e", e=E1),
                                      counts[:, :, :].rearrange("p e i -> p i e"), ALU.add))
            st.step(dve.scalar_tensor_tensor(gsel[:, :, :], pos[:, :, :], float(CAP), gsel[:, :, :],
                                             ALU.is_lt, ALU.mult))
            split3(dve, st, gsel[:, :, :], rem1[:, :, :], rw3, E1, s)
            rw3T_dve(dve, s)
            with dve.Fori(0, chunks_to_do(dve)) as c:
                def gated(k):
                    g = c * E1 + k
                    dve.wait_ge(s["s_ready"], g + 1)
                    dve.wait_ge(s["c_ps"], g + 1)
                    if k >= 2:
                        dve.wait_ge(s["h_ready"], g - 1)
                    dve.tensor_tensor(zbuf[0:F1, k % 2, :], hact[0:F1, k % 2, :], ps[0:F1, 4 + k % 2, :],
                                      ALU.mult).then_inc(s["z_ready"], 1)

                def weigh(k):
                    g = c * E1 + k
                    dve.wait_ge(s["z_ready"], g + 1)
                    dve.wait_ge(s["w_ps"], g + 1)
                    if k >= 2:
                        dve.wait_ge(s["h_used"], g - 1)
                    dve.tensor_tensor(hbuf[0:F1, k % 2, :], zbuf[0:F1, k % 2, :], ps[0:F1, 6 + k % 2, :],
                                      ALU.mult).then_inc(s["h_ready"], 1)

                for k in range(E1 + 1):
                    if k < E1:
                        gated(k)
                    if k >= 1:
                        weigh(k - 1)
                moe_tail_dve(dve, s, Dl, c)
            dve.memset(carrier[:, :], 0.0).then_inc(finished, 1)

        def ffn1_act(act):
            s = s1
            for c in range(CHUNKS):
                ln_act(act, Dl, c)
            act.wait_ge(s["l_centred"], 1)
            act.activation(logit1[:, :, :], logit1[:, :, :], ACT.Exp).then_inc(s["l_exp"], 1)
            with act.Fori(0, chunks_to_do(act)) as c:
                for k in range(E1):
                    g = c * E1 + k
                    act.wait_ge(s["a_ps"], g + 1)
                    if k >= 2:
                        act.wait_ge(s["z_ready"], g - 1)
                    act.activation(hact[0:F1, k % 2, :], ps[0:F1, 2 + k % 2, :],
                                   ACT.Silu).then_inc(s["s_ready"], 1)
                moe_tail_act(act, s, c, E1)

        def ffn1_pe(pe):
            s = s1
            loaded_for(pe, "ffn1")
            pe.wait_ge(C.x_updated, CHUNKS + 1)
            logits_pe(pe, s, Dl, E1, w["gwT1"][:, :])
            pe.wait_ge(mask_ready, 1)
            pe.matmul(ps[:, 3, :], w["minus_from"][:, :], mask1[:, :, :].rearrange("p i e -> p (i e)"),
                      start=True, stop=True)
            pe.matmul(ps[:, 4, :], w["onesb"][:, :], mask1[:, :, :].rearrange("p i e -> p e i"), start=True,
                      stop=True).then_inc(ranks_ps, 1)
            pe.wait_ge(s["rw_ready"], 1)
            for i in range(TILES):
                last = turn_rw3(pe, i)
            last.then_inc(s["rw_turned"], 1)
            pe.wait_ge(s["rw3T_ready"], 2)
            with pe.Fori(0, chunks_to_do(pe)) as c:
                xnT = xnT_all[:, bass.ds(c * N, N)]

                def products(k):
                    g = c * E1 + k
                    if k >= 2:
                        pe.wait_ge(s["s_ready"], g - 1)
                    pe.matmul(ps[0:F1, 2 + k % 2, :], w["wg"][:, k, :], xnT, start=True,
                              stop=True).then_inc(s["a_ps"], 1)
                    if k >= 2:
                        pe.wait_ge(s["z_ready"], g - 1)
                    pe.matmul(ps[0:F1, 4 + k % 2, :], w["wu"][:, k, :], xnT, start=True,
                              stop=True).then_inc(s["c_ps"], 1)
                    if k >= 2:
                        pe.wait_ge(s["h_ready"], g - 1)
                    pe.matmul(ps[0:F1, 6 + k % 2, :], w["sel1"][:, k, :], rw3T[:, bass.ds(c * N, N)], start=True,
                              stop=True).then_inc(s["w_ps"], 1)

                def down(k):
                    pe.wait_ge(s["h_ready"], c * E1 + k + 1)
                    pe.matmul(ps[:, 0, :], w["wd"][:, k, :], hbuf[0:F1, k % 2, :], start=(k == 0),
                              stop=(k == E1 - 1), skip_group_check=True).then_inc(s["h_used"], 1)

                for k in range(E1 + 2):
                    if k < E1:
                        products(k)
                    if k >= 2:
                        down(k - 2)
                moe_tail_pe(pe, s, c)

        groups = {
            "attn": ("wkT", "bk", "headmask", "wqT", "bq", "wvT", "bv", "woT", "bo"),
            "ffn0": ("gwT0", "gate_b", "identb", "w1", "b1", "w3", "b3", "sel0", "w2", "b2"),
            "mlstm": ("gk_q", "gk_k", "gk_v", "gk_bias", "head_ind", "seq_sel", "causal", "out_scale"),
            "ffn1": ("gwT1", "minus_from", "onesb", "wg", "wu", "sel1", "wd"),
        }
        assert sorted(sum(groups.values(), ("ident",))) == sorted(w)
        loads = {g: sem("load_" + g) for g in groups}

        def loaded_for(eng, g):
            eng.wait_ge(loads[g], 16 * len(groups[g]) + (64 if g == "attn" else 16 if g == "mlstm" else 0))
            eng.wait_ge(consts_set, 1)

        block = ctx.enter_context(nc.Block())

        @block.sync
        def _(sp):
            for c in range(CHUNKS):
                tl = slice(c * TPC, (c + 1) * TPC)
                sp.dma_start(x[:, tl, :], t["x"][:, tl, :]).then_inc(load_x[c], 16)
            for g in ("ffn0", "mlstm", "ffn1"):
                if g == "mlstm":
                    sp.dma_start(ctx_tok[:, :, :], t["ctx"]).then_inc(loads[g], 16)
                for n in groups[g]:
                    sp.dma_start(w[n].ap(), t[n]).then_inc(loads[g], 16)
            gates_sp(sp)
            sp.wait_ge(finished, 1)
            sp.dma_start(out, x[:, :, :]).then_inc(stored, 16)
            sp.wait_ge(stored, 16)

        @block.gpsimd
        def _(pool):
            pool.wait_ge(consts_set, 1)
            loaded_for(pool, "attn")
            attn_pool(pool)
            ffn0_pool(pool)
            gates_pool(pool)
            mlstm_pool(pool)
            ffn1_pool(pool)

        @block.vector
        def _(dve):
            for n, L in enumerate((A, Bf, C, Dl)):
                dve.memset(minus_half[:, 4 * n:4 * n + 4], -0.5).then_inc(L.x_updated, 1)
            dve.memset(ones_r[:, :], 1.0).then_inc(cmat_ready, 1)
            dve.memset(seg[:, :, :], 1.0).then_inc(dmat_taken, 1)
            dve.memset(carrier[:, :], 0.0).then_inc(h_read, 1)
            dve.memset(vbd[:, :, :, :, :], 0.0)
            dve.memset(vext[:, :, :, :, :], 0.0)
            dve.memset(biased[:, :, E0:16], LOWEST)
            dve.memset(chosen[:, :, 2:8], LOWEST)
            dve.memset(rw[:, :, E0:E0 + 1], 1.0)
            dve.memset(rw3[:, :, :], 0.0).then_inc(set_step, 1)
            dve.wait_ge(set_step, 1)
            for half in range(2):
                rows = slice(S * half, S * half + S)
                dve.memset(vbd[rows, :, :, half, DK:DK + 1], 1.0)
                dve.memset(vext[rows, half, :, :, DH:DH + 1], 1.0)
            dve.memset(seg[:, :, 0:1], 0.0)
            dve.memset(rw3[:, :, E0:E0 + 1], 1.0).then_inc(consts_set, 1)
            attn_dve(dve)
            ffn0_dve(dve)
            gates_dve(dve)
            mlstm_dve(dve)
            ffn1_dve(dve)

        @block.scalar
        def _(act):
            act.dma_start(ident.ap(), t["ident"]).then_inc(load_ident, 16)
            for c in range(CHUNKS):
                cols = slice(c * N, (c + 1) * N)
                act.dma_start(ctxT[:, cols], t["ctxT"][:, cols]).then_inc(loads["attn"], 16)
            for n in groups["attn"]:
                act.dma_start(w[n].ap(), t[n]).then_inc(loads["attn"], 16)
            attn_act(act)
            ffn0_act(act)
            gates_act(act)
            mlstm_act(act)
            ffn1_act(act)

        @block.tensor
        def _(pe):
            pe.wait_ge(load_ident, 16)
            attn_pe(pe)
            ffn0_pe(pe)
            gates_pe(pe)
            mlstm_pe(pe)
            ffn1_pe(pe)


def _layout(inputs):
    bf16 = np.dtype(mybir.dt.np(BF16))
    f = {k: np.asarray(v) for k, v in inputs.items()}
    a = {}
    a["x"] = f["x"].reshape(TILES, P, D).transpose(1, 0, 2)
    a["ctx"] = f["ctx_1024"].reshape(TILES, P, D).transpose(1, 0, 2)
    a["ctxT"] = f["ctx_1024"].reshape(TILES * P, D).T
    a["ident"] = np.eye(P, dtype=np.float32)
    for n in "qkvo":
        a[f"w{n}T"] = f[f"L0_xattn_W_{n}"].T
    for n in "qkv":
        a[f"b{n}"] = f[f"L0_xattn_b_{n}"][:, None]
    a["bo"] = np.broadcast_to(f["L0_xattn_b_o"], (P, D))
    a["headmask"] = (np.arange(P)[:, None] % 32 // DK == np.arange(4)[None, :]).astype(np.float32)
    a["identb"] = np.eye(P).astype(bf16)
    a["gwT0"] = f["L0_ffn_gate_w"].T
    a["gate_b"] = np.broadcast_to(f["L0_ffn_gate_b"], (P, E0))
    for n in "13":
        a[f"w{n}"] = np.concatenate([f[f"L0_ffn_w{n}"].transpose(1, 0, 2).reshape(D, E0 * HID0),
                                     f[f"L0_ffn_sw{n}"], np.zeros((D, HPAD), np.float32)], axis=1)
        flat = np.concatenate([f[f"L0_ffn_b{n}"].reshape(-1), f[f"L0_ffn_sb{n}"],
                               np.zeros(HPAD, np.float32)])
        a[f"b{n}"] = flat.reshape(HT, P).T
    w2 = np.concatenate([f["L0_ffn_w2"].reshape(E0 * HID0, D), f["L0_ffn_sw2"],
                         np.zeros((HPAD, D), np.float32)], axis=0)
    a["w2"] = w2.reshape(HT, P, D).transpose(1, 0, 2)
    a["b2"] = np.concatenate([f["L0_ffn_b2"], f["L0_ffn_sb2"][None]], axis=0)
    sel = np.zeros((3 * PART, HT * P), np.float32)
    for part in range(3):
        for e in range(E0 + 1):
            sel[part * PART + e, e * HID0:(e + 1) * HID0] = 1
    a["sel0"] = sel.astype(bf16)
    def gate_cols(ig, fg):
        g = np.zeros((ig.shape[0], GATE_ROW + NH), np.float32)
        g[:, 0:NH], g[:, GATE_ROW:] = ig, fg
        return g
    for n, name in enumerate("qkv"):
        a[f"gk_{name}"] = gate_cols(f["L1_xattn_igate_kernel"][n * D:(n + 1) * D],
                                    f["L1_xattn_fgate_kernel"][n * D:(n + 1) * D])
    a["gk_bias"] = gate_cols(f["L1_xattn_igate_bias"][None], f["L1_xattn_fgate_bias"][None]).T
    a["out_scale"] = np.broadcast_to(f["L1_xattn_outnorm_scale"], (P, D))
    a["head_ind"] = np.repeat(np.eye(NH, dtype=np.float32), S, axis=1)
    a["seq_sel"] = np.repeat(np.eye(2, dtype=np.float32), S, axis=1)
    key_time, query_time = np.arange(P)[:, None] % S, np.arange(NH * S)[None, :] % S
    a["causal"] = np.where(key_time <= query_time, 0.0, LOWEST).astype(bf16)
    a["gwT1"] = f["L1_ffn_gate_weight"].T
    gu = f["L1_ffn_gate_up_proj"].transpose(2, 0, 1)
    a["wg"], a["wu"] = gu[:, :, :F1], gu[:, :, F1:]
    a["wd"] = f["L1_ffn_down_proj"].transpose(2, 0, 1)
    sel = np.zeros((3 * PART, E1, F1), np.float32)
    for part in range(3):
        for e in range(E1):
            sel[part * PART + e, e] = 1
    a["sel1"] = sel.astype(bf16)
    a["minus_from"] = -np.tril(np.ones((P, P))).astype(bf16)
    a["onesb"] = np.ones((P, P)).astype(bf16)
    return {k: np.ascontiguousarray(v) for k, v in a.items()}


def kernel(**inputs):
    import concourse.bacc as bacc
    from concourse.bass_utils import run_bass_kernel_spmd

    nc = bacc.Bacc("TRN2", target_bir_lowering=False, num_devices=1)
    arrays = _layout(inputs)
    aps = {n: nc.dram_tensor(f"in_{n}", a.shape, mybir.dt.from_np(a.dtype), kind="ExternalInput").ap()
           for n, a in arrays.items()}
    out = nc.dram_tensor("out", (P, TILES, D), F32, kind="ExternalOutput").ap()
    build(nc, aps, out)
    r = run_bass_kernel_spmd(nc, [{f"in_{n}": a for n, a in arrays.items()}], core_ids=[0])
    y = r.results[0]["out"]
    return y.transpose(1, 0, 2).reshape(B, S, D)
```

```python
from contextlib import ExitStack

import numpy as np
import concourse.bass as bass
from concourse import mybir

ALU = mybir.AluOpType
ACT = mybir.ActivationFunctionType
AX = mybir.AxisListType
F32 = mybir.dt.float32
BF16 = mybir.dt.bfloat16
F32R = mybir.dt.float32r

P = 128
D = 128
B, S = 32, 64
TILES = B * S // P
TPC = 4
CHUNKS = TILES // TPC
N = TPC * P
SPC = N // S
BANK = 512

HEADS, DK = 16, 8
E0, HID0 = 8, 176
HCOLS = (E0 + 1) * HID0
HT = -(-HCOLS // P)
HPAD = HT * P - HCOLS
NH, DH = 4, 32
E1, F1, TOP1, CAP = 32, 96, 8, 128
LN_EPS = 1e-5
MLSTM_EPS = 1e-6
GATE_ROW = 32
PART = 32
LOWEST = -1e30
RING0, RING1 = 7, 8
AHEAD = 2
LAG = 4
OVERLAP = LAG + 1
W0, W1 = 3 * P, 2 * F1 + D


def build(nc, t, out):
    with ExitStack() as ctx:
        def sb(name, shape, dt=F32):
            return ctx.enter_context(nc.sbuf_tensor(name, shape, dt))

        def sem(name):
            return ctx.enter_context(nc.semaphore(name))

        ps = ctx.enter_context(nc.psum_tensor("ps", [P, 8, BANK], F32))
        psb = ps[:, :, :].bitcast(BF16)

        x = sb("x_sb", [P, TILES, D])
        ctxT = sb("ctxT_sb", [P, TILES * P])
        xnT_all = sb("xnT_all", [P, TILES * P])
        region_size = 4 * (2 * TILES * P + 4 * N + 2 * RING0 * W0 + 5 * TILES * E1)
        region_start = nc.sbuf_base
        sb("region", [P, region_size // 4])

        class Region:
            def __init__(self):
                self.at = region_start

            def __call__(self, name, shape, dt=F32):
                size = 4 * int(np.prod(shape[1:]))
                assert self.at + size <= region_start + region_size, (name, self.at + size - region_start, region_size)
                tensor = nc.alloc_sbuf_tensor_at(name, shape, dt, offset=self.at)
                self.at += -(-size // 32) * 32
                return tensor

        attn_region = Region()
        moe_region = Region()
        mlstm_region = Region()
        xh, xl = moe_region("xh", [P, TILES * P], F32R), moe_region("xl", [P, TILES * P], F32R)
        hh, hl = moe_region("hh", [P, 2, N], F32R), moe_region("hl", [P, 2, N], F32R)
        wh, wl = moe_region("wh", [P, RING0 * W0], F32R), moe_region("wl", [P, RING0 * W0], F32R)
        ctx_tok = mlstm_region("ctx_tok", [P, TILES, D])
        loaded = {}
        for name, ap in t.items():
            if name in ("x", "ctx", "ctxT", "head_ind", "seq_sel"):
                continue
            loaded[name] = sb(name + "_sb", list(ap.shape), ap.dtype)
        w = loaded
        ident, identb = w["ident"], w["identb"]

        ln_stats = sb("ln_stats", [P, TILES, 6])
        ln_mv = sb("ln_mv", [P, TILES, 2])
        ln_var = sb("ln_var", [P, TILES])
        ln_rstd = sb("ln_rstd", [P, TILES])
        xn = sb("xn", [P, 2, TPC, D])
        carrier = sb("carrier", [P, 2])
        minus_half = sb("minus_half", [P, 16])

        load_ident, load_late = sem("load_ident"), sem("load_late")
        load_x = [sem(f"load_x{i}") for i in range(CHUNKS)]
        consts_set = sem("consts_set")
        set_step = sem("set_step")
        stored = sem("stored")

        class Layer:
            def __init__(self, k):
                self.ln_var_ready, self.ln_rstd_ready = sem(f"ln_var_ready_{k}"), sem(f"ln_rstd_ready_{k}")
                self.xn_ready, self.turned, self.xnT_ready = (sem(f"xn_ready_{k}"), sem(f"turned_{k}"),
                                                              sem(f"xnT_ready_{k}"))
                self.x_updated = sem(f"x_updated_{k}")
                self.ln_step, self.dve_step, self.pool_step = (sem(f"ln_step_{k}"), sem(f"dve_step_{k}"),
                                                               sem(f"pool_step_{k}"))

        A, Bf, C, Dl = (Layer(k) for k in ("attn", "ffn0", "mlstm", "ffn1"))

        class Steps:
            def __init__(self, eng, s, base=0):
                self.eng, self.s, self.base, self.n = eng, s, base, 0

            def step(self, ins):
                ins.then_inc(self.s, 1)
                self.n += 1
                self.eng.wait_ge(self.s, self.base + self.n)

            def close(self, per_chunk):
                assert self.n == per_chunk, (self.n, per_chunk)

        EARLY = TILES - TPC
        LN_PARTS = (slice(0, EARLY), slice(EARLY, TILES))
        LN_EARLY_STAGES = CHUNKS + 2

        def ln_stats_of(dve, c):
            for i in range(c * TPC, (c + 1) * TPC):
                last = dve.bn_stats(ln_stats[:, i, :], x[:, i, :])
            return last

        def ln_variances(dve, L, part):
            tiles = LN_PARTS[part]
            dve.wait_ge(L.ln_step, 2 * part + 1)
            for i in range(tiles.start, tiles.stop):
                last = dve.bn_aggr(ln_mv[:, i, :], ln_stats[:, i, :])
            last.then_inc(L.ln_step, 1)
            dve.wait_ge(L.ln_step, 2 * part + 2)
            dve.tensor_scalar(ln_var[:, tiles], ln_mv[:, tiles, 1], LN_EPS, None, ALU.add).then_inc(L.ln_var_ready, 1)

        def ln_apply(dve, L, c):
            if c >= 2:
                dve.wait_ge(L.turned, c - 1)
            for j in range(TPC):
                i = c * TPC + j
                last = dve.tensor_scalar(xn[:, c % 2, j, :], x[:, i, :], ln_mv[:, i, 0:1],
                                         ln_rstd[:, i:i + 1], ALU.subtract, ALU.mult)
            last.then_inc(L.xn_ready, 1)

        def ln_early(dve, L, stage, arrived=None):
            if stage < CHUNKS - 1:
                if arrived:
                    dve.wait_ge(arrived[stage], 16)
                last = ln_stats_of(dve, stage)
                if stage == CHUNKS - 2:
                    last.then_inc(L.ln_step, 1)
            elif stage == CHUNKS - 1:
                ln_variances(dve, L, 0)
            else:
                dve.wait_ge(L.ln_rstd_ready, 1)
                ln_apply(dve, L, stage - CHUNKS)

        def ln_dve(dve, L, arrived=None):
            if arrived:
                dve.wait_ge(arrived[CHUNKS - 1], 16)
            ln_stats_of(dve, CHUNKS - 1).then_inc(L.ln_step, 1)
            ln_variances(dve, L, 1)
            for c in range(2, CHUNKS - 1):
                ln_apply(dve, L, c)
            dve.wait_ge(L.ln_rstd_ready, 2)
            ln_apply(dve, L, CHUNKS - 1)

        def ln_pool(pool, L, part):
            tiles = LN_PARTS[part]
            pool.wait_ge(L.ln_var_ready, part + 1)
            pool.tensor_tensor(ln_rstd[:, tiles], ln_var[:, tiles], minus_half[:, tiles],
                               ALU.pow).then_inc(L.ln_rstd_ready, 1)

        def ln_pe(pe, L, c):
            pe.wait_ge(L.xn_ready, c + 1)
            if c >= 2:
                pe.wait_ge(L.xnT_ready, c - 1)
            for j in range(TPC):
                last = pe.transpose(ps[:, c % 2, j * P:(j + 1) * P], xn[:, c % 2, j, :], ident[:, :])
            last.then_inc(L.turned, 1)

        def ln_act(act, L, c):
            act.wait_ge(L.turned, c + 1)
            act.activation(xnT_all[:, c * N:(c + 1) * N], ps[:, c % 2, :], ACT.Copy).then_inc(L.xnT_ready, 1)

        kT, qT = sb("kT", [P, N]), sb("qT", [P, N])
        kbd = attn_region("kbd", [P, 4, N])
        ctxdup = attn_region("ctxdup", [P, SPC, 2, S])
        vbd = attn_region("vbd", [P, SPC, HEADS // 2, 2, DK + 1])
        smax = sb("smax", [P, HEADS])
        attn_work = attn_region("attn_work", [P, 4 * HEADS * S])
        prob = attn_work[:, 0:2 * HEADS * S].rearrange("p (a h k) -> p a h k", a=2, h=HEADS)
        probT = attn_work[:, 2 * HEADS * S:].rearrange("p (a h q) -> p a h q", a=2, h=HEADS // 2)
        rden = sb("rden", [P, 2, HEADS])
        o_tok = attn_region("o_tok", [P, TPC, D])
        oT = sb("oT", [P, N])
        ctx_copied, q_proj, k_proj, v_proj = sem("ctx_copied"), sem("q_proj"), sem("k_proj"), sem("v_proj")
        qT_ready, kT_ready, v_ready, kbd_ready = sem("qT_ready"), sem("kT_ready"), sem("v_ready"), sem("kbd_ready")
        scores_ready, centred, exp_done = sem("scores_ready"), sem("centred"), sem("exp_done")
        prob_turned, probT_ready, v_ready_act = sem("prob_turned"), sem("probT_ready"), sem("v_ready_act")
        pv_done, o_ready, o_turned, oT_ready, y_ready = (sem("pv_done"), sem("o_ready"), sem("o_turned"),
                                                         sem("oT_ready"), sem("y_ready"))
        A_DVE = 3 * TPC + 1
        HALF = HEADS // 2

        def attn_pool(pool):
            ln_pool(pool, A, 0)
            ln_pool(pool, A, 1)
            loaded_for(pool, "attn")
            with pool.Fori(0, CHUNKS) as c:
                chunk = ctxT[:, bass.ds(c * N, N)].rearrange("p (b s) -> p b s", s=S)
                for half in range(2):
                    last = pool.tensor_copy(ctxdup[:, :, half, :], chunk)
                last.then_inc(ctx_copied, 1)
                pool.wait_ge(v_proj, c + 1)

        def vbd_block(bank, half):
            rows = slice(S * half, S * half + S)
            src = ps[rows, 2 + bank, :].rearrange("p (n a d) -> p n a d", a=2, d=DK)[:, :, half, :]
            dst = vbd[rows, bank * 4:bank * 4 + 4, :, half, 0:DK].rearrange("p b h d -> p (b h) d")
            return dst, src

        def attn_dve(dve):
            for stage in range(LN_EARLY_STAGES):
                ln_early(dve, A, stage, load_x)
            ln_dve(dve, A, load_x)
            loaded_for(dve, "attn")

            def spread_keys(c):
                dve.wait_ge(kT_ready, c + 1)
                for h in range(4):
                    last = dve.tensor_scalar(kbd[:, h, :], kT[:, :], w["headmask"][:, h:h + 1], None, ALU.mult)
                last.then_inc(kbd_ready, 1)

            def softmax(c, j, hf, st):
                dve.wait_ge(scores_ready, c * 2 * TPC + 2 * j + hf + 1)
                sc = ps[:, 4 + 2 * hf:6 + 2 * hf, 0:4 * S].rearrange("p i (h k) -> p i h k", h=4)
                mx = smax[:, HALF * hf:HALF * hf + HALF].rearrange("p (i h) -> p i h", i=2)
                st.step(dve.tensor_reduce(mx, sc, AX.X, ALU.max))
                pr = prob[:, j % 2, HALF * hf:HALF * hf + HALF, :].rearrange("p (i h) k -> p i h k", i=2)
                dve.wait_ge(prob_turned, c * TPC + j - 1 + TPC)
                dve.tensor_tensor(pr, sc, mx.unsqueeze(3).to_broadcast([P, 2, 4, S]),
                                  ALU.subtract).then_inc(centred, 1)

            def spread_values(c):
                dve.wait_ge(v_proj, c + 1)
                for half in range(2):
                    last = dve.tensor_copy(*vbd_block(1, half))
                last.then_inc(v_ready, 1)

            def normalise(c, j, st):
                dve.wait_ge(pv_done, c * TPC + j + 1 + TPC)
                o = ps[:, j % 2, 0:HEADS * (DK + 1)].rearrange("p (h d) -> p h d", d=DK + 1)
                st.step(dve.reciprocal(rden[:, j % 2, :], o[:, :, DK]))
                dve.tensor_tensor(o_tok[:, j, :].rearrange("p (h d) -> p h d", d=DK), o[:, :, 0:DK],
                                  rden[:, j % 2, :].unsqueeze(2).to_broadcast([P, HEADS, DK]),
                                  ALU.mult).then_inc(o_ready, 1)

            def add(c, st):
                dve.wait_ge(y_ready, c + 1)
                xc = x[:, bass.ds(c * TPC, TPC), :]
                st.step(dve.tensor_tensor(xc, xc, ps[:, 1, :].rearrange("p (j d) -> p j d", d=D), ALU.add))
                dve.tensor_tensor(xc, xc, w["bo"][:, :].unsqueeze(1).to_broadcast([P, TPC, D]),
                                  ALU.add).then_inc(A.x_updated, 1)

            def first_tile(c, st):
                spread_keys(c)
                softmax(c, 0, 0, st)
                softmax(c, 0, 1, st)

            def other_tiles(c, st, last=False):
                for j in range(1, TPC):
                    softmax(c, j, 0, st)
                    softmax(c, j, 1, st)
                    if j < TPC - 1:
                        normalise(c, j - 1, st)
                    if last:
                        for stage in range(2 * j - 2, 2 * j):
                            ln_early(dve, Bf, stage)

            st = Steps(dve, A.dve_step)
            first_tile(0, st)
            spread_values(0)
            first_steps = st.n
            with dve.Fori(0, CHUNKS - 1) as c:
                st = Steps(dve, A.dve_step, c * A_DVE + first_steps)
                other_tiles(c, st)
                spread_keys(c + 1)
                normalise(c, TPC - 2, st)
                softmax(c + 1, 0, 0, st)
                normalise(c, TPC - 1, st)
                softmax(c + 1, 0, 1, st)
                spread_values(c + 1)
                add(c, st)
                st.close(A_DVE)
            st = Steps(dve, A.dve_step, (CHUNKS - 1) * A_DVE + first_steps)
            dve.wait_ge(A.x_updated, CHUNKS)
            other_tiles(CHUNKS - 1, st, last=True)
            normalise(CHUNKS - 1, TPC - 2, st)
            normalise(CHUNKS - 1, TPC - 1, st)
            add(CHUNKS - 1, st)
            dve.wait_ge(A.x_updated, CHUNKS + 1)

        def attn_act(act):
            for c in range(CHUNKS):
                ln_act(act, A, c)
            loaded_for(act, "attn")

            def project(c):
                act.wait_ge(k_proj, c + 1)
                act.activation(kT[:, :], ps[:, 6, :], ACT.Identity, bias=w["bk"][:, :]).then_inc(kT_ready, 1)
                act.wait_ge(q_proj, c + 1)
                act.activation(qT[:, :], ps[:, 7, :], ACT.Identity, bias=w["bq"][:, :]).then_inc(qT_ready, 1)

            def spread_values(c):
                act.wait_ge(v_proj, c + 1)
                for half in range(2):
                    last = act.activation(*vbd_block(0, half), ACT.Copy)
                last.then_inc(v_ready_act, 1)

            def exps(c, j, hf):
                act.wait_ge(centred, c * 2 * TPC + 2 * j + hf + 1)
                pr = prob[:, j % 2, HALF * hf:HALF * hf + HALF, :]
                act.activation(pr, pr, ACT.Exp, scale=float(1 / np.sqrt(np.float32(DK)))).then_inc(exp_done, 1)

            def copy_turned(c, j):
                act.wait_ge(prob_turned, c * TPC + j + 1 + TPC)
                act.wait_ge(pv_done, c * TPC + j - 1 + TPC)
                act.activation(probT[:, j % 2, :, :].rearrange("p h q -> p (h q)"),
                               ps[:, 2:4, :].rearrange("p a n -> p (a n)"), ACT.Copy).then_inc(probT_ready, 1)

            def tiles(c):
                for j in range(TPC):
                    if j + 1 < TPC:
                        exps(c, j + 1, 0)
                    copy_turned(c, j)
                    if j + 1 < TPC:
                        exps(c, j + 1, 1)

            def copy_output(c):
                act.wait_ge(o_turned, c + 1)
                act.activation(oT[:, :], ps[:, 0, :], ACT.Identity, bias=w["bv"][:, :]).then_inc(oT_ready, 1)

            project(0)
            exps(0, 0, 0)
            exps(0, 0, 1)
            spread_values(0)
            with act.Fori(0, CHUNKS - 1) as c:
                tiles(c)
                project(c + 1)
                exps(c + 1, 0, 0)
                exps(c + 1, 0, 1)
                spread_values(c + 1)
                copy_output(c)
            tiles(CHUNKS - 1)
            copy_output(CHUNKS - 1)

        def attn_pe(pe):
            for c in range(CHUNKS):
                ln_pe(pe, A, c)
            loaded_for(pe, "attn")
            pe.wait_ge(A.xnT_ready, CHUNKS)

            def project(c):
                cols = bass.ds(c * N, N)
                pe.matmul(ps[:, 6, :], w["wkT"][:, :], ctxT[:, cols], start=True, stop=True).then_inc(k_proj, 1)
                pe.matmul(ps[:, 7, :], w["wqT"][:, :], xnT_all[:, cols], start=True, stop=True).then_inc(q_proj, 1)

            def values(c):
                pe.wait_ge(ctx_copied, c + 1)
                for b in range(SPC):
                    last = pe.matmul(ps[:, 2 + b // 4, (b % 4) * D:(b % 4 + 1) * D], ctxdup[:, b, :, :],
                                     w["wvT"][:, :], start=True, stop=True)
                last.then_inc(v_proj, 1)

            def scores(c, j, hf):
                if j == 0:
                    pe.wait_ge(qT_ready, c + 1)
                    pe.wait_ge(kbd_ready, c + 1)
                else:
                    pe.wait_ge(centred, c * 2 * TPC + 2 * j - 1 + hf)
                for i in (2 * hf, 2 * hf + 1):
                    for b2 in range(2):
                        b = 2 * j + b2
                        last = pe.matmul(ps[S * b2:S * b2 + S, 4 + i, 0:4 * S],
                                         qT[32 * i:32 * i + 32, b * S:b * S + S],
                                         kbd[32 * i:32 * i + 32, :, b * S:b * S + S], start=True, stop=True)
                last.then_inc(scores_ready, 1)

            def turn(c, j):
                pe.wait_ge(exp_done, c * 2 * TPC + 2 * j + 2)
                if j == 0:
                    pe.wait_ge(v_ready, c + 1)
                    pe.wait_ge(v_ready_act, c + 1)
                else:
                    pe.wait_ge(probT_ready, c * TPC + j)
                for hp in range(HEADS // 2):
                    last = pe.transpose(ps[:, 2 + hp // 4, (hp % 4) * P:(hp % 4 + 1) * P],
                                        prob[:, j % 2, 2 * hp:2 * hp + 2, :], ident[:, :])
                last.then_inc(prob_turned, 1)

            def weighted(c, j):
                pe.wait_ge(probT_ready, c * TPC + j + 1)
                pe.wait_ge(o_ready, c * TPC + j - 1 + TPC)
                if j == 1:
                    pe.wait_ge(A.x_updated, c + 1)
                W = 2 * (DK + 1)
                for hp in range(HEADS // 2):
                    for b2 in range(2):
                        last = pe.matmul(ps[S * b2:S * b2 + S, j % 2, hp * W:(hp + 1) * W],
                                         probT[:, j % 2, hp, S * b2:S * b2 + S],
                                         vbd[:, 2 * j + b2, hp, :, :], start=True, stop=True)
                last.then_inc(pv_done, 1)

            def tiles(c):
                for j in range(TPC):
                    if j + 1 < TPC:
                        scores(c, j + 1, 0)
                    turn(c, j)
                    if j + 1 < TPC:
                        scores(c, j + 1, 1)
                        weighted(c, j)

            def outputs(c):
                pe.wait_ge(o_ready, c * TPC + TPC + TPC)
                for j in range(TPC):
                    last = pe.transpose(ps[:, 0, j * P:(j + 1) * P], o_tok[:, j, :], ident[:, :])
                last.then_inc(o_turned, 1)
                pe.wait_ge(oT_ready, c + 1)
                for j in range(TPC):
                    last = pe.matmul(ps[:, 1, j * D:(j + 1) * D], oT[:, j * P:(j + 1) * P], w["woT"][:, :],
                                     start=True, stop=True)
                last.then_inc(y_ready, 1)

            project(0)
            scores(0, 0, 0)
            scores(0, 0, 1)
            values(0)
            with pe.Fori(0, CHUNKS - 1) as c:
                tiles(c)
                project(c + 1)
                weighted(c, TPC - 1)
                scores(c + 1, 0, 0)
                scores(c + 1, 0, 1)
                values(c + 1)
                outputs(c)
            tiles(CHUNKS - 1)
            weighted(CHUNKS - 1, TPC - 1)
            outputs(CHUNKS - 1)

        logit = sb("logit", [P, TILES, E0])
        lmax = sb("lmax", [P, TILES])
        lsum = sb("lsum", [P, TILES])
        gate = sb("gate", [P, TILES, E0])
        biased = sb("biased", [P, TILES, 16])
        top8 = sb("top8", [P, TILES, 8])
        chosen = sb("chosen", [P, TILES, 8])
        rest = sb("rest", [P, TILES, 16])
        rw = sb("rw", [P, TILES, E0])
        rw3 = sb("rw3", [P, TILES, 3 * PART], BF16)
        rwrem = sb("rwrem", [P, TILES, E0])
        layer_place = moe_region.at
        b2_parts = moe_region("b2_parts", [3 * PART, 3, D], BF16)
        b2_rem = moe_region("b2_rem", [3 * PART, D])
        b2_split = sem("b2_split")
        rw3T = sb("rw3T", [3 * PART, TILES * P], BF16)
        up_a = sb("up_a", [P, 2, N])
        zbuf = sb("zbuf", [P, 2, N])
        hact = sb("hact", [P, 2, N])
        hbuf = sb("hbuf", [P, 2, N])
        yT = oT
        names = ("logits", "l_centred", "l_exp", "rw_ready", "rw_turned", "rw3T_ready", "a_ps", "c_ps", "w_ps",
                 "a_ready", "z_ready", "s_ready", "h_ready", "yT_ready", "y_turned",
                 "h_used", "xh_ready", "x_split", "hh_ready", "h_split", "wh_ready", "w_split")
        s0 = {n: sem("f0_" + n) for n in names}
        s1 = {n: sem("f1_" + n) for n in names}

        def xh_act(act, L, s):
            for c in range(CHUNKS):
                cols = slice(c * N, (c + 1) * N)
                act.wait_ge(L.xnT_ready, c + 1)
                act.activation(xh[:, cols], xnT_all[:, cols], ACT.Copy).then_inc(s["xh_ready"], 1)

        def split_x(pool, L, s):
            for c in range(CHUNKS):
                cols = slice(c * N, (c + 1) * N)
                pool.wait_ge(s["xh_ready"], c + 1)
                pool.tensor_tensor(xl[:, cols], xnT_all[:, cols], xh[:, cols], ALU.subtract).then_inc(s["x_split"], 1)

        def through_all(step, per, eng, last):
            for k in range(OVERLAP):
                step(0, None, k, None)
            with eng.Fori(0, last) as c:
                for k in range(OVERLAP, per):
                    step(c, None, k, c + 1)
                for k in range(OVERLAP):
                    step(c + 1, c, k, None)
            for k in range(OVERLAP, per):
                step(last, None, k, None)
            for k in range(OVERLAP):
                step(None, last, k, None)

        def lagging(c, prev, k, lag, per):
            if k >= lag:
                return None if c is None else (c, k - lag)
            return None if prev is None else (prev, per + k - lag)

        def count(tile, per):
            return tile[0] * per + tile[1] + 1

        def wait_pair(eng, s, tile, first, per):
            c, k = tile
            if k >= 2:
                eng.wait_ge(s, c * per + k - 1)
            elif not first:
                prior = per - 2 + (k - per) % 2
                eng.wait_ge(s, c * per - (per - 1 - prior))

        class Weights:
            def __init__(self, s, name, width, per, ring):
                self.s, self.name, self.width, self.per = s, name, width, per
                view = lambda a: a[:, 0:ring * width].rearrange("p (r w) -> p r w", w=width)
                self.high, self.low = view(wh), view(wl)
                self.place = [k % ring for k in range(per)] if per % ring == 0 else [
                    ring - 1 if k == per - 1 else k % (ring - 1) for k in range(per)]

            def freed(self, c, k):
                same = [i for i in range(self.per) if self.place[i] == self.place[k]]
                before = [i for i in same if i < k]
                if before:
                    return c * self.per + before[-1] + 1 + self.per
                return c * self.per + same[-1] + 1

            def split_high(self, act, c, k):
                act.wait_ge(self.s["h_used"], self.freed(c, k))
                act.activation(self.high[:, self.place[k], :], w[self.name][:, k, :],
                               ACT.Copy).then_inc(self.s["wh_ready"], 1)

            def split_low(self, pool, c, k):
                pool.wait_ge(self.s["wh_ready"], c * self.per + k + 1)
                pool.tensor_tensor(self.low[:, self.place[k], :], w[self.name][:, k, :],
                                   self.high[:, self.place[k], :], ALU.subtract).then_inc(self.s["w_split"], 1)

            def ahead(self, act, c, k, following):
                if k + AHEAD < self.per:
                    if c is not None:
                        self.split_high(act, c, k + AHEAD)
                elif following is not None:
                    self.split_high(act, following, k + AHEAD - self.per)

            def product(self, pe, o, k, rows, cols, high, low, start=True, stop=True):
                kh, kl = self.high[rows, self.place[k], cols], self.low[rows, self.place[k], cols]
                pe.matmul(o, kh, high, start=start, stop=False, skip_group_check=True)
                pe.matmul(o, kh, low, start=False, stop=False, skip_group_check=True)
                return pe.matmul(o, kl, high, start=False, stop=stop, skip_group_check=True)

        def hh_act(act, s, rows, tile, first, per):
            k = tile[1]
            act.wait_ge(s["h_ready"], count(tile, per))
            if k >= 2:
                act.wait_ge(s["h_used"], tile[0] * per + k - 1 + per)
            elif not first:
                prior = per - 2 + (k - per) % 2
                act.wait_ge(s["h_used"], tile[0] * per - (per - 1 - prior) + per)
            act.activation(hh[0:rows, k % 2, :], hbuf[0:rows, k % 2, :], ACT.Copy).then_inc(s["hh_ready"], 1)

        def hl_dve(dve, s, rows, tile, per):
            k = tile[1]
            dve.wait_ge(s["hh_ready"], count(tile, per))
            dve.tensor_tensor(hl[0:rows, k % 2, :], hbuf[0:rows, k % 2, :], hh[0:rows, k % 2, :],
                              ALU.subtract).then_inc(s["h_split"], 1)

        def moe_tail_act(act, s, c, per):
            act.wait_ge(s["h_used"], c * per + 2 * per)
            act.activation(yT[:, :], ps[:, 0, :], ACT.Copy).then_inc(s["yT_ready"], 1)

        def moe_tail_pe(pe, s, c):
            pe.wait_ge(s["yT_ready"], c + 2)
            for j in range(TPC):
                last = pe.transpose(ps[:, 1, j * P:(j + 1) * P], yT[:, j * P:(j + 1) * P], ident[:, :])
            last.then_inc(s["y_turned"], 1)

        def moe_tail_dve(dve, s, L, c):
            dve.wait_ge(s["y_turned"], c + 1)
            xc = x[:, bass.ds(c * TPC, TPC), :]
            dve.tensor_tensor(xc, xc, ps[:, 1, :].rearrange("p (j d) -> p j d", d=D),
                              ALU.add).then_inc(L.x_updated, 1)
            dve.wait_ge(L.x_updated, c + 2)

        weights0 = Weights(s0, "wexp0", W0, HT, RING0)
        weights1 = Weights(s1, "wexp1", W1, E1, RING1)

        def ffn0_pool(pool):
            ln_pool(pool, Bf, 0)
            ln_pool(pool, Bf, 1)
            split_x(pool, Bf, s0)
            loaded_for(pool, "ffn0")
            with pool.Fori(0, CHUNKS - 1) as c:
                for k in range(HT):
                    weights0.split_low(pool, c, k)
            for k in range(HT):
                weights0.split_low(pool, CHUNKS - 1, k)
            ln_pool(pool, C, 0)

        def softmax_dve(dve, st, s, E, lg, pr):
            dve.wait_ge(s["logits"], 1)
            src = ps[:, 7, 0:TILES * E].rearrange("p (j e) -> p j e", e=E)
            st.step(dve.tensor_reduce(lmax[:, :], src, AX.X, ALU.max))
            dve.tensor_tensor(lg, src, lmax[:, :].unsqueeze(2).to_broadcast([P, TILES, E]),
                              ALU.subtract).then_inc(s["l_centred"], 1)
            dve.wait_ge(s["l_exp"], 1)
            st.step(dve.tensor_reduce(lsum[:, :], lg, AX.X, ALU.add))
            st.step(dve.reciprocal(lsum[:, :], lsum[:, :]))
            st.step(dve.tensor_tensor(pr, lg, lsum[:, :].unsqueeze(2).to_broadcast([P, TILES, E]), ALU.mult))

        def split3(dve, st, src, rem, dst, E, s):
            st.step(dve.tensor_copy(dst[:, :, 0:E], src))
            st.step(dve.tensor_tensor(rem, src, dst[:, :, 0:E], ALU.subtract))
            st.step(dve.tensor_copy(dst[:, :, PART:PART + E], rem))
            st.step(dve.tensor_tensor(rem, rem, dst[:, :, PART:PART + E], ALU.subtract))
            dve.tensor_copy(dst[:, :, 2 * PART:2 * PART + E], rem).then_inc(s["rw_ready"], 1)

        def logits_pe(pe, s, L, E, gw, before=None):
            for pair in range(0, CHUNKS, 2):
                ln_pe(pe, L, pair)
                if pair == 0 and before:
                    pe.wait_ge(before.x_updated, CHUNKS + 1)
                ln_pe(pe, L, pair + 1)
                for c in (pair, pair + 1):
                    pe.wait_ge(L.xnT_ready, c + 1)
                    for i in range(c * TPC, (c + 1) * TPC):
                        last = pe.matmul(ps[:, 7, i * E:(i + 1) * E], xnT_all[:, i * P:(i + 1) * P], gw,
                                         start=True, stop=True)
            last.then_inc(s["logits"], 1)

        def turn_rw3(pe, i):
            return pe.transpose(psb[0:3 * PART, 6 + i // 8, (i % 8) * P:(i % 8 + 1) * P], rw3[:, i, :], identb[:, :])

        def rw3T_dve(dve, s):
            dve.wait_ge(s["rw_turned"], 1)
            for half in range(2):
                cols = slice(half * TILES * P // 2, (half + 1) * TILES * P // 2)
                dve.tensor_copy(rw3T[:, cols], psb[0:3 * PART, 6 + half, :]).then_inc(s["rw3T_ready"], 1)

        GR = GATE_ROW + NH
        gk_ctx = sb("gk_ctx", [P, GR])
        gk_summed = sem("gk_summed")

        def ffn0_dve(dve):
            s = s0
            loaded_for(dve, "ffn0")
            ln_dve(dve, Bf)
            st = Steps(dve, Bf.dve_step)
            st.step(dve.tensor_copy(b2_parts[:, 0, :], w["b2"][:, :]))
            st.step(dve.tensor_tensor(b2_rem[:, :], w["b2"][:, :], b2_parts[:, 0, :], ALU.subtract))
            st.step(dve.tensor_copy(b2_parts[:, 1, :], b2_rem[:, :]))
            st.step(dve.tensor_tensor(b2_rem[:, :], b2_rem[:, :], b2_parts[:, 1, :], ALU.subtract))
            dve.tensor_copy(b2_parts[:, 2, :], b2_rem[:, :]).then_inc(b2_split, 1)
            loaded_for(dve, "mlstm")
            dve.tensor_tensor(gk_ctx[:, :], w["gk_k"][:, :], w["gk_v"][:, :], ALU.add).then_inc(gk_summed, 1)
            softmax_dve(dve, st, s, E0, logit[:, :, :], gate[:, :, :])
            st.step(dve.tensor_tensor(biased[:, :, 0:E0], gate[:, :, :],
                                      w["gate_b"][:, :].unsqueeze(1).to_broadcast([P, TILES, E0]), ALU.add))
            for j in range(TILES):
                last = dve.max(top8[:, j, :], biased[:, j, :])
            st.step(last)
            st.step(dve.tensor_copy(chosen[:, :, 0:2], top8[:, :, 0:2]))
            for j in range(TILES):
                last = dve.match_replace(rest[:, j, :], chosen[:, j, :], biased[:, j, :], 2 * LOWEST)
            st.step(last)
            st.step(dve.tensor_tensor(rest[:, :, 0:E0], rest[:, :, 0:E0], biased[:, :, 0:E0], ALU.not_equal))
            st.step(dve.tensor_tensor(rw[:, :, :], gate[:, :, :], rest[:, :, 0:E0], ALU.mult))
            split3(dve, st, rw[:, :, :], rwrem[:, :, :], rw3, E0, s)
            rw3T_dve(dve, s)

            def gated(tile, first):
                k = tile[1]
                dve.wait_ge(s["a_ready"], count(tile, HT))
                dve.wait_ge(s["c_ps"], count(tile, HT))
                wait_pair(dve, s["s_ready"], tile, first, HT)
                dve.scalar_tensor_tensor(zbuf[:, k % 2, :], ps[:, 4 + k % 2, :], w["b3"][:, k:k + 1],
                                         up_a[:, k % 2, :], ALU.add, ALU.mult).then_inc(s["z_ready"], 1)

            def weigh(tile, first):
                k = tile[1]
                dve.wait_ge(s["s_ready"], count(tile, HT))
                dve.wait_ge(s["w_ps"], count(tile, HT))
                wait_pair(dve, s["h_split"], tile, first, HT)
                dve.tensor_tensor(hbuf[:, k % 2, :], hact[:, k % 2, :], ps[:, 6 + k % 2, :],
                                  ALU.mult).then_inc(s["h_ready"], 1)

            def step(c, prev, k, following):
                first = prev is None
                if k == 0 and not first:
                    weigh((prev, HT - 1), first)
                if c is not None:
                    gated((c, k), first)
                if tile := lagging(c, prev, k, 2, HT):
                    hl_dve(dve, s, P, tile, HT)
                if k > 0 and (tile := lagging(c, prev, k, 1, HT)):
                    weigh(tile, first)
                if k == OVERLAP - 1 and prev is not None:
                    moe_tail_dve(dve, s, Bf, prev)
                if prev is None and following is None and 0 <= k - OVERLAP < CHUNKS:
                    ln_early(dve, C, k - OVERLAP)
                if c is None and k in (1, 2):
                    ln_early(dve, C, CHUNKS + k - 1)

            through_all(step, HT, dve, CHUNKS - 1)

        def ffn0_act(act):
            s = s0
            for c in range(CHUNKS):
                ln_act(act, Bf, c)
            xh_act(act, Bf, s)
            act.wait_ge(s["l_centred"], 1)
            act.activation(logit[:, :, :], logit[:, :, :], ACT.Exp).then_inc(s["l_exp"], 1)
            loaded_for(act, "ffn0")

            def up(tile, first):
                k = tile[1]
                act.wait_ge(s["a_ps"], count(tile, HT))
                wait_pair(act, s["z_ready"], tile, first, HT)
                act.activation(up_a[:, k % 2, :], ps[:, 2 + k % 2, :], ACT.Identity,
                               bias=w["b1"][:, k:k + 1]).then_inc(s["a_ready"], 1)

            def silu(tile, first):
                k = tile[1]
                act.wait_ge(s["z_ready"], count(tile, HT))
                wait_pair(act, s["h_ready"], tile, first, HT)
                act.activation(hact[:, k % 2, :], zbuf[:, k % 2, :], ACT.Silu).then_inc(s["s_ready"], 1)

            def step(c, prev, k, following):
                first = prev is None
                weights0.ahead(act, c, k, following)
                if k == LAG - 1 and prev is not None:
                    moe_tail_act(act, s, prev, HT)
                if k == 0 and not first:
                    silu((prev, HT - 1), first)
                if c is not None:
                    up((c, k), first)
                if tile := lagging(c, prev, k, 2, HT):
                    hh_act(act, s, P, tile, first, HT)
                if k > 0 and (tile := lagging(c, prev, k, 1, HT)):
                    silu(tile, first)

            for k in range(AHEAD):
                weights0.split_high(act, 0, k)
            through_all(step, HT, act, CHUNKS - 1)

        def ffn0_pe(pe):
            s = s0
            loaded_for(pe, "ffn0")
            logits_pe(pe, s, Bf, E0, w["gwT0"][:, :], before=A)

            def up_and_gate(tile, first):
                c, k = tile
                cols = bass.ds(c * N, N)
                xhc, xlc = xh[:, cols], xl[:, cols]
                everyone = slice(0, P)
                pe.wait_ge(s["w_split"], count(tile, HT))
                wait_pair(pe, s["a_ready"], tile, first, HT)
                weights0.product(pe, ps[:, 2 + k % 2, :], k, everyone, slice(0, P), xhc, xlc).then_inc(s["a_ps"], 1)
                wait_pair(pe, s["z_ready"], tile, first, HT)
                weights0.product(pe, ps[:, 4 + k % 2, :], k, everyone, slice(P, 2 * P), xhc,
                                 xlc).then_inc(s["c_ps"], 1)

            def spread_routing(tile, first):
                c, k = tile
                cols = bass.ds(c * N, N)
                wait_pair(pe, s["h_ready"], tile, first, HT)
                pe.matmul(ps[:, 6 + k % 2, :], w["sel0"][:, k * P:(k + 1) * P], rw3T[:, cols], start=True,
                          stop=True).then_inc(s["w_ps"], 1)

            def down(tile):
                c, k = tile
                if k == 0:
                    pe.wait_ge(s["yT_ready"], c + 1)
                    for part in range(3):
                        pe.matmul(ps[:, 0, :], b2_parts[:, part, :], rw3T[:, bass.ds(c * N, N)],
                                  start=(part == 0), stop=False, skip_group_check=True)
                pe.wait_ge(s["h_split"], count(tile, HT))
                weights0.product(pe, ps[:, 0, :], k, slice(0, P), slice(2 * P, 3 * P), hh[:, k % 2, :],
                                 hl[:, k % 2, :], start=False, stop=(k == HT - 1)).then_inc(s["h_used"], 1)

            def step(c, prev, k, following):
                if tile := lagging(c, prev, k, LAG, HT):
                    down(tile)
                first = prev is None
                if c is not None:
                    if not (first and k < 2):
                        up_and_gate((c, k), first)
                    spread_routing((c, k), first)
                if k == LAG - 1 and prev is not None:
                    moe_tail_pe(pe, s, prev)

            pe.wait_ge(s["x_split"], 1)
            for k in range(2):
                up_and_gate((0, k), True)
            pe.wait_ge(s["rw_ready"], 1)
            for i in range(TILES):
                last = turn_rw3(pe, i)
            last.then_inc(s["rw_turned"], 1)
            pe.wait_ge(s["rw3T_ready"], 2)
            pe.wait_ge(b2_split, 1)
            pe.wait_ge(s["x_split"], CHUNKS)
            through_all(step, HT, pe, CHUNKS - 1)

        gates = mlstm_region("gates", [GR, TILES * P])
        ig_r, fg_r = sb("ig_r", [P, S]), sb("fg_r", [P, S])
        t0, t1, t2 = sb("row_t0", [P, S]), sb("row_t1", [P, S]), sb("row_t2", [P, S])
        cum, g_r, m_r, neg_m, en_r = (sb("cum", [P, S]), sb("g_r", [P, S]), sb("m_r", [P, S]), sb("neg_m", [P, S]),
                                      sb("en_r", [P, S]))
        ones_r = sb("ones_r", [P, S])
        g4 = mlstm_region("g4", [NH, TILES * P])
        by_key = sb("by_key", [NH + 2, N])
        by_query = mlstm_region("by_query", [NH + 2, NH, TILES, S])
        en_tok = sb("en_tok", [P, TILES, NH])
        gates_ps, gates_ready, rows_in = sem("gates_ps"), sem("gates_ready"), sem("rows_in")
        row_dve, row_act, row_ready, rows_out = sem("row_dve"), sem("row_act"), sem("row_ready"), sem("rows_out")
        en_turned, en_copied = sem("en_turned"), sem("en_copied")

        minus_abs_ready, g_ready, neg_m_ready, row_max_ready = (sem("minus_abs_ready"), sem("g_ready"),
                                                                sem("neg_m_ready"), sem("row_max_ready"))

        def gates_pool(pool):
            ln_pool(pool, C, 1)

        def gates_pe(pe):
            def gate_product(c, weights, moving, **flags):
                return pe.matmul(ps[0:GR, 2 + c, :], weights, moving[:, c * N:(c + 1) * N], skip_group_check=True,
                                 **flags)

            pe.wait_ge(gk_summed, 1)
            for c in range(CHUNKS):
                gate_product(c, gk_ctx[:, :], ctxT, start=True, stop=False)
            for c in range(CHUNKS):
                if c == 1:
                    pe.wait_ge(Bf.x_updated, CHUNKS + 1)
                ln_pe(pe, C, c)
            for c in range(CHUNKS):
                pe.wait_ge(C.xnT_ready, c + 1)
                gate_product(c, w["gk_q"][:, :], xnT_all, start=False, stop=True).then_inc(gates_ps, 1)
            pe.wait_ge(row_ready, 1)
            pe.transpose(ps[0:S, 0, 0:P], en_r[:, :], ident[:, :]).then_inc(en_turned, 1)

        def gates_act(act):
            for c in range(CHUNKS):
                ln_act(act, C, c)
            for c in range(CHUNKS):
                act.wait_ge(gates_ps, c + 1)
                act.activation(gates[:, c * N:(c + 1) * N], ps[0:GR, 2 + c, :], ACT.Identity,
                               bias=w["gk_bias"][:, :]).then_inc(gates_ready, 1)
            act.wait_ge(minus_abs_ready, 1)
            act.activation(t0[:, :], t0[:, :], ACT.Exp).then_inc(row_act, 1)
            act.wait_ge(row_act, 1)
            act.activation(t0[:, :], t0[:, :], ACT.Ln, bias=1.0).then_inc(row_act, 1)
            act.wait_ge(row_max_ready, 1)
            act.activation(en_r[:, :], t2[:, :], ACT.Exp, scale=-1.0).then_inc(row_ready, 1)

        def gates_dve(dve):
            ln_dve(dve, C)
            dve.wait_ge(rows_in, 16 * 2)
            dve.scalar_tensor_tensor(t0[:, :], fg_r[:, :], -1.0, fg_r[:, :], ALU.mult,
                                     ALU.min).then_inc(minus_abs_ready, 1)
            st = Steps(dve, row_dve)
            st.step(dve.tensor_scalar(t1[:, :], fg_r[:, :], 0.0, None, ALU.min))
            dve.wait_ge(row_act, 2)
            st.step(dve.tensor_tensor(t1[:, :], t1[:, :], t0[:, :], ALU.subtract))
            st.step(dve.tensor_tensor_scan(cum[:, :], ones_r[:, :], t1[:, :], 0.0, ALU.mult, ALU.add))
            dve.tensor_tensor(g_r[:, :], ig_r[:, :], cum[:, :], ALU.subtract).then_inc(g_ready, 1)
            dve.wait_ge(g_ready, 1)
            st.step(dve.tensor_tensor_scan(m_r[:, :], g_r[:, :], g_r[:, :], -3e38, ALU.max, ALU.max))
            dve.tensor_scalar(neg_m[:, :], m_r[:, :], -1.0, None, ALU.mult).then_inc(neg_m_ready, 1)
            dve.tensor_tensor(t2[:, :], cum[:, :], m_r[:, :], ALU.add).then_inc(row_max_ready, 1)
            dve.wait_ge(en_turned, 1)
            src = ps[0:S, 0, 0:P].rearrange("s (h p b) -> s p h b", h=NH, b=2)
            for b2 in range(2):
                last = dve.tensor_copy(en_tok[S * b2:S * b2 + S, :, :], src[:, :, :, b2])
            last.then_inc(en_copied, 1)

        def gates_sp(sp):
            sp.wait_ge(gates_ready, CHUNKS)
            for row, dst in ((0, ig_r), (GATE_ROW, fg_r)):
                sp.dma_start(dst[:, :],
                             gates[row:row + NH, :].rearrange("h (b s) -> h b s", s=S)).then_inc(rows_in, 16)
            sp.wait_ge(g_ready, 1)
            sp.dma_start(g4[:, :].rearrange("h (b s) -> h b s", s=S),
                         g_r[:, :]).then_inc(rows_out, 16)
            sp.wait_ge(neg_m_ready, 1)
            for b2 in range(2):
                sp.dma_start(by_query[NH + b2:NH + b2 + 1, :, :, :].rearrange("o h p s -> o (h p) s"),
                             neg_m[b2::2, :]).then_inc(rows_out, 16)

        xnTc, ctxTc = kT, qT
        vext = sb("vext", [P, 2, TPC, NH, DH + 1])
        dmat = up_a[:, :, :].rearrange("p a (b h s) -> p (a b) h s", b=2, h=NH)
        cmat = zbuf[:, :, :].rearrange("p a (b h s) -> p (a b) h s", b=2, h=NH)
        n_a, n_b = sb("n_a", [P, TPC, NH]), sb("n_b", [P, TPC, NH])
        ho = hact[:, 0, :].rearrange("p (j h d) -> p j h d", j=TPC, h=NH)
        hsq = hbuf[:, 0, :].rearrange("p (j h d) -> p j h d", j=TPC, h=NH)
        hm, hv = sb("hm", [P, TPC * NH]), sb("hv", [P, TPC * NH])
        by_key_ready, qk_in, vext_ready = sem("by_key_ready"), sem("qk_in"), sem("vext_ready")
        qk_ps, logd_ps, h_ps = sem("qk_ps"), sem("logd_ps"), sem("h_ps")
        hc_ready, hsq_ready, hvar_ready, hrstd_ready = (sem("hc_ready"), sem("hsq_ready"), sem("hvar_ready"),
                                                        sem("hrstd_ready"))
        cmat_ready, dmat_taken, h_read = sem("cmat_ready"), sem("dmat_taken"), sem("h_read")
        C_DVE = 10

        def mlstm_pool(pool):
            def values(c, first=False):
                if not first:
                    pool.wait_ge(h_ps, c)
                for b2 in range(2):
                    rows = slice(S * b2, S * b2 + S)
                    pool.tensor_copy(
                        vext[rows, b2, :, :, 0:DH],
                        ctx_tok[rows, bass.ds(c * TPC, TPC), :].rearrange("p j (h d) -> p j h d", h=NH)
                    ).then_inc(vext_ready, 1)

            def root(c, copied):
                pool.wait_ge(vext_ready, copied * 2)
                pool.wait_ge(hvar_ready, c + 1)
                pool.tensor_tensor(hv[:, :], hv[:, :], minus_half[:, :], ALU.pow).then_inc(hrstd_ready, 1)
                pool.wait_ge(hrstd_ready, c + 1)

            pool.wait_ge(C.ln_rstd_ready, 2)
            pool.wait_ge(load_late, 16 * 3)
            values(0, first=True)
            with pool.Fori(0, CHUNKS - 1) as c:
                values(c + 1)
                root(c, c + 2)
            root(CHUNKS - 1, CHUNKS)

        def mlstm_act(act):
            def prepare(c, first=False):
                if not first:
                    act.wait_ge(logd_ps, c)
                act.activation(by_key[0:NH, :], g4[:, bass.ds(c * N, N)], ACT.Copy).then_inc(by_key_ready, 1)
                if not first:
                    act.wait_ge(qk_ps, c)
                act.activation(xnTc[:, :], xnT_all[:, bass.ds(c * N, N)], ACT.Copy)
                act.activation(ctxTc[:, :], ctxT[:, bass.ds(c * N, N)], ACT.Copy).then_inc(qk_in, 1)
                act.wait_ge(logd_ps, c + 1)
                act.wait_ge(cmat_ready, c + 1)
                act.activation(dmat[:, :, :, :].rearrange("p j h s -> p (j h s)"),
                               ps[:, 4:6, :].rearrange("p a n -> p (a n)"), ACT.Exp).then_inc(dmat_taken, 1)

            def squares(c):
                act.wait_ge(hc_ready, c + 1)
                act.activation(hsq[:, :, :, :], ho[:, :, :, :], ACT.Square).then_inc(hsq_ready, 1)

            act.wait_ge(rows_out, 16 * 3)
            prepare(0, first=True)
            with act.Fori(0, CHUNKS - 1) as c:
                prepare(c + 1)
                squares(c)
            squares(CHUNKS - 1)

        def mlstm_pe(pe):
            def log_d(c):
                pe.wait_ge(by_key_ready, c + 1)
                pe.wait_ge(dmat_taken, c + 1)
                for j in range(TPC):
                    o = ps[:, 4 + j // 2, (j % 2) * NH * S:(j % 2 + 1) * NH * S]
                    pe.matmul(o, by_key[:, j * P:(j + 1) * P],
                              by_query[:, :, bass.ds(c * TPC + j, 1), :].rearrange("b h a s -> b (h a) s"),
                              start=True, stop=False)
                    last = pe.matmul(o, identb[:, :], w["causal"][:, :], start=False, stop=True)
                last.then_inc(logd_ps, 1)

            def q_dot_k(c):
                pe.wait_ge(qk_in, c + 1)
                pe.wait_ge(cmat_ready, c + 1)
                for j in range(TPC):
                    for h in range(NH):
                        for b2 in range(2):
                            rows, cols = slice(DH * h, DH * h + DH), slice((2 * j + b2) * S, (2 * j + b2 + 1) * S)
                            last = pe.matmul(ps[S * b2:S * b2 + S, h, j * S:(j + 1) * S], ctxTc[rows, cols],
                                             xnTc[rows, cols], start=True, stop=True)
                last.then_inc(qk_ps, 1)

            def outputs(c):
                pe.wait_ge(vext_ready, c * 2 + 2)
                pe.wait_ge(cmat_ready, c + 2)
                pe.wait_ge(h_read, c + 1)
                for j in range(TPC):
                    for h in range(NH):
                        for b2 in range(2):
                            col = (j % 2) * NH * (DH + 1) + h * (DH + 1)
                            last = pe.matmul(ps[S * b2:S * b2 + S, 6 + j // 2, col:col + DH + 1],
                                             cmat[:, j, h, :], vext[:, b2, j, h, :], start=True, stop=True)
                last.then_inc(h_ps, 1)

            pe.wait_ge(en_copied, 1)
            pe.wait_ge(load_late, 16 * 3)
            log_d(0)
            q_dot_k(0)
            with pe.Fori(0, CHUNKS - 1) as c:
                log_d(c + 1)
                outputs(c)
                q_dot_k(c + 1)
            outputs(CHUNKS - 1)

        def mlstm_dve(dve):
            W = DH + 1
            hn = ho[:, :, :, :].rearrange("p j h d -> p (j h) d")
            hd = ho[:, :, :, :].rearrange("p j h d -> p j (h d)")

            def combine(c):
                dve.wait_ge(dmat_taken, c + 2)
                dve.wait_ge(qk_ps, c + 1)
                for j in range(TPC):
                    last = dve.scalar_tensor_tensor(cmat[:, j, :, :], ps[:, 0:NH, j * S:(j + 1) * S],
                                                    float(1 / np.sqrt(np.float32(DH))), dmat[:, j, :, :],
                                                    ALU.mult, ALU.mult)
                last.then_inc(cmat_ready, 1)

            def divide_and_centre(c, st):
                dve.wait_ge(h_ps, c + 1)
                o = ps[:, 6:8, 0:2 * NH * W].rearrange("p a (n d) -> p a n d", d=W)
                two = lambda a: a.rearrange("p (a j) h -> p a (j h)", a=2)
                na = two(n_a[:, :, :])
                st.step(dve.tensor_copy(na, o[:, :, :, DH]))
                st.step(dve.scalar_tensor_tensor(n_b[:, :, :], n_a[:, :, :], -1.0, n_a[:, :, :], ALU.mult, ALU.max))
                st.step(dve.tensor_tensor(n_a[:, :, :], n_b[:, :, :], en_tok[:, bass.ds(c * TPC, TPC), :], ALU.max))
                st.step(dve.tensor_scalar(n_b[:, :, :], n_a[:, :, :], MLSTM_EPS, None, ALU.add))
                st.step(dve.reciprocal(n_a[:, :, :], n_b[:, :, :]))
                dve.tensor_tensor(ho[:, :, :, :].rearrange("p (a j) h d -> p a (j h) d", a=2), o[:, :, :, 0:DH],
                                  na.unsqueeze(3).to_broadcast([P, 2, 2 * NH, DH]), ALU.mult).then_inc(h_read, 1)
                dve.wait_ge(h_read, c + 2)
                st.step(dve.tensor_reduce(hm[:, :], hn, AX.X, ALU.add))
                st.step(dve.tensor_scalar(hm[:, :], hm[:, :], -1.0 / DH, None, ALU.mult))
                dve.tensor_tensor(hn, hn, hm[:, :].unsqueeze(2).to_broadcast([P, TPC * NH, DH]),
                                  ALU.add).then_inc(hc_ready, 1)

            def scale_and_add(c, st, last=False):
                dve.wait_ge(hsq_ready, c + 1)
                st.step(dve.tensor_reduce(hv[:, :], hsq[:, :, :, :].rearrange("p j h d -> p (j h) d"), AX.X, ALU.add))
                dve.tensor_scalar(hv[:, :], hv[:, :], 1.0 / DH, LN_EPS, ALU.mult, ALU.add).then_inc(hvar_ready, 1)
                if last:
                    for stage in range(CHUNKS):
                        ln_early(dve, Dl, stage)
                dve.wait_ge(hrstd_ready, c + 1)
                st.step(dve.tensor_tensor(hn, hn, hv[:, :].unsqueeze(2).to_broadcast([P, TPC * NH, DH]), ALU.mult))
                st.step(dve.tensor_tensor(hd, hd, w["out_scale"][:, :].unsqueeze(1).to_broadcast([P, TPC, D]),
                                          ALU.mult))
                xc = x[:, bass.ds(c * TPC, TPC), :]
                dve.tensor_tensor(xc, xc, hd, ALU.add).then_inc(C.x_updated, 1)
                dve.wait_ge(C.x_updated, c + 2)
                st.close(C_DVE)

            dve.wait_ge(en_copied, 1)
            combine(0)
            with dve.Fori(0, CHUNKS - 1) as c:
                st = Steps(dve, C.dve_step, c * C_DVE)
                divide_and_centre(c, st)
                combine(c + 1)
                scale_and_add(c, st)
            st = Steps(dve, C.dve_step, (CHUNKS - 1) * C_DVE)
            divide_and_centre(CHUNKS - 1, st)
            scale_and_add(CHUNKS - 1, st, last=True)
            for stage in range(CHUNKS, LN_EARLY_STAGES):
                ln_early(dve, Dl, stage)

        moe_region.at = layer_place
        logit1, gate1, rest1, gsel = (moe_region(n, [P, TILES, E1]) for n in ("logit1", "gate1", "rest1", "gsel"))
        mask1 = sb("mask1", [P, TILES, E1], BF16)
        rem1 = logit1
        pos = rest1
        seg = sb("seg", [P, E1, TILES])
        counts = moe_region("counts", [P, E1, TILES])
        least = sb("least", [P, CHUNKS - 1])
        open_chunks, last_open = sb("open_chunks", [P, 1]), sb("last_open", [P, 1], mybir.dt.int32)
        mask_ready, ranks_ps, n_ready, finished = sem("mask_ready"), sem("ranks_ps"), sem("n_ready"), sem("finished")

        def last_chunk(eng):
            eng.wait_ge(n_ready, 1)
            return eng.value_load(last_open[0:1, 0:1], min_val=1, max_val=CHUNKS - 1)

        def ffn1_pool(pool):
            ln_pool(pool, Dl, 0)
            ln_pool(pool, Dl, 1)
            split_x(pool, Dl, s1)
            loaded_for(pool, "ffn1")
            for k in range(AHEAD):
                weights1.split_low(pool, 0, k)
            last = last_chunk(pool)
            for k in range(AHEAD, E1):
                weights1.split_low(pool, 0, k)
            with pool.Fori(1, last + 1) as c:
                for k in range(E1):
                    weights1.split_low(pool, c, k)

        def ffn1_dve(dve):
            s = s1
            ln_dve(dve, Dl)
            st = Steps(dve, Dl.dve_step)
            softmax_dve(dve, st, s, E1, logit1[:, :, :], gate1[:, :, :])
            for j in range(TILES):
                last = dve.max(top8[:, j, :], gate1[:, j, :])
            st.step(last)
            for j in range(TILES):
                last = dve.match_replace(rest1[:, j, :], top8[:, j, :], gate1[:, j, :], -1.0)
            st.step(last)
            dve.tensor_tensor(mask1[:, :, :], rest1[:, :, :], gate1[:, :, :],
                              ALU.not_equal).then_inc(mask_ready, 1)
            dve.wait_ge(mask_ready, 1)
            st.step(dve.tensor_tensor(gsel[:, :, :], gate1[:, :, :], mask1[:, :, :], ALU.mult))
            st.step(dve.tensor_reduce(lsum[:, :], gsel[:, :, :], AX.X, ALU.add))
            st.step(dve.reciprocal(lmax[:, :], lsum[:, :]))
            st.step(dve.tensor_tensor(gsel[:, :, :], gsel[:, :, :],
                                      lmax[:, :].unsqueeze(2).to_broadcast([P, TILES, E1]), ALU.mult))
            dve.wait_ge(ranks_ps, 1)
            st.step(dve.tensor_tensor_scan(counts[:, :, :].rearrange("p e i -> p (e i)"),
                                           seg[:, :, :].rearrange("p e i -> p (e i)"), ps[:, 7, :], 0.0,
                                           ALU.mult, ALU.add))
            st.step(dve.tensor_tensor(pos[:, :, :], ps[:, 6, :].rearrange("p (i e) -> p i e", e=E1),
                                      counts[:, :, :].rearrange("p e i -> p i e"), ALU.add))
            st.step(dve.scalar_tensor_tensor(gsel[:, :, :], pos[:, :, :], float(CAP), gsel[:, :, :],
                                             ALU.is_lt, ALU.mult))
            split3(dve, st, gsel[:, :, :], rem1[:, :, :], rw3, E1, s)
            st.step(dve.tensor_reduce(least[:, :], counts[:, :, TPC - 1:TILES - 1:TPC].rearrange("p e c -> p c e"),
                                      AX.X, ALU.min))
            st.step(dve.tensor_scalar(least[:, :], least[:, :], float(CAP), None, ALU.is_lt))
            st.step(dve.tensor_reduce(open_chunks[:, :], least[:, :], AX.X, ALU.add))
            dve.tensor_scalar(last_open[:, :], open_chunks[:, :], 1.0, None, ALU.max).then_inc(n_ready, 1)
            rw3T_dve(dve, s)

            def gated(tile, first):
                k = tile[1]
                dve.wait_ge(s["s_ready"], count(tile, E1))
                dve.wait_ge(s["c_ps"], count(tile, E1))
                wait_pair(dve, s["h_ready"], tile, first, E1)
                dve.tensor_tensor(zbuf[0:F1, k % 2, :], hact[0:F1, k % 2, :], ps[0:F1, 4 + k % 2, :],
                                  ALU.mult).then_inc(s["z_ready"], 1)

            def weigh(tile, first):
                k = tile[1]
                dve.wait_ge(s["z_ready"], count(tile, E1))
                dve.wait_ge(s["w_ps"], count(tile, E1))
                wait_pair(dve, s["h_split"], tile, first, E1)
                dve.tensor_tensor(hbuf[0:F1, k % 2, :], zbuf[0:F1, k % 2, :], ps[0:F1, 6 + k % 2, :],
                                  ALU.mult).then_inc(s["h_ready"], 1)

            def step(c, prev, k, following):
                first = prev is None
                if c is not None:
                    gated((c, k), first)
                if tile := lagging(c, prev, k, 2, E1):
                    hl_dve(dve, s, F1, tile, E1)
                if tile := lagging(c, prev, k, 1, E1):
                    weigh(tile, first)
                if k == OVERLAP - 1 and prev is not None:
                    moe_tail_dve(dve, s, Dl, prev)

            through_all(step, E1, dve, last_chunk(dve))
            dve.memset(carrier[:, :], 0.0).then_inc(finished, 1)

        def ffn1_act(act):
            s = s1
            for c in range(CHUNKS):
                ln_act(act, Dl, c)
            xh_act(act, Dl, s)
            act.wait_ge(s["l_centred"], 1)
            act.activation(logit1[:, :, :], logit1[:, :, :], ACT.Exp).then_inc(s["l_exp"], 1)

            def silu(tile, first):
                k = tile[1]
                act.wait_ge(s["a_ps"], count(tile, E1))
                wait_pair(act, s["z_ready"], tile, first, E1)
                act.activation(hact[0:F1, k % 2, :], ps[0:F1, 2 + k % 2, :], ACT.Silu).then_inc(s["s_ready"], 1)

            def step(c, prev, k, following):
                first = prev is None
                weights1.ahead(act, c, k, following)
                if k == LAG - 1 and prev is not None:
                    moe_tail_act(act, s, prev, E1)
                if c is not None:
                    silu((c, k), first)
                if tile := lagging(c, prev, k, 2, E1):
                    hh_act(act, s, F1, tile, first, E1)

            for k in range(AHEAD):
                weights1.split_high(act, 0, k)
            through_all(step, E1, act, last_chunk(act))

        def ffn1_pe(pe):
            s = s1
            loaded_for(pe, "ffn1")
            logits_pe(pe, s, Dl, E1, w["gwT1"][:, :])

            def up_and_gate(tile, first):
                c, k = tile
                cols = bass.ds(c * N, N)
                xhc, xlc = xh[:, cols], xl[:, cols]
                everyone = slice(0, P)
                pe.wait_ge(s["w_split"], count(tile, E1))
                wait_pair(pe, s["s_ready"], tile, first, E1)
                weights1.product(pe, ps[0:F1, 2 + k % 2, :], k, everyone, slice(0, F1), xhc,
                                 xlc).then_inc(s["a_ps"], 1)
                wait_pair(pe, s["z_ready"], tile, first, E1)
                weights1.product(pe, ps[0:F1, 4 + k % 2, :], k, everyone, slice(F1, 2 * F1), xhc,
                                 xlc).then_inc(s["c_ps"], 1)

            def spread_routing(tile, first):
                c, k = tile
                cols = bass.ds(c * N, N)
                wait_pair(pe, s["h_ready"], tile, first, E1)
                pe.matmul(ps[0:F1, 6 + k % 2, :], w["sel1"][:, k, :], rw3T[:, cols], start=True,
                          stop=True).then_inc(s["w_ps"], 1)

            def down(tile):
                c, k = tile
                if k == 0:
                    pe.wait_ge(s["yT_ready"], c + 1)
                pe.wait_ge(s["h_split"], count(tile, E1))
                weights1.product(pe, ps[:, 0, :], k, slice(0, F1), slice(2 * F1, W1), hh[0:F1, k % 2, :],
                                 hl[0:F1, k % 2, :], start=(k == 0), stop=(k == E1 - 1)).then_inc(s["h_used"], 1)

            def step(c, prev, k, following):
                if tile := lagging(c, prev, k, LAG, E1):
                    down(tile)
                first = prev is None
                if c is not None:
                    if not (first and k < 2):
                        up_and_gate((c, k), first)
                    spread_routing((c, k), first)
                if k == LAG - 1 and prev is not None:
                    moe_tail_pe(pe, s, prev)

            pe.wait_ge(s["x_split"], 1)
            for k in range(2):
                up_and_gate((0, k), True)
            pe.wait_ge(mask_ready, 1)
            pe.matmul(ps[:, 6, :], w["minus_from"][:, :], mask1[:, :, :].rearrange("p i e -> p (i e)"),
                      start=True, stop=True)
            pe.matmul(ps[:, 7, :], w["onesb"][:, :], mask1[:, :, :].rearrange("p i e -> p e i"), start=True,
                      stop=True).then_inc(ranks_ps, 1)
            pe.wait_ge(s["rw_ready"], 1)
            for i in range(TILES):
                last = turn_rw3(pe, i)
            last.then_inc(s["rw_turned"], 1)
            pe.wait_ge(s["rw3T_ready"], 2)
            pe.wait_ge(s["x_split"], CHUNKS)
            through_all(step, E1, pe, last_chunk(pe))

        groups = {
            "attn": ("wkT", "bk", "headmask", "wqT", "bq", "wvT", "bv", "woT", "bo"),
            "ffn0": ("gwT0", "gate_b", "identb", "wexp0", "b1", "b3", "sel0", "b2"),
            "mlstm": ("gk_q", "gk_k", "gk_v", "gk_bias", "causal", "out_scale"),
            "ffn1": ("gwT1", "minus_from", "onesb", "wexp1", "sel1"),
        }
        assert sorted(sum(groups.values(), ("ident",))) == sorted(w)
        loads = {g: sem("load_" + g) for g in groups}

        def loaded_for(eng, g):
            eng.wait_ge(loads[g], 16 * len(groups[g]) + (64 if g == "attn" else 0))
            eng.wait_ge(consts_set, 1)

        block = ctx.enter_context(nc.Block())

        @block.sync
        def _(sp):
            for c in range(CHUNKS):
                tl = slice(c * TPC, (c + 1) * TPC)
                sp.dma_start(x[:, tl, :], t["x"][:, tl, :]).then_inc(load_x[c], 16)
            for g in ("ffn0", "ffn1", "mlstm"):
                for n in groups[g]:
                    sp.dma_start(w[n].ap(), t[n]).then_inc(loads[g], 16)
            sp.wait_ge(Bf.x_updated, CHUNKS + 1)
            sp.dma_start(ctx_tok[:, :, :], t["ctx"]).then_inc(load_late, 16)
            sp.dma_start(by_query[0:NH, :, :, :], t["head_ind"]).then_inc(load_late, 16)
            sp.dma_start(by_key[NH:, :], t["seq_sel"]).then_inc(load_late, 16)
            gates_sp(sp)
            sp.wait_ge(Dl.x_updated, 2)
            sp.dma_start(out[:, 0:TPC, :], x[:, 0:TPC, :]).then_inc(stored, 16)
            sp.wait_ge(finished, 1)
            sp.dma_start(out[:, TPC:, :], x[:, TPC:, :]).then_inc(stored, 16)
            sp.wait_ge(stored, 32)

        @block.gpsimd
        def _(pool):
            pool.wait_ge(consts_set, 1)
            attn_pool(pool)
            ffn0_pool(pool)
            gates_pool(pool)
            mlstm_pool(pool)
            ffn1_pool(pool)

        @block.vector
        def _(dve):
            for n, L in enumerate((A, Bf, C, Dl)):
                dve.memset(minus_half[:, 4 * n:4 * n + 4], -0.5).then_inc(L.x_updated, 1)
            dve.memset(ones_r[:, :], 1.0).then_inc(cmat_ready, 1)
            dve.memset(seg[:, :, :], 1.0).then_inc(dmat_taken, 1)
            dve.memset(carrier[:, :], 0.0).then_inc(h_read, 1)
            dve.memset(least[:, :], 0.0).then_inc(s0["h_used"], HT)
            dve.memset(open_chunks[:, :], 0.0).then_inc(s1["h_used"], E1)
            for n, counter in enumerate((prob_turned, pv_done, o_ready)):
                dve.memset(smax[:, 4 * n:4 * n + 4], 0.0).then_inc(counter, TPC)
            dve.memset(hm[:, :], 0.0).then_inc(s0["yT_ready"], 1)
            dve.memset(hv[:, :], 0.0).then_inc(s1["yT_ready"], 1)
            dve.memset(vbd[:, :, :, :, :], 0.0)
            dve.memset(vext[:, :, :, :, :], 0.0)
            dve.memset(biased[:, :, E0:16], LOWEST)
            dve.memset(chosen[:, :, 2:8], LOWEST)
            dve.memset(rw3[:, :, :], 0.0).then_inc(set_step, 1)
            dve.wait_ge(set_step, 1)
            for half in range(2):
                rows = slice(S * half, S * half + S)
                dve.memset(vbd[rows, :, :, half, DK:DK + 1], 1.0)
                dve.memset(vext[rows, half, :, :, DH:DH + 1], 1.0)
            dve.memset(seg[:, :, 0:1], 0.0)
            dve.memset(rw3[:, :, E0:E0 + 1], 1.0).then_inc(consts_set, 1)
            attn_dve(dve)
            ffn0_dve(dve)
            gates_dve(dve)
            mlstm_dve(dve)
            ffn1_dve(dve)

        @block.scalar
        def _(act):
            act.dma_start(ident.ap(), t["ident"]).then_inc(load_ident, 16)
            for c in range(CHUNKS):
                cols = slice(c * N, (c + 1) * N)
                act.dma_start(ctxT[:, cols], t["ctxT"][:, cols]).then_inc(loads["attn"], 16)
            for n in groups["attn"]:
                act.dma_start(w[n].ap(), t[n]).then_inc(loads["attn"], 16)
            attn_act(act)
            ffn0_act(act)
            gates_act(act)
            mlstm_act(act)
            ffn1_act(act)

        @block.tensor
        def _(pe):
            pe.wait_ge(load_ident, 16)
            attn_pe(pe)
            ffn0_pe(pe)
            gates_pe(pe)
            mlstm_pe(pe)
            ffn1_pe(pe)


def _layout(inputs):
    bf16 = np.dtype(mybir.dt.np(BF16))
    f = {k: np.asarray(v) for k, v in inputs.items()}
    a = {}
    a["x"] = f["x"].reshape(TILES, P, D).transpose(1, 0, 2)
    a["ctx"] = f["ctx_1024"].reshape(TILES, P, D).transpose(1, 0, 2)
    a["ctxT"] = f["ctx_1024"].reshape(TILES * P, D).T
    a["ident"] = np.eye(P, dtype=np.float32)
    for n in "qkvo":
        a[f"w{n}T"] = f[f"L0_xattn_W_{n}"].T
    for n in "qkv":
        a[f"b{n}"] = f[f"L0_xattn_b_{n}"][:, None]
    a["bo"] = np.broadcast_to(f["L0_xattn_b_o"], (P, D))
    a["headmask"] = (np.arange(P)[:, None] % 32 // DK == np.arange(4)[None, :]).astype(np.float32)
    a["identb"] = np.eye(P).astype(bf16)
    a["gwT0"] = f["L0_ffn_gate_w"].T
    a["gate_b"] = np.broadcast_to(f["L0_ffn_gate_b"], (P, E0))
    for n in "13":
        up = np.concatenate([f[f"L0_ffn_w{n}"].transpose(1, 0, 2).reshape(D, E0 * HID0),
                             f[f"L0_ffn_sw{n}"], np.zeros((D, HPAD), np.float32)], axis=1)
        a[f"w{n}"] = up.reshape(D, HT, P)
        flat = np.concatenate([f[f"L0_ffn_b{n}"].reshape(-1), f[f"L0_ffn_sb{n}"],
                               np.zeros(HPAD, np.float32)])
        a[f"b{n}"] = flat.reshape(HT, P).T
    w2 = np.concatenate([f["L0_ffn_w2"].reshape(E0 * HID0, D), f["L0_ffn_sw2"],
                         np.zeros((HPAD, D), np.float32)], axis=0)
    w2 = w2.reshape(HT, P, D).transpose(1, 0, 2)
    a["wexp0"] = np.concatenate([a.pop("w1"), a.pop("w3"), w2], axis=2)
    b2 = np.zeros((3, PART, D), np.float32)
    b2[:, :E0], b2[:, E0] = f["L0_ffn_b2"], f["L0_ffn_sb2"]
    a["b2"] = b2.reshape(3 * PART, D)
    sel = np.zeros((3 * PART, HT * P), np.float32)
    for part in range(3):
        for e in range(E0 + 1):
            sel[part * PART + e, e * HID0:(e + 1) * HID0] = 1
    a["sel0"] = sel.astype(bf16)
    def gate_cols(ig, fg):
        g = np.zeros((ig.shape[0], GATE_ROW + NH), np.float32)
        g[:, 0:NH], g[:, GATE_ROW:] = ig, fg
        return g
    for n, name in enumerate("qkv"):
        a[f"gk_{name}"] = gate_cols(f["L1_xattn_igate_kernel"][n * D:(n + 1) * D],
                                    f["L1_xattn_fgate_kernel"][n * D:(n + 1) * D])
    a["gk_bias"] = gate_cols(f["L1_xattn_igate_bias"][None], f["L1_xattn_fgate_bias"][None]).T
    a["out_scale"] = np.broadcast_to(f["L1_xattn_outnorm_scale"], (P, D))
    a["head_ind"] = np.repeat(np.eye(NH, dtype=np.float32), TILES * S, axis=1).reshape(NH, NH, TILES, S)
    a["seq_sel"] = np.tile(np.repeat(np.eye(2, dtype=np.float32), S, axis=1), (1, TPC))
    key_time, query_time = np.arange(P)[:, None] % S, np.arange(NH * S)[None, :] % S
    a["causal"] = np.where(key_time <= query_time, 0.0, LOWEST).astype(bf16)
    a["gwT1"] = f["L1_ffn_gate_weight"].T
    gu = f["L1_ffn_gate_up_proj"].transpose(2, 0, 1)
    down = np.zeros((P, E1, D), np.float32)
    down[:F1] = f["L1_ffn_down_proj"].transpose(2, 0, 1)
    a["wexp1"] = np.concatenate([gu, down], axis=2)
    sel = np.zeros((3 * PART, E1, F1), np.float32)
    for part in range(3):
        for e in range(E1):
            sel[part * PART + e, e] = 1
    a["sel1"] = sel.astype(bf16)
    a["minus_from"] = -np.tril(np.ones((P, P))).astype(bf16)
    a["onesb"] = np.ones((P, P)).astype(bf16)
    return {k: np.ascontiguousarray(v) for k, v in a.items()}


def kernel(**inputs):
    import concourse.bacc as bacc
    from concourse.bass_utils import run_bass_kernel_spmd

    nc = bacc.Bacc("TRN2", target_bir_lowering=False, num_devices=1)
    arrays = _layout(inputs)
    aps = {n: nc.dram_tensor(f"in_{n}", a.shape, mybir.dt.from_np(a.dtype), kind="ExternalInput").ap()
           for n, a in arrays.items()}
    out = nc.dram_tensor("out", (P, TILES, D), F32, kind="ExternalOutput").ap()
    build(nc, aps, out)
    r = run_bass_kernel_spmd(nc, [{f"in_{n}": a for n, a in arrays.items()}], core_ids=[0])
    y = r.results[0]["out"]
    return y.transpose(1, 0, 2).reshape(B, S, D)
```
